# Optimizing a Trainium2 kernel written in Bass

```python
import numpy as np
import jax
import jax.numpy as jnp

def _softmax(x, axis=-1):
    return jax.nn.softmax(x, axis=axis)

def _gelu(x):
    return jax.nn.gelu(x, approximate=True)

def _silu(x):
    return jax.nn.silu(x)

def _sigmoid(x):
    return jax.nn.sigmoid(x)

def _layernorm(x, axis=-1, eps=1e-05):
    m = jnp.mean(x, axis=axis, keepdims=True)
    v = jnp.var(x, axis=axis, keepdims=True)
    return (x - m) / jnp.sqrt(v + eps)

def _scatter_add(tgt, idx, src, axis=0):
    return tgt.at[idx].add(src)

def _segment_sum(src, seg, n):
    return jax.ops.segment_sum(src, seg, n)
kernel_name = 'mk_pixart_resid_d1_seqx_r4_3b6d75'

def setup_inputs(seed: int=0):
    np.random.seed(seed)
    _w = jnp.asarray

    def _rec_inputs():
        import jax
        import jax.numpy as jnp
        _rk = jax.random.key(seed)
        x = -0.0002928 + 1 * jax.random.normal(jax.random.fold_in(_rk, 1), (16, 112, 256), jnp.float32)
        _lenS = 112 - jax.random.randint(jax.random.fold_in(_rk, 7), (16,), 0, max(1, 112 // 4) + 1, jnp.int32)
        _lenS2 = 375 - jax.random.randint(jax.random.fold_in(_rk, 8), (16,), 0, max(1, 375 // 4) + 1, jnp.int32)
        _ctx_1024P = jax.random.normal(jax.random.fold_in(_rk, 11), (16, 16, 256), jnp.float32)
        _ctx_1024c = jax.random.dirichlet(jax.random.fold_in(_rk, 511), 0.3 * jnp.ones((16,), jnp.float32), (16, 375))
        _ctx_1024t = jnp.einsum('bsk,bkd->bsd', _ctx_1024c, _ctx_1024P)
        _ctx_1024t = _ctx_1024t * jax.lax.rsqrt(jnp.mean(jnp.square(_ctx_1024t)) + 1e-12) * 0.953939
        ctx_1024 = -1.39393e-06 + 0.999914 * (_ctx_1024t + 0.3 * jax.random.normal(jax.random.fold_in(_rk, 611), (16, 375, 256), jnp.float32))
        condB_tau = jax.random.uniform(jax.random.fold_in(_rk, 12), (16,), jnp.float32, 0.0, 1.23395)
        fside_BxS2_0 = -0.00205293 + 0.99739 * jax.random.normal(jax.random.fold_in(_rk, 13), (16, 375), jnp.float32)
        return (x, ctx_1024, condB_tau, fside_BxS2_0)
    x, ctx_1024, condB_tau, fside_BxS2_0 = _rec_inputs()

    def _L0_xcond_setup():
        import jax, jax.numpy as jnp
        import numpy as np
        B, S, D, H = (2, 512, 256, 16)
        DK = D // H

        def _split_heads(x):
            b, s, _ = x.shape
            return x.reshape(b, s, H, DK).transpose(0, 2, 1, 3)
        key = jax.random.key(seed)
        ks = jax.random.split(key, 14)
        inp = {'query': jax.random.normal(ks[0], (B, S, D), jnp.float32), 'key': jax.random.normal(ks[1], (B, S, D), jnp.float32), 'value': jax.random.normal(ks[2], (B, S, D), jnp.float32), 'tau': jax.random.uniform(ks[3], (B, 1), jnp.float32, 0.5, 1.5), 'delta': jax.random.normal(ks[4], (B, S), jnp.float32)}
        sc = 1.0 / np.sqrt(D)
        for i, name in enumerate(['q', 'k', 'v', 'o']):
            inp[f'W{name}'] = jax.random.normal(ks[5 + 2 * i], (D, D), jnp.float32) * sc
            inp[f'b{name}'] = jax.random.normal(ks[6 + 2 * i], (D,), jnp.float32) * 0.01
        return inp
    _L0_xcond_all = _L0_xcond_setup()
    _L0_xcond_in = {k: v for k, v in _L0_xcond_all.items() if k in ('Wq', 'bq', 'Wk', 'bk', 'Wv', 'bv', 'Wo', 'bo')}
    del _L0_xcond_all

    def _L0_ffn_setup():
        import jax, jax.numpy as jnp
        import numpy as np
        B, S, D = (2, 512, 256)
        H, E, P, K = (8, 8, 128, 2)
        SCALE = 1.0 / np.sqrt(P)

        def _get_sel_gate(x, w, route_scale):
            logits = jnp.einsum('bsd,ed->bse', x, w).astype(jnp.float32)
            raw = logits.reshape(x.shape[0], x.shape[1], H, E)
            probs = jax.nn.sigmoid(raw)
            vals, idx = jax.lax.top_k(probs, K)
            vals = vals / jnp.clip(vals.sum(-1, keepdims=True), 1e-09)
            vals = vals * route_scale
            gate = (jax.nn.one_hot(idx, E, dtype=vals.dtype) * vals[..., None]).sum(-2)
            return gate
        key = jax.random.key(seed)
        ks = jax.random.split(key, 8)
        std = 1.0 / np.sqrt(D)
        return {'x': jax.random.normal(ks[0], (B, S, D), jnp.float32), 'q_w': jax.random.normal(ks[1], (H * P, D), jnp.float32) * std, 'k_w': jax.random.normal(ks[2], (H * P, D), jnp.float32) * std, 'v_w': jax.random.normal(ks[3], (H * E, D, P), jnp.float32) * std, 'o_w': jax.random.normal(ks[4], (H * E, P, D), jnp.float32) * (1.0 / np.sqrt(H * P)), 'sel_v_w': jax.random.normal(ks[5], (H * E, D), jnp.float32) * std, 'sel_o_w': jax.random.normal(ks[6], (H * E, D), jnp.float32) * std, 'route_scale': jnp.ones((1,), jnp.float32)}
    _L0_ffn_all = _L0_ffn_setup()
    _L0_ffn_in = {k: v for k, v in _L0_ffn_all.items() if k in ('q_w', 'k_w', 'v_w', 'o_w', 'sel_v_w', 'sel_o_w', 'route_scale')}
    del _L0_ffn_all
    return {'x': x, 'ctx_1024': ctx_1024, 'condB_tau': condB_tau, 'fside_BxS2_0': fside_BxS2_0, 'L0_xcond_Wq': _L0_xcond_in['Wq'], 'L0_xcond_bq': _L0_xcond_in['bq'], 'L0_xcond_Wk': _L0_xcond_in['Wk'], 'L0_xcond_bk': _L0_xcond_in['bk'], 'L0_xcond_Wv': _L0_xcond_in['Wv'], 'L0_xcond_bv': _L0_xcond_in['bv'], 'L0_xcond_Wo': _L0_xcond_in['Wo'], 'L0_xcond_bo': _L0_xcond_in['bo'], 'L0_ffn_q_w': _L0_ffn_in['q_w'], 'L0_ffn_k_w': _L0_ffn_in['k_w'], 'L0_ffn_v_w': _L0_ffn_in['v_w'], 'L0_ffn_o_w': _L0_ffn_in['o_w'], 'L0_ffn_sel_v_w': _L0_ffn_in['sel_v_w'], 'L0_ffn_sel_o_w': _L0_ffn_in['sel_o_w'], 'L0_ffn_route_scale': _L0_ffn_in['route_scale']}

def reference(x, ctx_1024, condB_tau, fside_BxS2_0, L0_xcond_Wq, L0_xcond_bq, L0_xcond_Wk, L0_xcond_bk, L0_xcond_Wv, L0_xcond_bv, L0_xcond_Wo, L0_xcond_bo, L0_ffn_q_w, L0_ffn_k_w, L0_ffn_v_w, L0_ffn_o_w, L0_ffn_sel_v_w, L0_ffn_sel_o_w, L0_ffn_route_scale):
    import jax
    import jax.numpy as jnp

    def _L0_xcond_ref(query, key, value, tau, delta, Wq, bq, Wk, bk, Wv, bv, Wo, bo):
        import jax, jax.numpy as jnp
        import numpy as np
        B, S, D, H = (2, 512, 256, 16)
        DK = D // H

        def _split_heads(x):
            b, s, _ = x.shape
            return x.reshape(b, s, H, DK).transpose(0, 2, 1, 3)
        q = _split_heads(query @ Wq.T + bq)
        k = _split_heads(key @ Wk.T + bk)
        v = _split_heads(value @ Wv.T + bv)
        scores = jnp.einsum('bhqd,bhkd->bhqk', q, k)
        scores = scores * tau[:, :, None, None] + delta[:, None, None, :]
        scores = scores / jnp.sqrt(jnp.asarray(DK, scores.dtype))
        p_attn = jax.nn.softmax(scores, axis=-1)
        x = jnp.einsum('bhqk,bhkd->bhqd', p_attn, v)
        x = x.transpose(0, 2, 1, 3).reshape(query.shape[0], -1, H * DK)
        return x @ Wo.T + bo

    def _L0_ffn_ref(x, q_w, k_w, v_w, o_w, sel_v_w, sel_o_w, route_scale):
        import jax, jax.numpy as jnp
        import numpy as np
        B, S, D = (2, 512, 256)
        H, E, P, K = (8, 8, 128, 2)
        SCALE = 1.0 / np.sqrt(P)

        def _get_sel_gate(x, w, route_scale):
            logits = jnp.einsum('bsd,ed->bse', x, w).astype(jnp.float32)
            raw = logits.reshape(x.shape[0], x.shape[1], H, E)
            probs = jax.nn.sigmoid(raw)
            vals, idx = jax.lax.top_k(probs, K)
            vals = vals / jnp.clip(vals.sum(-1, keepdims=True), 1e-09)
            vals = vals * route_scale
            gate = (jax.nn.one_hot(idx, E, dtype=vals.dtype) * vals[..., None]).sum(-2)
            return gate
        rs = route_scale[0]
        gate_v = _get_sel_gate(x, sel_v_w, rs)
        gate_o = _get_sel_gate(x, sel_o_w, rs)
        q = jnp.einsum('bsd,hpd->bhsp', x, q_w.reshape(H, P, D))
        k = jnp.einsum('bsd,hpd->bhsp', x, k_w.reshape(H, P, D))
        xv = jnp.einsum('bsd,hedp->bshep', x, v_w.reshape(H, E, D, P))
        v = jnp.einsum('bshep,bshe->bhsp', xv, gate_v)
        att = jax.nn.softmax(jnp.einsum('bhqp,bhkp->bhqk', q, k) * SCALE, axis=-1)
        ctx = jnp.einsum('bhqk,bhkp->bqhp', att, v)
        weighted = ctx[:, :, :, None, :] * gate_o[..., None]
        out = jnp.einsum('bshep,hepd->bsd', weighted, o_w.reshape(H, E, P, D))
        return out
    x = x + _L0_xcond_ref(_layernorm(x, axis=-1), ctx_1024, ctx_1024, condB_tau[:, None], fside_BxS2_0, L0_xcond_Wq, L0_xcond_bq, L0_xcond_Wk, L0_xcond_bk, L0_xcond_Wv, L0_xcond_bv, L0_xcond_Wo, L0_xcond_bo)
    x = x + _L0_ffn_ref(_layernorm(x, axis=-1), L0_ffn_q_w, L0_ffn_k_w, L0_ffn_v_w, L0_ffn_o_w, L0_ffn_sel_v_w, L0_ffn_sel_o_w, L0_ffn_route_scale)
    return x

_drawn_inputs = setup_inputs


def setup_inputs(seed=0):
    import zlib

    import numpy as np

    out = dict(_drawn_inputs(seed))
    spreads = {}
    factors = {'fside_BxS2_0': 2.868,
     'L0_xcond_bq': 26.785,
     'L0_xcond_bk': 64.0,
     'L0_xcond_bv': 3.371,
     'L0_xcond_bo': 3.885}
    for name, (base, spread) in spreads.items():
        noise = np.random.default_rng([zlib.crc32(name.encode()), seed]).standard_normal(out[name].shape)
        drawn = base * np.exp(spread * noise) if base else spread * noise
        out[name] = jnp.asarray(drawn.astype(out[name].dtype))
    for name, factor in factors.items():
        out[name] = (out[name] * factor).astype(out[name].dtype)
    return out
```

```python
from contextlib import ExitStack

import numpy as np

import concourse.bass as bass
from concourse import mybir

F32 = mybir.dt.float32
F32R = mybir.dt.float32r
ALU = mybir.AluOpType
ACT = mybir.ActivationFunctionType
AX = mybir.AxisListType

B, S, D = 16, 112, 256
SK, KC = 375, 125
NC = SK // KC
SKP = SK + SK % 2
XH, DK = 16, 16
H, E, P = 8, 8, 128
KD = D // 128
HALF = XH // 2
VCH = H * E * P // B
EPS = 1e-5
TOK = 256
NT = B * S // TOK
BIG = 1e30

ROW_D = 3 * DK
ROW_M = ROW_D + 2
ROWS_S = ROW_M
ROWS_T = ROW_M + 2


def spread(ap, axis, n):
    ap = ap.unsqueeze(axis)
    shape = list(ap.shape)
    shape[axis] = n
    return ap.broadcast_to(shape)


def is_first(b):
    return isinstance(b, int) and b == 0


def cross_block(nc, t, dr):
    with ExitStack() as ctx:
        def sb(name, shape, dt=F32):
            return ctx.enter_context(nc.sbuf_tensor(name, shape, dt))

        def sem(name):
            return ctx.enter_context(nc.semaphore(name))

        names = ("wq", "wk", "wv", "wo")
        w_hi = {n: sb(n + "_hi", [128, KD, D], F32R) for n in names}
        w_lo = {n: sb(n + "_lo", [128, KD, D], F32R) for n in names}
        bq = sb("bq", [128, KD]); bk = sb("bk", [128, KD])
        bv = sb("bv", [128, D]); bo = sb("bo", [128, D])
        tau4 = sb("tau4", [128, B])
        tick = sb("tick", [128, 1])
        half_pow = sb("half_pow", [128, 1])
        vstage = sb("vstage", [128, KD, VCH])
        stage = vstage[:, 0, 0:KD * D]
        cst = sb("cst", [128, KD, SKP])
        ch = sb("ch", [128, KD, SKP], F32R); cl = sb("cl", [128, KD, SKP], F32R)
        d_in, d_q, d_hi, d_lo = cst[0:B, 0], cst[0:B, 1], ch[0:B, 0], cl[0:B, 0]
        xin = sb("xin", [S, D]); xb = sb("xb", [S, D]); xq = sb("xq", [128, D]); xn = xq[0:S, :]
        stat = sb("stat", [S, 6]); mv = sb("mv", [S, 2]); ve = sb("ve", [S, 1]); rstd = sb("rstd", [S, 1])
        stat2 = sb("stat2", [S, 6]); mv2 = sb("mv2", [S, 2]); ve2 = sb("ve2", [S, 1]); rstd2 = sb("rstd2", [S, 1])
        xth = sb("xth", [128, KD, S], F32R); xtl = sb("xtl", [128, KD, S], F32R)
        qf = xq[:, 0:KD * S].rearrange("p (k s) -> p k s", k=KD); qh = sb("qh", [128, KD, S], F32R); ql = sb("ql", [128, KD, S], F32R)
        kh = sb("kh", [128, KD, SKP], F32R); kl = sb("kl", [128, KD, SKP], F32R)
        kst = sb("kst", [128, HALF, SKP], F32R); qst = sb("qst", [128, HALF, S], F32R)
        vx = sb("vx", [KC, NC, XH, DK + 1])
        nm = sb("nm", [S, XH])
        mh = sb("mh", [XH, S], F32R); ml = sb("ml", [XH, S], F32R)
        pt = [sb(f"pt{i}", [KC, NC, 4 * S]) for i in range(2)]
        rs = sb("rs", [S, XH]); af = sb("af", [S, D])
        ah = sb("ah", [128, KD, S], F32R); al = sb("al", [128, KD, S], F32R)
        x1 = sb("x1", [S, D]); x2 = af
        x2s = sb("x2s", [128, 2, KD, S], F32R)

        PS = ctx.enter_context(nc.psum_tensor("ps1", [128, 8, 512], F32))

        s = {n: sem("a_" + n) for n in (
            "stage_in", "small_in", "w_hi", "w_lo", "d_q", "d_hi", "d_lo", "d_out", "ones", "tau", "pow_c",
            "vst_in", "v_hi", "v_lo",
            "ctx_in", "x_in", "c_hi", "c_lo", "st", "mv", "ve", "rstd", "xn", "xb", "xT", "xt_hi", "xt_lo",
            "kp", "k_hi", "k_lo", "qp", "qf", "q_hi", "q_lo", "k_out", "q_out", "kst_in", "qst_in",
            "vp", "vx", "sc", "mx", "mT", "m_hi", "m_lo", "m_in", "st_sc", "exp", "pv", "rs", "af",
            "aT", "a_hi", "a_lo", "op", "x1", "x1_out", "st2", "mv2", "ve2", "rstd2", "x2", "x2T", "x2_hi", "x2_lo", "x2_out")}
        block = ctx.enter_context(nc.Block())
        bank7 = PS[:, 7, 0:KD * S].rearrange("p (k s) -> p k s", k=KD)
        kscr, qscr, dscr = dr["kscr"], dr["qscr"], dr["dscr"]
        ident = t["ident"]

        @block.sync
        def _(sp):
            for i, n in enumerate(names):
                if i:
                    sp.wait_ge(s["w_lo"], i)
                sp.dma_start(stage, dr[n]).then_inc(s["stage_in"], 16)
            smalls = [(bq[:], dr["bq"]), (bk[:], dr["bk"]),
                      (bv[:], spread(dr["bv"], 0, 128)),
                      (bo[:], spread(dr["bo"], 0, 128)),
                      (tau4[:], spread(dr["tau"], 0, 128)),
                      (d_in, dr["delta"])]
            for o, i in smalls:
                sp.dma_start(o, i).then_inc(s["small_in"], 16)
            sp.wait_ge(s["d_hi"], 1)
            sp.wait_ge(s["d_lo"], 1)
            sp.dma_start(dscr[0], d_hi.bitcast(F32)).then_inc(s["d_out"], 16)
            sp.dma_start(dscr[1], d_lo.bitcast(F32)).then_inc(s["d_out"], 16)
            sp.wait_ge(s["d_out"], 32)
            sp.wait_ge(s["ones"], 4)

            def load(b):
                if not is_first(b):
                    sp.wait_ge(s["c_lo"], b)
                    sp.wait_ge(s["xn"], b)
                    sp.wait_ge(s["xb"], b)
                sp.dma_start(cst[:], dr["ctxT"][b]).then_inc(s["ctx_in"], 16)
                sp.dma_start(xin[:], dr["x"][b]).then_inc(s["x_in"], 16)

            def bounce(b, before=None):
                if not is_first(b):
                    sp.wait_ge(s["kst_in"], 128 * before + 128)
                    sp.wait_ge(s["qst_in"], 96 * before + 96)
                sp.wait_ge(s["k_hi"], 2 * b + 2)
                sp.wait_ge(s["k_lo"], 2 * b + 2)
                sp.dma_start(kscr[0], kh[:].bitcast(F32)).then_inc(s["k_out"], 16)
                sp.dma_start(kscr[1], kl[:].bitcast(F32)).then_inc(s["k_out"], 16)
                sp.wait_ge(s["q_hi"], b + 1)
                sp.wait_ge(s["q_lo"], b + 1)
                sp.dma_start(qscr[0], qh[:].bitcast(F32)).then_inc(s["q_out"], 16)
                sp.dma_start(qscr[1], ql[:].bitcast(F32)).then_inc(s["q_out"], 16)

            def stack(b, before=None):
                sp.wait_ge(s["k_out"], 32 * b + 32)
                sp.wait_ge(s["q_out"], 32 * b + 32)
                if not is_first(b):
                    sp.wait_ge(s["st_sc"], 4 * before + 4)
                for half in range(2):
                    for j, part in enumerate((0, 1, 0)):
                        r = 64 * half + DK * j
                        src = kscr[part, :, half].rearrange("(i r) k -> r i k", r=DK)
                        sp.dma_start(kst[r:r + DK].bitcast(F32), src).then_inc(s["kst_in"], 16)
                    for j, part in enumerate((0, 0, 1)):
                        r = 64 * half + DK * j
                        src = qscr[part, :, half].rearrange("(i r) k -> r i k", r=DK)
                        sp.dma_start(qst[r:r + DK].bitcast(F32), src).then_inc(s["qst_in"], 16)
                    r = 64 * half + ROW_D
                    src = spread(dscr[:, b, :], 1, HALF)
                    sp.dma_start(kst[r:r + 2].bitcast(F32), src).then_inc(s["kst_in"], 16)

            def maxima(b):
                sp.wait_ge(s["m_hi"], b + 1)
                sp.wait_ge(s["m_lo"], b + 1)
                for half in range(2):
                    for j, m in enumerate((mh, ml)):
                        r = 64 * half + ROW_M + j
                        sp.dma_start(qst[r:r + 1].bitcast(F32), m[HALF * half:HALF * half + HALF, :].bitcast(F32)).then_inc(s["m_in"], 16)

            def store(b):
                sp.wait_ge(s["x1"], b + 1)
                sp.dma_start(dr["x1scr"][b], x1[:]).then_inc(s["x1_out"], 16)
                sp.wait_ge(s["x2_hi"], b + 1)
                sp.wait_ge(s["x2_lo"], b + 1)
                sp.dma_start(dr["x2scr"][b], x2s[:].bitcast(F32)).then_inc(s["x2_out"], 16)

            def step(b, last=False):
                if not last:
                    load(b + 1)
                if is_first(b):
                    sp.wait_ge(s["w_lo"], len(names))
                else:
                    sp.wait_ge(s["v_lo"], b)
                sp.dma_start(vstage[:], dr["vw"][:, :, bass.ds(b * VCH, VCH)]).then_inc(s["vst_in"], 16)
                if not last:
                    bounce(b + 1, b)
                maxima(b)
                if not last:
                    stack(b + 1, b)
                store(b)

            load(0)
            bounce(0)
            stack(0)
            step(0)
            with sp.Fori(1, B - 1) as b:
                step(b)
            step(B - 1, last=True)
            sp.wait_ge(s["x1_out"], 16 * B)
            sp.wait_ge(s["x2_out"], 16 * B)

        @block.gpsimd
        def _(pool):
            g = nc.gpsimd
            g.memset(kst[32:64].bitcast(F32), 1.0).then_inc(s["ones"], 1)
            g.memset(kst[96:128].bitcast(F32), 1.0).then_inc(s["ones"], 1)
            g.memset(qst[32:64].bitcast(F32), 1.0).then_inc(s["ones"], 1)
            g.memset(qst[96:128].bitcast(F32), 1.0).then_inc(s["ones"], 1)
            pool.wait_ge(s["ones"], 4)
            g.memset(vx[:], 1.0).then_inc(s["pow_c"], 1)
            g.memset(half_pow[:], -0.5).then_inc(s["pow_c"], 1)
            pool.wait_ge(s["pow_c"], 2)
            for i, n in enumerate(names):
                pool.wait_ge(s["w_hi"], i + 1)
                g.tensor_tensor(w_lo[n][:].rearrange("p k d -> p (k d)"), stage,
                                w_hi[n][:].rearrange("p k d -> p (k d)").bitcast(F32), ALU.subtract).then_inc(s["w_lo"], 1)

            def pre(b):
                pool.wait_ge(s["c_hi"], b + 1)
                if not is_first(b):
                    pool.wait_ge(s["vp"], 2 * b)
                g.tensor_tensor(cl[:], cst[:], ch[:].bitcast(F32), ALU.subtract).then_inc(s["c_lo"], 1)
                pool.wait_ge(s["ve"], b + 1)
                g.tensor_tensor(rstd[:], ve[:], half_pow[0:S, :], ALU.pow).then_inc(s["rstd"], 1)
                pool.wait_ge(s["q_hi"], b + 1)
                g.tensor_tensor(ql[:], qf, qh[:].bitcast(F32), ALU.subtract).then_inc(s["q_lo"], 1)

            def residual(b):
                pool.wait_ge(s["x_in"], 16 * b + 16)
                if is_first(b):
                    pool.wait_ge(s["small_in"], 96)
                else:
                    pool.wait_ge(s["x1"], b)
                g.tensor_tensor(xb[:], xin[:], bo[0:S, :], ALU.add).then_inc(s["xb"], 1)

            def vsplit(b):
                pool.wait_ge(s["vst_in"], 16 * b + 16)
                hi = t["v_hi"][:, :, bass.ds(b * VCH, VCH)]
                lo = t["v_lo"][:, :, bass.ds(b * VCH, VCH)]
                g.tensor_copy(hi, vstage[:]).then_inc(s["v_hi"], 1)
                pool.wait_ge(s["v_hi"], b + 1)
                g.tensor_tensor(lo, vstage[:], hi.bitcast(F32), ALU.subtract).then_inc(s["v_lo"], 1)

            def step(b, last=False):
                if not last:
                    pre(b + 1)
                vsplit(b)
                pool.wait_ge(s["ve2"], b + 1)
                g.tensor_tensor(rstd2[:], ve2[:], half_pow[0:S, :], ALU.pow).then_inc(s["rstd2"], 1)
                if not last:
                    residual(b + 1)

            pre(0)
            residual(0)
            step(0)
            with pool.Fori(1, B - 1) as b:
                step(b)
            step(B - 1, last=True)

        @block.scalar
        def _(act):
            a = nc.scalar
            for i, n in enumerate(names):
                act.wait_ge(s["stage_in"], 16 * i + 16)
                a.copy(w_hi[n][:].rearrange("p k d -> p (k d)"), stage).then_inc(s["w_hi"], 1)
            act.wait_ge(s["d_q"], 1)
            a.copy(d_hi, d_q).then_inc(s["d_hi"], 1)

            def pre(b):
                act.wait_ge(s["ctx_in"], 16 * b + 16)
                if not is_first(b):
                    act.wait_ge(s["vp"], 2 * b)
                a.copy(ch[:], cst[:]).then_inc(s["c_hi"], 1)
                act.wait_ge(s["xT"], b + 1)
                a.copy(xth[:], bank7).then_inc(s["xt_hi"], 1)
                if is_first(b):
                    act.wait_ge(s["small_in"], 96)
                else:
                    act.wait_ge(s["k_out"], 32 * b)
                for m in range(KD):
                    act.wait_ge(s["kp"], KD * b + m + 1)
                    a.activation(kh[:, m], PS[:, 4 + m, 0:SKP], ACT.Identity, bias=bk[:, m:m + 1]).then_inc(s["k_hi"], 1)
                act.wait_ge(s["qf"], 2 * b + 2)
                if not is_first(b):
                    act.wait_ge(s["q_out"], 32 * b)
                a.copy(qh[:], qf).then_inc(s["q_hi"], 1)

            def step(b, last=False):
                if not last:
                    pre(b + 1)
                act.wait_ge(s["mT"], b + 1)
                if not is_first(b):
                    act.wait_ge(s["m_in"], 64 * b)
                a.copy(mh[:], PS[0:XH, 7, 0:S]).then_inc(s["m_hi"], 1)
                for g4 in range(4):
                    act.wait_ge(s["st_sc"], 4 * b + g4 + 1)
                    if g4 >= 2 or not is_first(b):
                        act.wait_ge(s["pv"], 4 * b + g4 - 1)
                    bank = 3 * (g4 % 2)
                    a.activation(pt[g4 % 2][:], PS[0:KC, bank:bank + NC, 0:4 * S], ACT.Exp).then_inc(s["exp"], 1)
                act.wait_ge(s["aT"], b + 1)
                a.copy(ah[:], bank7).then_inc(s["a_hi"], 1)
                act.wait_ge(s["x2T"], b + 1)
                if not is_first(b):
                    act.wait_ge(s["x2_out"], 16 * b)
                a.copy(x2s[:, 0], bank7).then_inc(s["x2_hi"], 1)

            pre(0)
            step(0)
            with act.Fori(1, B - 1) as b:
                step(b)
            step(B - 1, last=True)

        @block.vector
        def _(dve):
            v = nc.vector
            dve.wait_ge(s["small_in"], 96)
            v.tensor_scalar(tau4[:], tau4[:], 0.25, None, ALU.mult).then_inc(s["tau"], 1)
            v.tensor_scalar(d_q, d_in, 0.25, None, ALU.mult).then_inc(s["d_q"], 1)
            dve.wait_ge(s["d_hi"], 1)
            v.tensor_tensor(d_lo, d_q, d_hi.bitcast(F32), ALU.subtract).then_inc(s["d_lo"], 1)
            dve.wait_ge(s["tau"], 1)
            dve.wait_ge(s["pow_c"], 2)

            def stats(b):
                dve.wait_ge(s["x_in"], 16 * b + 16)
                v.bn_stats(stat[:], xin[:]).then_inc(s["st"], 1)
                dve.wait_ge(s["st"], b + 1)
                v.memset(tick[:], 0.0)
                v.bn_aggr(mv[:], stat[:]).then_inc(s["mv"], 1)
                dve.wait_ge(s["mv"], b + 1)
                v.tensor_scalar(ve[:], mv[:, 1:2], EPS, None, ALU.add).then_inc(s["ve"], 1)

            def norm(b):
                dve.wait_ge(s["rstd"], b + 1)
                if not is_first(b):
                    dve.wait_ge(s["q_lo"], b)
                v.tensor_scalar(xn, xin[:], mv[:, 0:1], rstd[:], ALU.subtract, ALU.mult).then_inc(s["xn"], 1)

            def lows(b):
                dve.wait_ge(s["xt_hi"], b + 1)
                v.tensor_tensor(xtl[:], bank7, xth[:].bitcast(F32), ALU.subtract).then_inc(s["xt_lo"], 1)
                for m in range(KD):
                    dve.wait_ge(s["k_hi"], KD * b + m + 1)
                    v.scalar_tensor_tensor(out=kl[:, m], in0=PS[:, 4 + m, 0:SKP], scalar=bk[:, m:m + 1],
                                           in1=kh[:, m].bitcast(F32), op0=ALU.add, op1=ALU.subtract).then_inc(s["k_lo"], 1)
                dve.wait_ge(s["qp"], b + 1)
                for m in range(KD):
                    v.tensor_scalar(qf[:, m], PS[:, 7, m * S:(m + 1) * S], bq[:, m:m + 1], tau4[:, bass.ds(b, 1)],
                                    ALU.add, ALU.mult).then_inc(s["qf"], 1)

            def values(b):
                for c in range(2):
                    dve.wait_ge(s["vp"], 2 * b + c + 1)
                    k = 2 - c
                    v.tensor_tensor(vx[:, 2 * c:2 * c + k, :, 0:DK],
                                    PS[0:KC, c, 0:k * D].rearrange("p (c h d) -> p c h d", c=k, h=XH),
                                    spread(bv[0:KC, :].rearrange("p (h d) -> p h d", h=XH), 1, k),
                                    ALU.add).then_inc(s["vx"], 1)

            def step(b, last=False):
                if not last:
                    stats(b + 1)
                for g in range(8):
                    dve.wait_ge(s["sc"], 8 * b + g + 1)
                    if g == 0 and not is_first(b):
                        dve.wait_ge(s["mT"], b)
                    bank = 2 * (g % 2)
                    v.tensor_reduce(nm[:, 2 * g:2 * g + 2], PS[0:S, bank:bank + 2, 0:SK], AX.X, ALU.max,
                                    negate=True).then_inc(s["mx"], 1)
                    if g == 3 and not last:
                        norm(b + 1)
                if not last:
                    lows(b + 1)
                dve.wait_ge(s["m_hi"], b + 1)
                if not is_first(b):
                    dve.wait_ge(s["m_in"], 64 * b)
                v.tensor_tensor(ml[:], PS[0:XH, 7, 0:S], mh[:].bitcast(F32), ALU.subtract).then_inc(s["m_lo"], 1)
                dve.wait_ge(s["pv"], 4 * b + 4)
                o = PS[0:S, 6, 0:XH * (DK + 1)].rearrange("p (h d) -> p h d", h=XH)
                v.reciprocal(rs[:], o[:, :, DK]).then_inc(s["rs"], 1)
                dve.wait_ge(s["rs"], b + 1)
                v.tensor_tensor(af[:].rearrange("p (h d) -> p h d", h=XH), o[:, :, 0:DK],
                                spread(rs[:], 2, DK), ALU.mult).then_inc(s["af"], 1)
                if not last:
                    values(b + 1)
                dve.wait_ge(s["a_hi"], b + 1)
                v.tensor_tensor(al[:], bank7, ah[:].bitcast(F32), ALU.subtract).then_inc(s["a_lo"], 1)
                dve.wait_ge(s["op"], b + 1)
                dve.wait_ge(s["xb"], b + 1)
                if not is_first(b):
                    dve.wait_ge(s["x1_out"], 16 * b)
                v.tensor_tensor(x1[:], PS[0:S, 7, 0:D], xb[:], ALU.add).then_inc(s["x1"], 1)
                dve.wait_ge(s["x1"], b + 1)
                v.bn_stats(stat2[:], x1[:]).then_inc(s["st2"], 1)
                dve.wait_ge(s["st2"], b + 1)
                v.memset(tick[:], 0.0)
                v.bn_aggr(mv2[:], stat2[:]).then_inc(s["mv2"], 1)
                dve.wait_ge(s["mv2"], b + 1)
                v.tensor_scalar(ve2[:], mv2[:, 1:2], EPS, None, ALU.add).then_inc(s["ve2"], 1)
                dve.wait_ge(s["rstd2"], b + 1)
                v.tensor_scalar(x2[:], x1[:], mv2[:, 0:1], rstd2[:], ALU.subtract, ALU.mult).then_inc(s["x2"], 1)
                dve.wait_ge(s["x2_hi"], b + 1)
                v.tensor_tensor(x2s[:, 1], bank7, x2s[:, 0].bitcast(F32), ALU.subtract).then_inc(s["x2_lo"], 1)

            stats(0)
            norm(0)
            lows(0)
            values(0)
            step(0)
            with dve.Fori(1, B - 1) as b:
                step(b)
            step(B - 1, last=True)

        @block.tensor
        def _(pe):
            mm = nc.tensor.matmul

            def three(out, pairs):
                n = 0
                for lh, ll, rh, rl in pairs:
                    for l, r in ((ll, rh), (lh, rl), (lh, rh)):
                        last = mm(out, l, r, start=(n == 0), stop=(n == 3 * len(pairs) - 1))
                        n += 1
                return last

            def x_transpose(b):
                pe.wait_ge(s["xn"], b + 1)
                if not isinstance(b, int) or b > 1:
                    pe.wait_ge(s["x2_lo"], b - 1)
                for k in range(KD):
                    last = nc.tensor.transpose(PS[:, 7, k * S:(k + 1) * S], xn[:, 128 * k:128 * k + 128], ident[0:S, 0:S])
                last.then_inc(s["xT"], 1)

            def k_project(b):
                if is_first(b):
                    pe.wait_ge(s["w_lo"], len(names))
                pe.wait_ge(s["c_lo"], b + 1)
                if not isinstance(b, int) or b > 1:
                    pe.wait_ge(s["exp"], 4 * b - 4)
                for m in range(KD):
                    c = slice(128 * m, 128 * m + 128)
                    three(PS[:, 4 + m, 0:SKP], [(w_hi["wk"][:, k, c], w_lo["wk"][:, k, c], ch[:, k], cl[:, k])
                                              for k in range(KD)]).then_inc(s["kp"], 1)

            def q_project(b):
                pe.wait_ge(s["xt_lo"], b + 1)
                for m in range(KD):
                    c = slice(128 * m, 128 * m + 128)
                    last = three(PS[:, 7, m * S:(m + 1) * S],
                                 [(w_hi["wq"][:, k, c], w_lo["wq"][:, k, c], xth[:, k], xtl[:, k]) for k in range(KD)])
                last.then_inc(s["qp"], 1)

            def v_project(b):
                if not is_first(b):
                    pe.wait_ge(s["exp"], 4 * b)
                for c in range(NC):
                    r = slice(KC * c, KC * c + KC)
                    last = three(PS[0:KC, c // 2, D * (c % 2):D * (c % 2) + D],
                                 [(ch[:, k, r], cl[:, k, r], w_hi["wv"][:, k], w_lo["wv"][:, k]) for k in range(KD)])
                    if c:
                        last.then_inc(s["vp"], 1)

            def step(b, last=False):
                pe.wait_ge(s["kst_in"], 128 * b + 128)
                pe.wait_ge(s["qst_in"], 96 * b + 96)
                for g in range(8):
                    if g < 2:
                        pe.wait_ge(s["vx"], 2 * b + 2)
                    if g >= 2:
                        pe.wait_ge(s["mx"], 8 * b + g - 1)
                    for j in range(2):
                        h = 2 * g + j
                        r = slice(64 * (h // HALF), 64 * (h // HALF) + ROWS_S)
                        m = mm(PS[0:S, 2 * (g % 2) + j, 0:SKP], qst[r, h % HALF], kst[r, h % HALF], start=True, stop=True)
                    m.then_inc(s["sc"], 1)
                if not last:
                    x_transpose(b + 1)
                    k_project(b + 1)
                    q_project(b + 1)
                    pe.wait_ge(s["qf"], 2 * b + 4)
                    pe.wait_ge(s["k_lo"], 2 * b + 4)
                else:
                    pe.wait_ge(s["x2_lo"], b)
                pe.wait_ge(s["mx"], 8 * b + 8)
                nc.tensor.transpose(PS[0:XH, 7, 0:S], nm[:], ident[0:S, 0:S]).then_inc(s["mT"], 1)
                pe.wait_ge(s["m_in"], 64 * b + 64)
                for g4 in range(5):
                    if g4 < 4:
                        if g4 >= 2:
                            pe.wait_ge(s["exp"], 4 * b + g4 - 1)
                        for c in range(NC):
                            for j in range(4):
                                h = 4 * g4 + j
                                r = slice(64 * (h // HALF), 64 * (h // HALF) + ROWS_T)
                                m = mm(PS[0:KC, 3 * (g4 % 2) + c, j * S:(j + 1) * S],
                                       kst[r, h % HALF, KC * c:KC * c + KC], qst[r, h % HALF], start=True, stop=True)
                        m.then_inc(s["st_sc"], 1)
                    if g4 >= 1:
                        q = g4 - 1
                        pe.wait_ge(s["exp"], 4 * b + q + 1)
                        if q == 0 and not is_first(b):
                            pe.wait_ge(s["af"], b)
                        for j in range(4):
                            h = 4 * q + j
                            for c in range(NC):
                                m = mm(PS[0:S, 6, h * (DK + 1):(h + 1) * (DK + 1)], pt[q % 2][:, c, j * S:(j + 1) * S],
                                       vx[:, c, h], start=(c == 0), stop=(c == NC - 1))
                        m.then_inc(s["pv"], 1)
                if not last:
                    v_project(b + 1)
                pe.wait_ge(s["af"], b + 1)
                for k in range(KD):
                    m = nc.tensor.transpose(PS[:, 7, k * S:(k + 1) * S], af[:, 128 * k:128 * k + 128], ident[0:S, 0:S])
                m.then_inc(s["aT"], 1)
                pe.wait_ge(s["a_lo"], b + 1)
                three(PS[0:S, 7, 0:D], [(ah[:, k], al[:, k], w_hi["wo"][:, k], w_lo["wo"][:, k])
                                        for k in range(KD)]).then_inc(s["op"], 1)
                pe.wait_ge(s["x2"], b + 1)
                for k in range(KD):
                    m = nc.tensor.transpose(PS[:, 7, k * S:(k + 1) * S], x2[:, 128 * k:128 * k + 128], ident[0:S, 0:S])
                m.then_inc(s["x2T"], 1)

            x_transpose(0)
            k_project(0)
            q_project(0)
            v_project(0)
            step(0)
            with pe.Fori(1, B - 1) as b:
                step(b)
            step(B - 1, last=True)


def attend_block(nc, t, dr):
    with ExitStack() as ctx:
        def sb(name, shape, dt=F32):
            return ctx.enter_context(nc.sbuf_tensor("b_" + name, shape, dt))

        G = 2 * H
        scale = float(P) ** -0.5
        n_stage = 2 * KD
        qk_hi = sb("qk_hi", [128, KD, 2 * H * P], F32R); qk_lo = sb("qk_lo", [128, KD, 2 * H * P], F32R)
        sel_hi = sb("sel_hi", [128, KD, G * E], F32R); sel_lo = sb("sel_lo", [128, KD, G * E], F32R)
        stage = [sb(f"stage{i}", [128, H * P]) for i in range(2)]
        sel_in = sb("sel_in", [128, KD, G * E])
        route = sb("route", [128, 1])
        rank = sb("rank", [S, G, E])
        x2a = sb("x2a", [128, 2, KD, S], F32R)
        x2v = sb("x2v", [128, 2, KD, S], F32R)
        lg = sb("lg", [S, G, E]); ex = sb("ex", [S, G, E]); pr = sb("pr", [S, G, E]); l2 = sb("l2", [S, G, E])
        ea = sb("ea", [S, G, E]); eb = sb("eb", [S, G, E]); oh1 = sb("oh1", [S, G, E]); oh2 = sb("oh2", [S, G, E])
        gm = sb("gm", [S, 4, G]); gr = sb("gr", [S, 3, G])
        gate = [sb(f"gate{i}", [S, H, E]) for i in range(2)]
        gsp = sb("gsp", [S, H, 2, E], F32R)
        gT = sb("gT", [128, S])
        qk = sb("qk", [128, 2 * H, S])
        nm = sb("nm", [S, H]); nms = sb("nms", [S, H]); den = sb("den", [S, H]); rden = sb("rden", [S, H])
        pe_ = sb("pe", [S, H, S]); att = sb("att", [S, H, S]); attT = sb("attT", [S, H, S])
        vacc = sb("vacc", [S, H, P])
        cs = sb("cs", [P, H, S])
        PS = ctx.enter_context(nc.psum_tensor("ps2", [128, 8, 512], F32))
        s = {n: ctx.enter_context(nc.semaphore("b_" + n)) for n in (
            "stage_in0", "stage_in1", "sel_in", "route_in", "w_hi", "w_lo", "sel_hi", "sel_lo", "rank",
            "x2a_in", "x2v_in", "lgp", "lg", "ex", "gs", "gate", "g_hi", "g_lo", "gTp", "gT", "gT_out",
            "qkp", "qk", "scp", "nm", "nms", "exp", "rden", "att", "attTp", "attT",
            "vp", "v0", "v_used", "acc", "cxp", "cs", "c_out")}
        block = ctx.enter_context(nc.Block())
        ident = t["ident"]
        v_hi, v_lo = t["v_hi"], t["v_lo"]
        units = [(2 * hp + j, half) for hp in range(H // 2) for half in range(2) for j in range(2)]
        NU = len(units)
        halves0 = [u for u, (_, half) in enumerate(units) if half == 0]

        @block.sync
        def _(sp):
            sp.dma_start(sel_in[:, :, 0:G * E // 2], dr["sel_v"]).then_inc(s["sel_in"], 16)
            sp.dma_start(sel_in[:, :, G * E // 2:], dr["sel_o"]).then_inc(s["sel_in"], 16)
            sp.dma_start(route[:], spread(dr["route"], 0, 128)).then_inc(s["route_in"], 16)

            def load_a(b):
                if not is_first(b):
                    sp.wait_ge(s["qkp"], 4 * (b - 1) + 4)
                sp.dma_start(x2a[:].bitcast(F32), dr["x2scr"][b]).then_inc(s["x2a_in"], 16)

            def load_v(b):
                if not is_first(b):
                    sp.wait_ge(s["vp"], NU * (b - 1) + NU)
                sp.dma_start(x2v[:].bitcast(F32), dr["x2scr"][b]).then_inc(s["x2v_in"], 16)

            load_a(0)
            load_v(0)
            for i in range(n_stage):
                if i >= 2:
                    sp.wait_ge(s["w_lo"], i - 1)
                sp.dma_start(stage[i % 2][:], dr["qkw"][:, i % KD, (i // KD) * H * P:(i // KD + 1) * H * P]).then_inc(s[f"stage_in{i % 2}"], 16)

            def step(b, last=False):
                if not last:
                    load_a(b + 1)
                sp.wait_ge(s["gT"], b + 1)
                sp.dma_start(dr["gscr"][:, bass.ds(b * S, S)], gT[:]).then_inc(s["gT_out"], 16)
                if not last:
                    load_v(b + 1)
                sp.wait_ge(s["cs"], 2 * b + 2)
                sp.dma_start(dr["cscr"][:, :, bass.ds(b * S, S)], cs[:]).then_inc(s["c_out"], 16)

            step(0)
            with sp.Fori(1, B - 1) as b:
                step(b)
            step(B - 1, last=True)
            sp.wait_ge(s["gT_out"], 16 * B)
            sp.wait_ge(s["c_out"], 16 * B)

        @block.gpsimd
        def _(pool):
            g = nc.gpsimd
            for e in range(E):
                m = g.memset(rank[:, :, e], float(E - e))
            m.then_inc(s["rank"], 1)
            pool.wait_ge(s["sel_hi"], 1)
            g.tensor_tensor(sel_lo[:], sel_in[:], sel_hi[:].bitcast(F32), ALU.subtract).then_inc(s["sel_lo"], 1)

            def normalise(b):
                pool.wait_ge(s["rden"], b + 1)
                if not is_first(b):
                    pool.wait_ge(s["attTp"], 2 * (b - 1) + 2)
                g.tensor_tensor(att[:], pe_[:], spread(rden[:], 2, S), ALU.mult).then_inc(s["att"], 1)

            normalise(0)
            with pool.Fori(1, B) as b:
                normalise(b)

        @block.scalar
        def _(act):
            a = nc.scalar
            act.wait_ge(s["sel_in"], 32)
            a.copy(sel_hi[:], sel_in[:]).then_inc(s["sel_hi"], 1)
            for i in range(n_stage):
                act.wait_ge(s[f"stage_in{i % 2}"], 16 * (i // 2) + 16)
                a.copy(qk_hi[:, i % KD, (i // KD) * H * P:(i // KD + 1) * H * P], stage[i % 2][:]).then_inc(s["w_hi"], 1)

            def pre(b):
                act.wait_ge(s["lgp"], b + 1)
                if not is_first(b):
                    act.wait_ge(s["gate"], 2 * (b - 1) + 2)
                a.copy(lg[:], PS[0:S, 4, 0:G * E].rearrange("p (g e) -> p g e", g=G)).then_inc(s["lg"], 1)
                a.activation(ex[:], PS[0:S, 4, 0:G * E].rearrange("p (g e) -> p g e", g=G), ACT.Exp, scale=-1.0).then_inc(s["ex"], 1)
                for i in range(4):
                    act.wait_ge(s["qkp"], 4 * b + i + 1)
                    a.copy(qk[:, 4 * i:4 * i + 4], PS[:, 5 - i % 2, 0:4 * S].rearrange("p (m s) -> p m s", m=4)).then_inc(s["qk"], 1)
                if not is_first(b):
                    act.wait_ge(s["att"], b)
                for h in range(H):
                    if h % 4 == 0:
                        act.wait_ge(s["nms"], 2 * b + h // 4 + 1)
                    a.activation(pe_[:, h], PS[0:S, 5 - h // 4, (h % 4) * S:(h % 4 + 1) * S], ACT.Exp, bias=nms[:, h:h + 1],
                                 scale=scale, accum_out=den[:, h:h + 1]).then_inc(s["exp"], 1)

            def step(b, last=False):
                for n, u in enumerate(halves0):
                    h, _ = units[u]
                    act.wait_ge(s["vp"], NU * b + u + 1)
                    if n == 0:
                        act.wait_ge(s["gate"], 2 * b + 2)
                        if not is_first(b):
                            act.wait_ge(s["cxp"], 2 * (b - 1) + 2)
                    a.activation(vacc[:, h], PS[0:S, u % 4, 0:P], ACT.Copy, scale=gate[0][:, h, 0:1]).then_inc(s["v0"], 1)
                    if n == 1:
                        act.wait_ge(s["gTp"], b + 1)
                        if not is_first(b):
                            act.wait_ge(s["gT_out"], 16 * (b - 1) + 16)
                        a.copy(gT[:], PS[:, 4, 0:S]).then_inc(s["gT"], 1)
                        for i in range(2):
                            act.wait_ge(s["attTp"], 2 * b + i + 1)
                            a.copy(attT[:, 4 * i:4 * i + 4], PS[0:S, 6 + i, 0:4 * S].rearrange("p (m s) -> p m s", m=4)).then_inc(s["attT"], 1)
                if not last:
                    pre(b + 1)
                for i in range(2):
                    act.wait_ge(s["cxp"], 2 * b + i + 1)
                    if i == 0 and not is_first(b):
                        act.wait_ge(s["c_out"], 16 * (b - 1) + 16)
                    a.copy(cs[:, 4 * i:4 * i + 4], PS[:, 6 + i, 0:4 * S].rearrange("p (m s) -> p m s", m=4)).then_inc(s["cs"], 1)

            pre(0)
            step(0)
            with act.Fori(1, B - 1) as b:
                step(b)
            step(B - 1, last=True)

        @block.vector
        def _(dve):
            v = nc.vector
            for i in range(n_stage):
                c = slice((i // KD) * H * P, (i // KD + 1) * H * P)
                dve.wait_ge(s["w_hi"], i + 1)
                v.tensor_tensor(qk_lo[:, i % KD, c], stage[i % 2][:], qk_hi[:, i % KD, c].bitcast(F32), ALU.subtract).then_inc(s["w_lo"], 1)
            dve.wait_ge(s["rank"], 1)
            dve.wait_ge(s["route_in"], 16)
            NG = 17

            def gates(b):
                count = [0]

                def then(ins):
                    count[0] += 1
                    ins.then_inc(s["gs"], 1)
                    dve.wait_ge(s["gs"], NG * b + count[0])

                dve.wait_ge(s["ex"], b + 1)
                if not is_first(b):
                    dve.wait_ge(s["g_lo"], b)
                v.tensor_scalar(pr[:], ex[:], 1.0, None, ALU.add)
                then(v.tensor_reduce(gm[:, 0], lg[:], AX.X, ALU.max))
                then(v.tensor_tensor(ea[:], lg[:], spread(gm[:, 0], 2, E), ALU.is_equal))
                then(v.reciprocal(pr[:], pr[:]))
                then(v.tensor_tensor(eb[:], ea[:], rank[:], ALU.mult))
                then(v.tensor_reduce(gm[:, 1], eb[:], AX.X, ALU.max))
                then(v.tensor_tensor(oh1[:], eb[:], spread(gm[:, 1], 2, E), ALU.is_equal))
                then(v.scalar_tensor_tensor(out=l2[:], in0=oh1[:], scalar=-BIG, in1=lg[:], op0=ALU.mult, op1=ALU.add))
                then(v.tensor_reduce(gm[:, 2], l2[:], AX.X, ALU.max))
                then(v.tensor_tensor(ea[:], l2[:], spread(gm[:, 2], 2, E), ALU.is_equal))
                then(v.tensor_tensor(eb[:], ea[:], rank[:], ALU.mult))
                then(v.tensor_reduce(gm[:, 3], eb[:], AX.X, ALU.max))
                then(v.tensor_tensor(oh2[:], eb[:], spread(gm[:, 3], 2, E), ALU.is_equal))
                then(v.tensor_tensor(ea[:], oh1[:], oh2[:], ALU.add))
                then(v.tensor_tensor(eb[:], ea[:], pr[:], ALU.mult))
                then(v.tensor_reduce(gr[:, 0], eb[:], AX.X, ALU.add))
                then(v.tensor_scalar(gr[:, 1], gr[:, 0], 1e-9, None, ALU.max))
                then(v.reciprocal(gr[:, 2], gr[:, 1]))
                for i in range(2):
                    v.scalar_tensor_tensor(out=gate[i][:], in0=eb[:, H * i:H * i + H], scalar=route[0:S, :],
                                           in1=spread(gr[:, 2, H * i:H * i + H], 2, E), op0=ALU.mult,
                                           op1=ALU.mult).then_inc(s["gate"], 1)
                dve.wait_ge(s["gate"], 2 * b + 2)
                if not is_first(b):
                    dve.wait_ge(s["gTp"], b)
                v.tensor_copy(gsp[:, :, 0], gate[1][:]).then_inc(s["g_hi"], 1)
                dve.wait_ge(s["g_hi"], b + 1)
                v.tensor_tensor(gsp[:, :, 1], gate[1][:], gsp[:, :, 0].bitcast(F32), ALU.subtract).then_inc(s["g_lo"], 1)

            def maxima(b):
                for i in range(2):
                    dve.wait_ge(s["scp"], 2 * b + i + 1)
                    v.tensor_reduce(nm[:, 4 * i:4 * i + 4], PS[0:S, 5 - i, 0:4 * S].rearrange("p (m s) -> p m s", m=4),
                                    AX.X, ALU.max, negate=True).then_inc(s["nm"], 1)
                    dve.wait_ge(s["nm"], 2 * b + i + 1)
                    v.tensor_scalar(nms[:, 4 * i:4 * i + 4], nm[:, 4 * i:4 * i + 4], scale, None, ALU.mult).then_inc(s["nms"], 1)

            def step(b, last=False):
                dve.wait_ge(s["exp"], H * b + H)
                v.reciprocal(rden[:], den[:]).then_inc(s["rden"], 1)
                PER = E * H - H
                for hp in range(H // 2):
                    for half in range(2):
                        for k in range(4):
                            if half == 0 and k == 0:
                                continue
                            for j in range(2):
                                u = 4 * hp + 2 * half + j
                                h = 2 * hp + j
                                e = 4 * half + k
                                i = 14 * hp + 2 * (e - 1) + j
                                if e == 1:
                                    dve.wait_ge(s["v0"], H * b + h + 1)
                                else:
                                    dve.wait_ge(s["acc"], PER * b + i - 1)
                                if k == 0:
                                    dve.wait_ge(s["vp"], NU * b + u + 1)
                                ins = v.scalar_tensor_tensor(out=vacc[:, h], in0=PS[0:S, u % 4, k * P:(k + 1) * P],
                                                             scalar=gate[0][:, h, e:e + 1], in1=vacc[:, h],
                                                             op0=ALU.mult, op1=ALU.add)
                                ins.then_inc(s["acc"], 1)
                if not last:
                    gates(b + 1)
                    maxima(b + 1)

            gates(0)
            maxima(0)
            step(0)
            with dve.Fori(1, B - 1) as b:
                step(b)
            step(B - 1, last=True)

        @block.tensor
        def _(pe):
            mm = nc.tensor.matmul
            PER = E * H - H

            def pre(b):
                if is_first(b):
                    pe.wait_ge(s["sel_lo"], 1)
                pe.wait_ge(s["x2a_in"], 16 * b + 16)
                if not is_first(b):
                    pe.wait_ge(s["gT"], b)
                xh, xl = x2a[:, 0], x2a[:, 1]
                n = 0
                for k in range(KD):
                    for l, r in ((xl, sel_hi), (xh, sel_lo), (xh, sel_hi)):
                        m = mm(PS[0:S, 4, 0:G * E], l[:, k], r[:, k], start=(n == 0), stop=(n == 5))
                        n += 1
                m.then_inc(s["lgp"], 1)
                if is_first(b):
                    pe.wait_ge(s["w_lo"], n_stage)
                for i in range(4):
                    bank = 5 - i % 2
                    if i == 0 and not is_first(b):
                        pe.wait_ge(s["exp"], H * (b - 1) + H)
                    if i == 1:
                        pe.wait_ge(s["ex"], b + 1)
                    if i >= 2:
                        pe.wait_ge(s["qk"], 4 * b + i - 1)
                    for j in range(4):
                        c = slice((4 * i + j) * P, (4 * i + j + 1) * P)
                        n = 0
                        for k in range(KD):
                            for l, r in ((qk_lo, xh), (qk_hi, xl), (qk_hi, xh)):
                                m = mm(PS[:, bank, j * S:(j + 1) * S], l[:, k, c], r[:, k], start=(n == 0), stop=(n == 5))
                                n += 1
                    m.then_inc(s["qkp"], 1)
                for i in range(2):
                    pe.wait_ge(s["qk"], 4 * b + 3 + i)
                    if i == 0:
                        pe.wait_ge(s["qk"], 4 * b + 4)
                    for j in range(4):
                        h = 4 * i + j
                        m = mm(PS[0:S, 5 - i, j * S:(j + 1) * S], qk[:, h], qk[:, H + h], start=True, stop=True)
                    m.then_inc(s["scp"], 1)

            def step(b, last=False):
                pe.wait_ge(s["x2v_in"], 16 * b + 16)
                for u, (h, half) in enumerate(units):
                    hp, j = h // 2, h % 2
                    if u >= 4 or not is_first(b):
                        w = u - 4 if u >= 4 else u - 4 + NU
                        ph, phalf = units[w]
                        place = 14 * (ph // 2) + 2 * (4 * phalf + 2) + ph % 2 + 1
                        pe.wait_ge(s["acc"], PER * b + place if u >= 4 else PER * (b - 1) + place)
                    c = slice(h * E * P + half * 512, h * E * P + half * 512 + 512)
                    n = 0
                    for k in range(KD):
                        for l, r in ((1, v_hi), (0, v_lo), (0, v_hi)):
                            m = mm(PS[0:S, u % 4], x2v[:, l, k], r[:, k, c], start=(n == 0), stop=(n == 5))
                            n += 1
                    m.then_inc(s["vp"], 1)
                    if u == 3:
                        pe.wait_ge(s["g_lo"], b + 1)
                        pe.wait_ge(s["exp"], H * b + H)
                        nc.tensor.transpose(PS[:, 4, 0:S], gsp[:].rearrange("p h a e -> p (h a e)").bitcast(F32), ident[0:S, 0:S]).then_inc(s["gTp"], 1)
                        pe.wait_ge(s["att"], b + 1)
                        for i in range(2):
                            if i == 0 and not is_first(b):
                                pe.wait_ge(s["cs"], 2 * (b - 1) + 2)
                            for jj in range(4):
                                m = nc.tensor.transpose(PS[0:S, 6 + i, jj * S:(jj + 1) * S], att[:, 4 * i + jj], ident[0:S, 0:S])
                            m.then_inc(s["attTp"], 1)
                if not last:
                    pre(b + 1)
                pe.wait_ge(s["attT"], 2 * b + 2)
                pe.wait_ge(s["acc"], PER * b + PER)
                for i in range(2):
                    for jj in range(4):
                        h = 4 * i + jj
                        m = mm(PS[:, 6 + i, jj * S:(jj + 1) * S], vacc[:, h], attT[:, h], start=True, stop=True)
                    m.then_inc(s["cxp"], 1)

            pre(0)
            step(0)
            with pe.Fori(1, B - 1) as b:
                step(b)
            step(B - 1, last=True)


def output_block(nc, t, dr):
    with ExitStack() as ctx:
        def sb(name, shape, dt=F32):
            return ctx.enter_context(nc.sbuf_tensor("c_" + name, shape, dt))

        TT = TOK // 128
        EP = E // 2
        UPC = H * EP
        ow = sb("ow", [P, H * E, 2, D], F32R)
        stage = [sb(f"stage{i}", [P, E, D]) for i in range(2)]
        pick = sb("pick", [2 * E, E, 128], F32R)
        pickf = stage[0][0:2 * E, 0:E // 2].rearrange("p a d -> p (a d)").rearrange("p (e m) -> p e m", e=E)
        gs = [sb(f"gs{i}", [2 * E, H, TOK], F32R) for i in range(2)]
        cx = [sb(f"cx{i}", [P, H, TOK]) for i in range(2)]
        xr = [sb(f"xr{i}", [128, TT, D]) for i in range(2)]
        wh = [sb(f"wh{i}", [P, 2, TOK], F32R) for i in range(EP)]
        wl = [sb(f"wl{i}", [P, 2, TOK], F32R) for i in range(EP)]
        y = sb("y", [128, TT, D])
        PS = ctx.enter_context(nc.psum_tensor("ps3", [128, 8, 512], F32))
        s = {n: ctx.enter_context(nc.semaphore("c_" + n)) for n in (
            "pick0", "pickf", "pick", "stage_in0", "stage_in1", "o_hi", "o_lo", "in0", "in1", "g", "w", "w_hi", "w_lo", "used", "y1", "y", "out")}
        w = [PS[:, q].rearrange("p (e t) -> p e t", e=2) for q in range(EP)]
        block = ctx.enter_context(nc.Block())

        def chunks(eng, f):
            f(0, 0, 0)
            with eng.Fori(0, (NT - 1) // 2) as i:
                f(2 * i + 1, 1, i)
                f(2 * i + 2, 0, i + 1)

        def heads(eng, f):
            f(0)
            with eng.Fori(1, H - 1) as h:
                f(h)
            f(H - 1)

        @block.sync
        def _(sp):
            def load(c, slot):
                if not isinstance(c, int) or c > 1:
                    sp.wait_ge(s["y"], TT * (c - 2) + TT)
                sp.dma_start(gs[slot][:].bitcast(F32), dr["gscr"][:, bass.ds(c * TOK, TOK)].rearrange("(h a) t -> a h t", h=H)).then_inc(s[f"in{slot}"], 16)
                sp.dma_start(cx[slot][:], dr["cscr"][:, :, bass.ds(c * TOK, TOK)]).then_inc(s[f"in{slot}"], 16)
                sp.dma_start(xr[slot][:], dr["x1scr"].rearrange("b s d -> (b s) d")[bass.ds(c * TOK, TOK)].rearrange("(a p) d -> p a d", p=128)).then_inc(s[f"in{slot}"], 16)

            def store(c):
                sp.wait_ge(s["y"], TT * c + TT)
                sp.dma_start(dr["out"].rearrange("b s d -> (b s) d")[bass.ds(c * TOK, TOK)].rearrange("(a p) d -> p a d", p=128), y[:]).then_inc(s["out"], 16)

            load(0, 0)
            sp.wait_ge(s["pick"], 1)
            for h in range(H):
                if h >= 2:
                    sp.wait_ge(s["o_lo"], h - 1)
                sp.dma_start(stage[h % 2][:], dr["ow"][:, E * h:E * h + E]).then_inc(s[f"stage_in{h % 2}"], 16)
            load(1, 1)
            store(0)
            with sp.Fori(0, (NT - 1) // 2 - 1) as i:
                load(2 * i + 2, 0)
                store(2 * i + 1)
                load(2 * i + 3, 1)
                store(2 * i + 2)
            load(NT - 1, 0)
            store(NT - 2)
            store(NT - 1)
            sp.wait_ge(s["out"], 16 * NT)

        @block.gpsimd
        def _(pool):
            g = nc.gpsimd
            g.memset(pickf, 0.0).then_inc(s["pick0"], 1)
            pool.wait_ge(s["pick0"], 1)
            for r in range(2):
                g.affine_select(out=pickf, in_=pickf, compare_op=ALU.not_equal, fill=1.0, base=-E * r,
                                pattern=[[-1, E], [0, 128]], channel_multiplier=1).then_inc(s["pickf"], 1)
                pool.wait_ge(s["pickf"], r + 1)
            g.tensor_copy(pick[:], pickf).then_inc(s["pick"], 1)
            for h in range(H):
                pool.wait_ge(s["o_hi"], h + 1)
                g.tensor_tensor(ow[:, E * h:E * h + E, 1], stage[h % 2][:], ow[:, E * h:E * h + E, 0].bitcast(F32),
                                ALU.subtract).then_inc(s["o_lo"], 1)

        @block.scalar
        def _(act):
            a = nc.scalar

            def o_high(h):
                act.wait_ge(s[f"stage_in{h % 2}"], 16 * (h // 2) + 16)
                a.copy(ow[:, E * h:E * h + E, 0], stage[h % 2][:]).then_inc(s["o_hi"], 1)

            def head(c, h):
                for q in range(EP):
                    n = UPC * c + EP * h + q
                    act.wait_ge(s["w"], n + 1)
                    if not (isinstance(n, int) and n < EP):
                        act.wait_ge(s["used"], UPC * c + EP * h + q - (EP - 1) if isinstance(n, int) else n - (EP - 1))
                    a.copy(wh[q][:], w[q]).then_inc(s["w_hi"], 1)

            o_high(0)
            for h in range(H):
                if h + 1 < H:
                    o_high(h + 1)
                head(0, h)
            with act.Fori(1, NT) as c:
                head(c, 0)
                with act.Fori(1, H) as h:
                    head(c, h)

        @block.vector
        def _(dve):
            v = nc.vector

            def low(n, q):
                dve.wait_ge(s["w_hi"], n + 1)
                v.tensor_tensor(wl[q][:], w[q], wh[q][:].bitcast(F32), ALU.subtract).then_inc(s["w_lo"], 1)

            def head(c, slot, h):
                for q in range(EP):
                    n = UPC * c + EP * h + q
                    dve.wait_ge(s["g"], n + 1)
                    v.tensor_tensor(w[q], spread(cx[slot][:, h], 1, 2), w[q], ALU.mult).then_inc(s["w"], 1)
                    if q:
                        low(n - 1, q - 1)
                low(UPC * c + EP * h + EP - 1, EP - 1)

            def chunk(c, slot, turn):
                dve.wait_ge(s[f"in{slot}"], 48 * turn + 48)
                heads(dve, lambda h: head(c, slot, h))
                dve.wait_ge(s["used"], UPC * c + UPC)
                if not is_first(c):
                    dve.wait_ge(s["out"], 16 * (c - 1) + 16)
                for i in range(TT):
                    v.tensor_tensor(xr[slot][:, i], PS[:, 4 + i, D:2 * D], xr[slot][:, i], ALU.add).then_inc(s["y1"], 1)
                for i in range(TT):
                    dve.wait_ge(s["y1"], TT * c + i + 1)
                    v.tensor_tensor(y[:, i], PS[:, 4 + i, 0:D], xr[slot][:, i], ALU.add).then_inc(s["y"], 1)

            chunks(dve, chunk)

        @block.tensor
        def _(pe):
            mm = nc.tensor.matmul

            def spread_gates(c, slot, h, q):
                for e in range(2):
                    m = mm(PS[:, q, e * TOK:(e + 1) * TOK], pick[:, 2 * q + e, :], gs[slot][:, h], start=True, stop=True)
                m.then_inc(s["g"], 1)

            def experts(c, h, q, first):
                if is_first(c) and q == 0:
                    pe.wait_ge(s["o_lo"], h + 1)
                pe.wait_ge(s["w_lo"], UPC * c + EP * h + q + 1)
                if first and not is_first(c):
                    pe.wait_ge(s["y"], TT * (c - 1) + TT)
                for e in range(2):
                    he = h * E + 2 * q + e
                    for i in range(TT):
                        r = slice(128 * i, 128 * i + 128)
                        mm(PS[:, 4 + i], wh[q][:, e, r], ow[:, he], start=(first and e == 0), stop=False, skip_group_check=True)
                        m = mm(PS[:, 4 + i, 0:D], wl[q][:, e, r], ow[:, he, 0], start=False,
                               stop=False, skip_group_check=True)
                m.then_inc(s["used"], 1)

            def chunk(c, slot, turn):
                pe.wait_ge(s[f"in{slot}"], 48 * turn + 48)
                for q in range(EP):
                    spread_gates(c, slot, 0, q)

                def head(h):
                    for q in range(EP):
                        experts(c, h, q, first=isinstance(h, int) and h == 0 and q == 0)
                        if not (isinstance(h, int) and h == H - 1):
                            spread_gates(c, slot, h + 1, q)
                heads(pe, head)

            pe.wait_ge(s["pick"], 1)
            chunks(pe, chunk)


def weights(w):
    return w.T.reshape(KD, 128, -1).transpose(1, 0, 2)


def laid_out(i):
    xc, ff = "L0_xcond_", "L0_ffn_"

    def pad(a):
        return np.pad(a, [(0, 0)] * (a.ndim - 1) + [(0, SKP - SK)])

    return {
        "x": i["x"],
        "ctxT": pad(i["ctx_1024"].transpose(0, 2, 1).reshape(B, KD, 128, SK).transpose(0, 2, 1, 3)),
        "tau": i["condB_tau"], "delta": pad(i["fside_BxS2_0"]),
        "wq": weights(i[xc + "Wq"]).reshape(128, -1), "wk": weights(i[xc + "Wk"]).reshape(128, -1),
        "wv": weights(i[xc + "Wv"]).reshape(128, -1), "wo": weights(i[xc + "Wo"]).reshape(128, -1),
        "bq": i[xc + "bq"].reshape(KD, 128).T, "bk": i[xc + "bk"].reshape(KD, 128).T,
        "bv": i[xc + "bv"], "bo": i[xc + "bo"],
        "vw": i[ff + "v_w"].reshape(H, E, KD, 128, P).transpose(3, 2, 0, 1, 4).reshape(128, KD, H * E * P),
        "qkw": np.concatenate([weights(i[ff + "q_w"]), weights(i[ff + "k_w"])], axis=2),
        "sel_v": weights(i[ff + "sel_v_w"]), "sel_o": weights(i[ff + "sel_o_w"]),
        "route": i[ff + "route_scale"],
        "ow": i[ff + "o_w"].transpose(1, 0, 2),
    }


def build(nc, dr):
    with ExitStack() as ctx:
        t = {"ident": ctx.enter_context(nc.sbuf_tensor("ident", [128, 128], F32))}
        ident_done = ctx.enter_context(nc.semaphore("ident_done"))
        with nc.Block() as block:
            @block.gpsimd
            def _(pool):
                nc.gpsimd.memset(t["ident"][:], 0.0).then_inc(ident_done, 1)
                pool.wait_ge(ident_done, 1)
                nc.gpsimd.affine_select(out=t["ident"][:], in_=t["ident"][:], compare_op=ALU.not_equal, fill=1.0, base=0,
                                        pattern=[[-1, 128]], channel_multiplier=1).then_inc(ident_done, 1)
                pool.wait_ge(ident_done, 2)
        with ExitStack() as both:
            for n in ("v_hi", "v_lo"):
                t[n] = both.enter_context(nc.sbuf_tensor(n, [128, KD, H * E * P], F32R))
            cross_block(nc, t, dr)
            attend_block(nc, t, dr)
        output_block(nc, t, dr)


def kernel(**inputs):
    import numpy as np
    import concourse.bacc as bacc
    from concourse.bass_utils import run_bass_kernel_spmd as run

    nc = bacc.Bacc("TRN2", target_bir_lowering=False, num_devices=1)
    arrays, dr = {}, {}
    for name, a in laid_out({k: np.asarray(v) for k, v in inputs.items()}).items():
        arrays["in_" + name] = np.ascontiguousarray(a)
        dr[name] = nc.dram_tensor("in_" + name, a.shape, F32, kind="ExternalInput").ap()
    for name, shape in (("kscr", [2, 128, KD, SKP]), ("qscr", [2, 128, KD, S]), ("dscr", [2, B, SKP]), ("x1scr", [B, S, D]),
                        ("x2scr", [B, 128, 2, KD, S]), ("gscr", [128, B * S]), ("cscr", [P, H, B * S])):
        dr[name] = nc.dram_tensor(name, shape, F32, kind="Internal").ap()
    dr["out"] = nc.dram_tensor("out", [B, S, D], F32, kind="ExternalOutput").ap()
    build(nc, dr)
    return run(nc, [arrays], core_ids=[0]).results[0]["out"]
```

```python
from contextlib import ExitStack

import numpy as np

import concourse.bass as bass
from concourse import mybir

F32 = mybir.dt.float32
F32R = mybir.dt.float32r
ALU = mybir.AluOpType
ACT = mybir.ActivationFunctionType
AX = mybir.AxisListType

B, S, D = 16, 112, 256
SK, KC = 375, 125
NC = SK // KC
SKP = SK + SK % 2
XH, DK = 16, 16
H, E, P = 8, 8, 128
KD = D // 128
HALF = XH // 2
QUAD = HALF // 2
HE = H - 3
VCH = HE * E * P // B
DV = 32
UN = 4 * NC
RING = 4
LEAD = RING - 1
V_AT = (3, 9)
K_AT = (3, 5, 6, 7)
EPS = 1e-5
TOK = 256
NT = B * S // TOK
BIG = 1e30

ROW_D = 3 * DK
ROW_M = ROW_D + 2
ROWS_S = ROW_M


def spread(ap, axis, n):
    ap = ap.unsqueeze(axis)
    shape = list(ap.shape)
    shape[axis] = n
    return ap.broadcast_to(shape)


def is_first(b):
    return isinstance(b, int) and b == 0


def cross_block(nc, t, dr):
    with ExitStack() as ctx:
        def sb(name, shape, dt=F32):
            return ctx.enter_context(nc.sbuf_tensor("a_" + name, shape, dt))

        names = ("wk", "wq", "wv", "wo")
        w_hi = {n: sb(n + "_hi", [128, KD, D], F32R) for n in names}
        w_lo = {n: sb(n + "_lo", [128, KD, D], F32R) for n in names}
        bq = sb("bq", [128, KD]); bk = sb("bk", [128, KD])
        bv = sb("bv", [128, D]); bo = sb("bo", [128, D])
        tau4 = sb("tau4", [128, B])
        tick = sb("tick", [128, 1])
        half_pow = sb("half_pow", [128, 1])
        staging = sb("staging", [128, 2 * KD * D])
        vstage = staging[:, 0:KD * VCH].rearrange("p (k c) -> p k c", k=KD)
        cst = sb("cst", [128, KD, SKP])
        ch = sb("ch", [128, KD, SKP], F32R); cl = sb("cl", [128, KD, SKP], F32R)
        d_in, d_q, d_hi, d_lo = cst[0:B, 0], cst[0:B, 1], ch[0:B, 0], cl[0:B, 0]
        xin = sb("xin", [S, D]); xb = sb("xb", [S, D])
        xq = sb("xq", [128, D]); xn = xq[0:S, :]
        stat = sb("stat", [S, 6]); mv = sb("mv", [S, 2]); ve = sb("ve", [S, 1]); rstd = sb("rstd", [S, 1])
        stat2 = sb("stat2", [S, 6]); mv2 = sb("mv2", [S, 2]); ve2 = sb("ve2", [S, 1]); rstd2 = sb("rstd2", [S, 1])
        xth = sb("xth", [128, KD, S], F32R); xtl = sb("xtl", [128, KD, S], F32R)
        ah, al = xth, xtl
        qf = xq[:, 0:KD * S].rearrange("p (k s) -> p k s", k=KD)
        qh = sb("qh", [128, KD, S], F32R); ql = sb("ql", [128, KD, S], F32R)
        kh = sb("kh", [128, KD, SKP], F32R); kl = sb("kl", [128, KD, SKP], F32R)
        kst = [sb(f"kst{i}", [128, HALF, SKP], F32R) for i in range(2)]
        qst = [sb(f"qst{i}", [128, HALF, 2 * S], F32R) for i in range(2)]
        vxh = sb("vxh", [KC, NC, XH, DV], F32R); vxl = sb("vxl", [KC, NC, XH, DV], F32R)
        vf = sb("vf", [KC, NC, XH, DK])
        nm = sb("nm", [S, 2, 2, QUAD])
        mh = [sb(f"mh{n}", [HALF, S], F32R) for n in range(2)]
        ml = [sb(f"ml{n}", [HALF, S], F32R) for n in range(2)]
        ph = [sb(f"ph{i}", [KC, 4 * S], F32R) for i in range(RING)]
        pl = [sb(f"pl{i}", [KC, 4 * S], F32R) for i in range(RING)]
        pf = [sb(f"pf{i}", [KC, 4 * S]) for i in range(RING // 2)]
        od = [sb(f"od{i}", [128, S]) for i in range(2)]
        rs = sb("rs", [S, XH]); af = sb("af", [S, D])
        x1 = sb("x1", [S, D]); x2 = af
        x2s = sb("x2s", [128, 2, KD, S], F32R)
        PS = ctx.enter_context(nc.psum_tensor("ps1", [128, 8, 512], F32))
        bank7 = PS[:, 7, 0:KD * S].rearrange("p (k s) -> p k s", k=KD)

        s = {n: ctx.enter_context(nc.semaphore("a_" + n)) for n in (
            "stage_in0", "stage_in1", "small_in", "w_hi", "w_lo", "d_q", "d_hi", "d_lo", "d_out", "zeros", "ones", "tau", "pow_c",
            "vst_in", "v_hi", "v_lo",
            "ctx_in", "x_in", "xb_in", "c_hi", "c_lo", "st", "mv", "ve", "rstd", "xn", "xb", "xT", "xt_hi", "xt_lo",
            "kp", "k_hi", "k_lo", "qp", "qf", "q_hi", "q_lo", "k_out", "q_out", "kst_in", "qst_in",
            "vp", "vf", "vx_hi", "vx_lo", "sc", "mx", "mT", "m_hi", "m_lo", "m_in0", "m_in1", "st_sc", "p", "p_hi", "p_lo", "pv", "od", "oT", "rs", "af",
            "aT", "a_hi", "a_lo", "op", "x1", "x1_out", "st2", "mv2", "ve2", "rstd2", "x2", "x2T", "x2_hi", "x2_lo", "x2_out")}
        block = ctx.enter_context(nc.Block())
        kscr, qscr, dscr = dr["kscr"], dr["qscr"], dr["dscr"]
        ident = t["ident"]
        stage = [staging[:, KD * D * i:KD * D * i + KD * D] for i in range(2)]

        def own_queries(g4, j):
            r = slice(DV * j, DV * j + DV)
            return od[g4 % 2][r], PS[r, 5 + g4 % 2, S * j:S * j + S]

        def more(b, n):
            return not isinstance(b, int) or b + n < B

        def run(eng, step):
            step(0, 0)
            step(1, 1)
            with eng.Fori(1, B // 2 - 1) as i:
                step(2 * i, 0)
                step(2 * i + 1, 1)
            step(B - 2, 0)
            step(B - 1, 1)

        @block.sync
        def _(sp):
            def load_ctx(b):
                if not is_first(b):
                    sp.wait_ge(s["c_lo"], b)
                sp.dma_start(cst[:], dr["ctxT"][b]).then_inc(s["ctx_in"], 16)

            def load_x(b):
                if not is_first(b):
                    sp.wait_ge(s["xn"], b)
                sp.dma_start(xin[:], dr["x"][b]).then_inc(s["x_in"], 16)

            def load_residual(b):
                if not is_first(b):
                    sp.wait_ge(s["x1"], b)
                sp.dma_start(xb[:], dr["x"][b]).then_inc(s["xb_in"], 16)

            for i, n in enumerate(names):
                if i >= 2:
                    sp.wait_ge(s["w_lo"], i - 1)
                sp.dma_start(stage[i % 2], dr[n]).then_inc(s[f"stage_in{i % 2}"], 16)
                if i == 1:
                    for o, a in ((d_in, dr["delta"]), (bq[:], dr["bq"]), (bk[:], dr["bk"]), (bv[:], spread(dr["bv"], 0, 128)),
                                 (bo[:], spread(dr["bo"], 0, 128)), (tau4[:], spread(dr["tau"], 0, 128))):
                        sp.dma_start(o, a).then_inc(s["small_in"], 16)
                    load_x(0)
                    load_residual(0)
                    sp.wait_ge(s["d_hi"], 1)
                    sp.wait_ge(s["d_lo"], 1)
                    sp.dma_start(dscr[0], d_hi.bitcast(F32)).then_inc(s["d_out"], 16)
                    sp.dma_start(dscr[1], d_lo.bitcast(F32)).then_inc(s["d_out"], 16)
                    sp.wait_ge(s["pow_c"], 2)
                    for j in (2, 3):
                        sp.dma_start(dscr[j], vxh[0:B].rearrange("p c h d -> p (c h d)")[:, 0:SKP].bitcast(F32)).then_inc(s["d_out"], 16)
                    sp.wait_ge(s["d_out"], 64)
                    load_ctx(0)
            sp.wait_ge(s["ones"], 4)

            def k_bounce(b, before=None):
                if not is_first(b):
                    sp.wait_ge(s["kst_in"], 128 * before + 128)
                sp.wait_ge(s["k_hi"], 2 * b + 2)
                sp.wait_ge(s["k_lo"], 2 * b + 2)
                sp.dma_start(kscr[0], kh[:].bitcast(F32)).then_inc(s["k_out"], 16)
                sp.dma_start(kscr[1], kl[:].bitcast(F32)).then_inc(s["k_out"], 16)

            def q_bounce(b, before=None):
                if not is_first(b):
                    sp.wait_ge(s["qst_in"], 96 * before + 96)
                sp.wait_ge(s["q_hi"], b + 1)
                sp.wait_ge(s["q_lo"], b + 1)
                sp.dma_start(qscr[0], qh[:].bitcast(F32)).then_inc(s["q_out"], 16)
                sp.dma_start(qscr[1], ql[:].bitcast(F32)).then_inc(s["q_out"], 16)

            def stack(b, slot):
                sp.wait_ge(s["k_out"], 32 * b + 32)
                sp.wait_ge(s["q_out"], 32 * b + 32)
                for half in range(2):
                    for j, part in enumerate((0, 1, 0)):
                        r = 64 * half + DK * j
                        src = kscr[part, :, half].rearrange("(i r) k -> r i k", r=DK)
                        sp.dma_start(kst[slot][r:r + DK].bitcast(F32), src).then_inc(s["kst_in"], 16)
                    for j, part in enumerate((0, 0, 1)):
                        r = 64 * half + DK * j
                        src = qscr[part, :, half].rearrange("(i r) k -> r i k", r=DK)
                        sp.dma_start(qst[slot][r:r + DK, :, S * half:S * half + S].bitcast(F32), src).then_inc(s["qst_in"], 16)
                    r = 64 * half + ROW_D
                    sp.dma_start(kst[slot][r:r + 4].bitcast(F32), spread(dscr[:, b, :], 1, HALF)).then_inc(s["kst_in"], 16)

            def maxima(b, n, slot):
                sp.wait_ge(s["m_hi"], 2 * b + n + 1)
                sp.wait_ge(s["m_lo"], 2 * b + n + 1)
                for half in range(2):
                    for j, m in enumerate((mh, ml)):
                        r = 64 * half + ROW_M + j
                        sp.dma_start(qst[slot][r:r + 1, QUAD * n:QUAD * n + QUAD, S * half:S * half + S].bitcast(F32),
                                     m[n][QUAD * half:QUAD * half + QUAD, :].bitcast(F32)).then_inc(s[f"m_in{n}"], 16)

            def store_x2(b):
                sp.wait_ge(s["x2_hi"], b + 1)
                sp.wait_ge(s["x2_lo"], b + 1)
                sp.dma_start(dr["x2scr"][b], x2s[:].bitcast(F32)).then_inc(s["x2_out"], 16)

            def finish(b):
                sp.wait_ge(s["x1"], b + 1)
                sp.dma_start(dr["x1scr"][b], x1[:]).then_inc(s["x1_out"], 16)

            def step(b, slot):
                if more(b, 2):
                    load_x(b + 2)
                    load_ctx(b + 2)
                if is_first(b):
                    sp.wait_ge(s["w_lo"], len(names))
                else:
                    sp.wait_ge(s["v_lo"], b)
                sp.dma_start(vstage, dr["vw"][:, :, bass.ds(b * VCH, VCH)]).then_inc(s["vst_in"], 16)
                if not is_first(b):
                    finish(b - 1)
                    load_residual(b)
                for n in range(2):
                    maxima(b, n, slot)
                if not is_first(b):
                    store_x2(b - 1)
                if more(b, 1):
                    k_bounce(b + 1, b)
                    q_bounce(b + 1, b)
                    stack(b + 1, 1 - slot)

            load_x(1)
            k_bounce(0)
            q_bounce(0)
            stack(0, 0)
            load_ctx(1)
            run(sp, step)
            finish(B - 1)
            store_x2(B - 1)
            sp.wait_ge(s["x1_out"], 16 * B)
            sp.wait_ge(s["x2_out"], 16 * B)

        @block.gpsimd
        def _(pool):
            g = nc.gpsimd
            g.memset(half_pow[:], -0.5).then_inc(s["pow_c"], 1)
            g.memset(vxh[:].bitcast(F32), 1.0).then_inc(s["pow_c"], 1)
            g.memset(vxl[:].bitcast(F32), 0.0).then_inc(s["pow_c"], 1)
            for i in range(2):
                g.memset(kst[i][:].bitcast(F32), 0.0).then_inc(s["zeros"], 1)
                g.memset(qst[i][:].bitcast(F32), 0.0).then_inc(s["zeros"], 1)
            pool.wait_ge(s["zeros"], 4)
            for half in range(2):
                for i in range(2):
                    g.memset(qst[i][64 * half + 32:64 * half + 64, :, S * half:S * half + S].bitcast(F32), 1.0).then_inc(s["ones"], 1)
            pool.wait_ge(s["ones"], 4)
            pool.wait_ge(s["pow_c"], 3)

            def c_low(b):
                pool.wait_ge(s["c_hi"], b + 1)
                g.tensor_tensor(cl[:], cst[:], ch[:].bitcast(F32), ALU.subtract).then_inc(s["c_lo"], 1)

            def inverse_root(b):
                pool.wait_ge(s["ve"], b + 1)
                g.tensor_tensor(rstd[:], ve[:], half_pow[0:S, :], ALU.pow).then_inc(s["rstd"], 1)

            def q_low(b):
                pool.wait_ge(s["q_hi"], b + 1)
                g.tensor_tensor(ql[:], qf, qh[:].bitcast(F32), ALU.subtract).then_inc(s["q_lo"], 1)

            def residual(b):
                pool.wait_ge(s["xb_in"], 16 * b + 16)
                if is_first(b):
                    pool.wait_ge(s["small_in"], 96)
                g.tensor_tensor(xb[:], xb[:], bo[0:S, :], ALU.add).then_inc(s["xb"], 1)

            def values_low(b):
                pool.wait_ge(s["vx_hi"], b + 1)
                g.tensor_tensor(vxl[:, :, :, 0:DK], vf[:], vxh[:, :, :, 0:DK].bitcast(F32), ALU.subtract).then_inc(s["vx_lo"], 1)

            def v_split(b):
                pool.wait_ge(s["vst_in"], 16 * b + 16)
                hi = t["v_hi"][:, :, bass.ds(b * VCH, VCH)]
                lo = t["v_lo"][:, :, bass.ds(b * VCH, VCH)]
                g.tensor_copy(hi, vstage).then_inc(s["v_hi"], 1)
                pool.wait_ge(s["v_hi"], b + 1)
                g.tensor_tensor(lo, vstage, hi.bitcast(F32), ALU.subtract).then_inc(s["v_lo"], 1)

            def finish(b):
                pool.wait_ge(s["ve2"], b + 1)
                g.tensor_tensor(rstd2[:], ve2[:], half_pow[0:S, :], ALU.pow).then_inc(s["rstd2"], 1)

            def step(b, slot):
                values_low(b)
                if not is_first(b):
                    finish(b - 1)
                v_split(b)
                if more(b, 1):
                    q_low(b + 1)
                if not is_first(b):
                    residual(b)
                if more(b, 2):
                    inverse_root(b + 2)
                    c_low(b + 2)

            inverse_root(0)
            residual(0)
            c_low(0)
            q_low(0)
            inverse_root(1)
            c_low(1)
            run(pool, step)
            finish(B - 1)

        @block.scalar
        def _(act):
            a = nc.scalar

            def c_high(b):
                act.wait_ge(s["ctx_in"], 16 * b + 16)
                if not is_first(b):
                    act.wait_ge(s["vp"], 2 * b)
                a.copy(ch[:], cst[:]).then_inc(s["c_hi"], 1)

            def x_high(b):
                act.wait_ge(s["xT"], b + 1)
                a.copy(xth[:], bank7).then_inc(s["xt_hi"], 1)

            def k_high(b):
                if not is_first(b):
                    act.wait_ge(s["k_out"], 32 * b)
                for m in range(KD):
                    act.wait_ge(s["kp"], KD * b + m + 1)
                    a.activation(kh[:, m], PS[:, 4 + m, 0:SKP], ACT.Identity, bias=bk[:, m:m + 1]).then_inc(s["k_hi"], 1)

            def q_high(b):
                act.wait_ge(s["qf"], 2 * b + 2)
                if not is_first(b):
                    act.wait_ge(s["q_out"], 32 * b)
                a.copy(qh[:], qf).then_inc(s["q_hi"], 1)

            def values_high(b):
                act.wait_ge(s["vf"], 2 * b + 2)
                if not is_first(b):
                    act.wait_ge(s["pv"], UN * b)
                a.copy(vxh[:, :, :, 0:DK], vf[:]).then_inc(s["vx_hi"], 1)

            def x2_high(b):
                act.wait_ge(s["x2T"], b + 1)
                if not is_first(b):
                    act.wait_ge(s["x2_out"], 16 * b)
                a.copy(x2s[:, 0], bank7).then_inc(s["x2_hi"], 1)

            def max_high(b, n):
                act.wait_ge(s["mT"], 2 * b + n + 1)
                if not is_first(b):
                    act.wait_ge(s[f"m_in{n}"], 64 * b)
                a.copy(mh[n][:], PS[0:HALF, 6, 128 * n:128 * n + S]).then_inc(s["m_hi"], 1)

            def diagonal_last(b):
                act.wait_ge(s["pv"], UN * b + UN)
                act.wait_ge(s["oT"], 4 * b + 2)
                for j in range(4):
                    o, i = own_queries(3, j)
                    m = a.copy(o, i)
                m.then_inc(s["od"], 1)

            def attention_high(b):
                act.wait_ge(s["aT"], b + 1)
                a.copy(ah[:], bank7).then_inc(s["a_hi"], 1)

            def step(b, slot):
                if not is_first(b):
                    diagonal_last(b - 1)
                values_high(b)
                if not is_first(b):
                    attention_high(b - 1)
                if more(b, 1):
                    x_high(b + 1)
                max_high(b, 0)
                if not is_first(b):
                    x2_high(b - 1)
                if more(b, 1):
                    k_high(b + 1)
                max_high(b, 1)
                for u in range(UN):
                    act.wait_ge(s["st_sc"], UN * b + u + 1)
                    if u >= 2 or not is_first(b):
                        act.wait_ge(s["p_lo"], UN * b + u - 1)
                    a.activation(pf[u % 2][:], PS[0:KC, u % RING, 0:4 * S], ACT.Exp).then_inc(s["p"], 1)
                    if u >= RING or not is_first(b):
                        act.wait_ge(s["pv"], UN * b + u - RING + 1)
                    a.activation(ph[u % RING][:], PS[0:KC, u % RING, 0:4 * S], ACT.Exp).then_inc(s["p_hi"], 1)
                    if u == 1 and more(b, 1):
                        q_high(b + 1)
                if more(b, 2):
                    c_high(b + 2)

            act.wait_ge(s["d_q"], 1)
            a.copy(d_hi, d_q).then_inc(s["d_hi"], 1)
            for i, n in enumerate(names):
                act.wait_ge(s[f"stage_in{i % 2}"], 16 * (i // 2) + 16)
                a.copy(w_hi[n][:].rearrange("p k d -> p (k d)"), stage[i % 2]).then_inc(s["w_hi"], 1)
            c_high(0)
            x_high(0)
            k_high(0)
            q_high(0)
            c_high(1)
            run(act, step)
            diagonal_last(B - 1)
            attention_high(B - 1)
            x2_high(B - 1)

        @block.vector
        def _(dve):
            v = nc.vector

            def stats(b):
                dve.wait_ge(s["x_in"], 16 * b + 16)
                v.bn_stats(stat[:], xin[:]).then_inc(s["st"], 1)
                dve.wait_ge(s["st"], b + 1)
                v.memset(tick[:], 0.0)
                v.bn_aggr(mv[:], stat[:]).then_inc(s["mv"], 1)
                dve.wait_ge(s["mv"], b + 1)
                v.tensor_scalar(ve[:], mv[:, 1:2], EPS, None, ALU.add).then_inc(s["ve"], 1)

            def norm(b):
                dve.wait_ge(s["rstd"], b + 1)
                if not is_first(b):
                    dve.wait_ge(s["q_lo"], b)
                v.tensor_scalar(xn, xin[:], mv[:, 0:1], rstd[:], ALU.subtract, ALU.mult).then_inc(s["xn"], 1)

            def x_low(b):
                dve.wait_ge(s["xt_hi"], b + 1)
                v.tensor_tensor(xtl[:], bank7, xth[:].bitcast(F32), ALU.subtract).then_inc(s["xt_lo"], 1)

            def k_low(b, m):
                dve.wait_ge(s["k_hi"], KD * b + m + 1)
                v.scalar_tensor_tensor(out=kl[:, m], in0=PS[:, 4 + m, 0:SKP], scalar=bk[:, m:m + 1],
                                       in1=kh[:, m].bitcast(F32), op0=ALU.add, op1=ALU.subtract).then_inc(s["k_lo"], 1)

            def max_low(b, n):
                dve.wait_ge(s["m_hi"], 2 * b + n + 1)
                if not is_first(b):
                    dve.wait_ge(s[f"m_in{n}"], 64 * b)
                v.tensor_tensor(ml[n][:], PS[0:HALF, 6, 128 * n:128 * n + S], mh[n][:].bitcast(F32), ALU.subtract).then_inc(s["m_lo"], 1)

            def q_scaled(b):
                dve.wait_ge(s["qp"], b + 1)
                for m in range(KD):
                    v.tensor_scalar(qf[:, m], PS[:, 7, m * S:(m + 1) * S], bq[:, m:m + 1], tau4[:, bass.ds(b, 1)],
                                    ALU.add, ALU.mult).then_inc(s["qf"], 1)

            def values(b, c):
                dve.wait_ge(s["vp"], 2 * b + c + 1)
                k = 2 - c
                if c == 0 and not is_first(b):
                    dve.wait_ge(s["vx_lo"], b)
                v.tensor_tensor(vf[:, 2 * c:2 * c + k],
                                PS[0:KC, 7, 0:k * D].rearrange("p (c h d) -> p c h d", c=k, h=XH),
                                spread(bv[0:KC, :].rearrange("p (h d) -> p h d", h=XH), 1, k), ALU.add).then_inc(s["vf"], 1)

            def diagonal(b, g4):
                dve.wait_ge(s["pv"], UN * b + NC * (g4 + 1))
                if g4 >= 2 or not is_first(b):
                    dve.wait_ge(s["oT"], 4 * b + g4 - 1)
                for j in range(4):
                    o, i = own_queries(g4, j)
                    m = v.tensor_copy(o, i)
                m.then_inc(s["od"], 1)

            def x2_norm(b):
                dve.wait_ge(s["rstd2"], b + 1)
                v.tensor_scalar(x2[:], x1[:], mv2[:, 0:1], rstd2[:], ALU.subtract, ALU.mult).then_inc(s["x2"], 1)

            def x2_low(b):
                dve.wait_ge(s["x2_hi"], b + 1)
                v.tensor_tensor(x2s[:, 1], bank7, x2s[:, 0].bitcast(F32), ALU.subtract).then_inc(s["x2_lo"], 1)

            def attended(b):
                dve.wait_ge(s["oT"], 4 * b + 4)
                o = PS[0:S, 4].rearrange("p (h d) -> p h d", h=XH)
                v.reciprocal(rs[:], o[:, :, DK]).then_inc(s["rs"], 1)
                dve.wait_ge(s["rs"], b + 1)
                v.tensor_tensor(af[:].rearrange("p (h d) -> p h d", h=XH), o[:, :, 0:DK],
                                spread(rs[:], 2, DK), ALU.mult).then_inc(s["af"], 1)

            def attention_low(b):
                dve.wait_ge(s["a_hi"], b + 1)
                v.tensor_tensor(al[:], bank7, ah[:].bitcast(F32), ALU.subtract).then_inc(s["a_lo"], 1)

            def residual_sum(b):
                dve.wait_ge(s["op"], b + 1)
                dve.wait_ge(s["xb"], b + 1)
                if not is_first(b):
                    dve.wait_ge(s["x1_out"], 16 * b)
                v.tensor_tensor(x1[:], PS[0:S, 7, 0:D], xb[:], ALU.add).then_inc(s["x1"], 1)
                dve.wait_ge(s["x1"], b + 1)
                v.bn_stats(stat2[:], x1[:]).then_inc(s["st2"], 1)
                dve.wait_ge(s["st2"], b + 1)
                v.memset(tick[:], 0.0)
                v.bn_aggr(mv2[:], stat2[:]).then_inc(s["mv2"], 1)
                dve.wait_ge(s["mv2"], b + 1)
                v.tensor_scalar(ve2[:], mv2[:, 1:2], EPS, None, ALU.add).then_inc(s["ve2"], 1)

            def step(b, slot):
                late = not is_first(b)
                for g in range(8):
                    dve.wait_ge(s["sc"], 8 * b + g + 1)
                    if g == 0 and late:
                        dve.wait_ge(s["mT"], 2 * b)
                    bank = 2 * (g % 2)
                    v.tensor_reduce(nm[:, g // QUAD, :, g % QUAD], PS[0:S, bank:bank + 2, 0:SK], AX.X, ALU.max,
                                    negate=True).then_inc(s["mx"], 1)
                    if g == 1 and late:
                        attended(b - 1)
                    if g == 2 and late:
                        attention_low(b - 1)
                    if g == 4 and late:
                        residual_sum(b - 1)
                    if g == 5:
                        max_low(b, 0)
                        if more(b, 1):
                            x_low(b + 1)
                    if g == 6 and late:
                        x2_norm(b - 1)
                    if g == 7 and late:
                        x2_low(b - 1)
                if more(b, 1):
                    k_low(b + 1, 0)
                max_low(b, 1)
                if more(b, 1):
                    k_low(b + 1, 1)
                for u in range(UN):
                    dve.wait_ge(s["p_hi"], UN * b + u + 1)
                    v.tensor_tensor(pl[u % RING][:], pf[u % 2][:], ph[u % RING][:].bitcast(F32),
                                    ALU.subtract).then_inc(s["p_lo"], 1)
                    if u == 0 and more(b, 1):
                        q_scaled(b + 1)
                    if u == 2 and more(b, 2):
                        stats(b + 2)
                    if u % NC == 1 and u > NC:
                        diagonal(b, u // NC - 1)
                    if u == 5 and more(b, 1):
                        values(b + 1, 0)
                    if u == 9 and more(b, 1):
                        values(b + 1, 1)
                if more(b, 2):
                    norm(b + 2)

            dve.wait_ge(s["small_in"], 96)
            v.tensor_scalar(d_q, d_in, 0.25, None, ALU.mult).then_inc(s["d_q"], 1)
            v.tensor_scalar(tau4[:], tau4[:], 0.25, None, ALU.mult).then_inc(s["tau"], 1)
            dve.wait_ge(s["d_hi"], 1)
            v.tensor_tensor(d_lo, d_q, d_hi.bitcast(F32), ALU.subtract).then_inc(s["d_lo"], 1)
            stats(0)
            for i, n in enumerate(names):
                dve.wait_ge(s["w_hi"], i + 1)
                v.tensor_tensor(w_lo[n][:].rearrange("p k d -> p (k d)"), stage[i % 2],
                                w_hi[n][:].rearrange("p k d -> p (k d)").bitcast(F32), ALU.subtract).then_inc(s["w_lo"], 1)
            dve.wait_ge(s["tau"], 1)
            norm(0)
            x_low(0)
            k_low(0, 0)
            k_low(0, 1)
            q_scaled(0)
            stats(1)
            dve.wait_ge(s["pow_c"], 3)
            dve.wait_ge(s["d_out"], 64)
            values(0, 0)
            values(0, 1)
            norm(1)
            run(dve, step)
            attended(B - 1)
            attention_low(B - 1)
            residual_sum(B - 1)
            x2_norm(B - 1)
            x2_low(B - 1)

        @block.tensor
        def _(pe):
            mm = nc.tensor.matmul

            def products(out, pairs, first=True, last=True):
                n, total = 0, 3 * len(pairs)
                for lh, ll, rh, rl in pairs:
                    for l, r in ((ll, rh), (lh, rl), (lh, rh)):
                        m = mm(out, l, r, start=(first and n == 0), stop=(last and n == total - 1))
                        n += 1
                return m

            def transposed(src):
                for k in range(KD):
                    m = nc.tensor.transpose(PS[:, 7, k * S:(k + 1) * S], src[:, 128 * k:128 * k + 128], ident[0:S, 0:S])
                return m

            def x_transpose(b):
                pe.wait_ge(s["xn"], b + 1)
                if not isinstance(b, int) or b > 1:
                    pe.wait_ge(s["x1"], b - 1)
                transposed(xn).then_inc(s["xT"], 1)

            def k_part(b, m, k):
                if m == 0 and k == 0:
                    if is_first(b):
                        pe.wait_ge(s["w_lo"], 1)
                    pe.wait_ge(s["c_lo"], b + 1)
                c = slice(128 * m, 128 * m + 128)
                x = products(PS[:, 4 + m, 0:SKP], [(w_hi["wk"][:, k, c], w_lo["wk"][:, k, c], ch[:, k], cl[:, k])],
                             first=(k == 0), last=(k == KD - 1))
                if k == KD - 1:
                    x.then_inc(s["kp"], 1)

            def q_project(b):
                if is_first(b):
                    pe.wait_ge(s["w_lo"], 2)
                pe.wait_ge(s["xt_lo"], b + 1)
                for m in range(KD):
                    c = slice(128 * m, 128 * m + 128)
                    x = products(PS[:, 7, m * S:(m + 1) * S],
                                 [(w_hi["wq"][:, k, c], w_lo["wq"][:, k, c], xth[:, k], xtl[:, k]) for k in range(KD)])
                x.then_inc(s["qp"], 1)

            def v_project(b, part):
                if is_first(b) and part == 0:
                    pe.wait_ge(s["w_lo"], len(names))
                if part == 0:
                    pe.wait_ge(s["qf"], 2 * b + 2)
                else:
                    pe.wait_ge(s["vf"], 2 * b + 1)
                for c in ((0, 1), (2,))[part]:
                    r = slice(KC * c, KC * c + KC)
                    x = products(PS[0:KC, 7, D * (c % 2):D * (c % 2) + D],
                                 [(ch[:, k, r], cl[:, k, r], w_hi["wv"][:, k], w_lo["wv"][:, k]) for k in range(KD)])
                x.then_inc(s["vp"], 1)

            def max_transpose(b, n):
                if n:
                    pe.wait_ge(s["m_lo"], 2 * b + n)
                nc.tensor.transpose(PS[0:HALF, 6, 128 * n:128 * n + S], nm[:, n].rearrange("p a i -> p (a i)"), ident[0:S, 0:S]).then_inc(s["mT"], 1)

            def attended(b, g4):
                pe.wait_ge(s["od"], 4 * b + g4 + 1)
                nc.tensor.transpose(PS[0:S, 4, 128 * g4:128 * g4 + 128], od[g4 % 2][:], ident[:]).then_inc(s["oT"], 1)

            def x2_transpose(b):
                pe.wait_ge(s["x2"], b + 1)
                if more(b, 2):
                    pe.wait_ge(s["xt_lo"], b + 3)
                transposed(x2).then_inc(s["x2T"], 1)

            def x2_transpose(b):
                pe.wait_ge(s["x2"], b + 1)
                if more(b, 2):
                    pe.wait_ge(s["xt_lo"], b + 3)
                transposed(x2).then_inc(s["x2T"], 1)

            def attention_transpose(b):
                pe.wait_ge(s["af"], b + 1)
                if more(b, 1):
                    pe.wait_ge(s["vf"], 2 * b + 4)
                transposed(af).then_inc(s["aT"], 1)

            def output_project(b):
                pe.wait_ge(s["a_lo"], b + 1)
                products(PS[0:S, 7, 0:D], [(ah[:, k], al[:, k], w_hi["wo"][:, k], w_lo["wo"][:, k])
                                           for k in range(KD)]).then_inc(s["op"], 1)

            def step(b, slot):
                ks, qs = kst[slot], qst[slot]
                pe.wait_ge(s["kst_in"], 128 * b + 128)
                pe.wait_ge(s["qst_in"], 96 * b + 96)
                if not is_first(b):
                    pe.wait_ge(s["p_hi"], UN * b)
                for g in range(8):
                    if g >= 2:
                        pe.wait_ge(s["mx"], 8 * b + g - 1)
                    for half in range(2):
                        r = slice(64 * half, 64 * half + ROWS_S)
                        m = mm(PS[0:S, 2 * (g % 2) + half, 0:SKP], qs[r, g, S * half:S * half + S], ks[r, g],
                               start=True, stop=True)
                    m.then_inc(s["sc"], 1)
                    late = not is_first(b)
                    if g == 1 and late:
                        attended(b - 1, 3)
                    if g == 2 and late:
                        attention_transpose(b - 1)
                    if g == 4 and late:
                        output_project(b - 1)
                    if g == 5:
                        max_transpose(b, 0)
                        if more(b, 1):
                            x_transpose(b + 1)
                    if g in K_AT and more(b, 1):
                        part = K_AT.index(g)
                        k_part(b + 1, part // KD, part % KD)
                if not is_first(b):
                    x2_transpose(b - 1)
                pe.wait_ge(s["mx"], 8 * b + 8)
                max_transpose(b, 1)
                if more(b, 1):
                    if not is_first(b):
                        pe.wait_ge(s["x2_lo"], b)
                    q_project(b + 1)
                for u in range(UN + LEAD):
                    if u < UN:
                        if u >= RING:
                            pe.wait_ge(s["p_hi"], UN * b + u - RING + 1)
                        g4, c = u // NC, u % NC
                        if u % (UN // 2) == 0:
                            pe.wait_ge(s[f"m_in{u // (UN // 2)}"], 64 * b + 64)
                        for j in range(2):
                            i = 2 * g4 + j
                            m = mm(PS[0:KC, u % RING, j * 2 * S:(j + 1) * 2 * S],
                                   ks[:, i, KC * c:KC * c + KC], qs[:, i], start=True, stop=True)
                        m.then_inc(s["st_sc"], 1)
                    if u in V_AT and more(b, 1):
                        v_project(b + 1, V_AT.index(u))
                    if u >= LEAD:
                        w = u - LEAD
                        g4, c = w // NC, w % NC
                        if w == 0:
                            pe.wait_ge(s["vx_lo"], b + 1)
                            if more(b, 1):
                                pe.wait_ge(s["k_lo"], 2 * b + 4)
                        pe.wait_ge(s["p_lo"], UN * b + w + 1)
                        val = [x[:, c].rearrange("p h d -> p (h d)")[:, 4 * DV * g4:4 * DV * g4 + 4 * DV] for x in (vxh, vxl)]
                        products(PS[:, 5 + g4 % 2, 0:4 * S], [(val[0], val[1], ph[w % RING][:], pl[w % RING][:])],
                                 first=(c == 0), last=(c == NC - 1)).then_inc(s["pv"], 1)
                        if c == 1 and g4:
                            attended(b, g4 - 1)
            x_transpose(0)
            for m in range(KD):
                for k in range(KD):
                    k_part(0, m, k)
            q_project(0)
            v_project(0, 0)
            v_project(0, 1)
            run(pe, step)
            attended(B - 1, 3)
            attention_transpose(B - 1)
            output_project(B - 1)
            x2_transpose(B - 1)


def attend_block(nc, t, dr):
    with ExitStack() as ctx:
        def sb(name, shape, dt=F32):
            return ctx.enter_context(nc.sbuf_tensor("b_" + name, shape, dt))

        G = 2 * H
        scale = float(P) ** -0.5
        n_stage = 2 * KD
        qk_hi = sb("qk_hi", [128, KD, 2 * H * P], F32R); qk_lo = sb("qk_lo", [128, KD, 2 * H * P], F32R)
        sel_hi = sb("sel_hi", [128, KD, G * E], F32R); sel_lo = sb("sel_lo", [128, KD, G * E], F32R)
        stage = [sb(f"stage{i}", [128, H * P]) for i in range(2)]
        sel_in = sb("sel_in", [128, KD, G * E])
        route = sb("route", [128, 1])
        rank = sb("rank", [S, G, E])
        x2a = sb("x2a", [128, 2, KD, S], F32R)
        x2v = sb("x2v", [128, 2, KD, S], F32R)
        lg = sb("lg", [S, G, E]); ex = sb("ex", [S, G, E]); pr = sb("pr", [S, G, E]); l2 = sb("l2", [S, G, E])
        ea = sb("ea", [S, G, E]); eb = sb("eb", [S, G, E]); oh1 = sb("oh1", [S, G, E]); oh2 = sb("oh2", [S, G, E])
        gm = sb("gm", [S, 4, G]); gr = sb("gr", [S, 3, G])
        gate = [sb(f"gate{i}", [S, H, E]) for i in range(2)]
        gsp = sb("gsp", [S, H, 2, E], F32R)
        gT = sb("gT", [128, S])
        qk = sb("qk", [128, 2 * H, S])
        nm = sb("nm", [S, H]); nms = sb("nms", [S, H]); den = sb("den", [S, H]); rden = sb("rden", [S, H])
        pe_ = sb("pe", [S, H, S]); att = sb("att", [S, H, S]); attT = sb("attT", [S, H, S])
        vacc = sb("vacc", [S, H, P])
        cs = sb("cs", [P, H, S])
        PS = ctx.enter_context(nc.psum_tensor("ps2", [128, 8, 512], F32))
        s = {n: ctx.enter_context(nc.semaphore("b_" + n)) for n in (
            "stage_in0", "stage_in1", "late_in0", "late_in1", "late_hi", "late_lo", "sel_in", "route_in", "w_hi", "w_lo", "sel_hi", "sel_lo", "rank",
            "x2a_in", "x2v_in", "lgp", "lg", "ex", "gs", "gate", "g_hi", "g_lo", "gTp", "gT", "gT_out",
            "qkp", "qk", "scp", "nm", "nms", "exp", "rden", "att", "attTp", "attT",
            "vp", "v0", "v_used", "acc", "cxp", "cs", "c_out")}
        block = ctx.enter_context(nc.Block())
        ident = t["ident"]
        late = [sb("v_late_" + n, [128, KD, (H - HE) * E * P], F32R) for n in ("hi", "lo")]
        LCH = 512
        n_late = (H - HE) * E * P // LCH

        def expert_columns(part, k, h, c):
            if h >= HE:
                return late[part][:, k, (h - HE) * E * P + c:(h - HE) * E * P + c + 512]
            return t["v_lo" if part else "v_hi"][:, k, h * E * P + c:h * E * P + c + 512]

        units = [(2 * hp + j, half) for hp in range(H // 2) for half in range(2) for j in range(2)]
        NU = len(units)
        halves0 = [u for u, (_, half) in enumerate(units) if half == 0]

        @block.sync
        def _(sp):
            sp.dma_start(sel_in[:, :, 0:G * E // 2], dr["sel_v"]).then_inc(s["sel_in"], 16)
            sp.dma_start(sel_in[:, :, G * E // 2:], dr["sel_o"]).then_inc(s["sel_in"], 16)
            sp.dma_start(route[:], spread(dr["route"], 0, 128)).then_inc(s["route_in"], 16)

            def load_a(b):
                if not is_first(b):
                    sp.wait_ge(s["qkp"], 4 * (b - 1) + 4)
                sp.dma_start(x2a[:].bitcast(F32), dr["x2scr"][b]).then_inc(s["x2a_in"], 16)

            def load_v(b):
                if not is_first(b):
                    sp.wait_ge(s["vp"], NU * (b - 1) + NU)
                sp.dma_start(x2v[:].bitcast(F32), dr["x2scr"][b]).then_inc(s["x2v_in"], 16)

            load_a(0)
            load_v(0)
            for i in range(n_stage):
                if i >= 2:
                    sp.wait_ge(s["w_lo"], i - 1)
                sp.dma_start(stage[i % 2][:], dr["qkw"][:, i % KD, (i // KD) * H * P:(i // KD + 1) * H * P]).then_inc(s[f"stage_in{i % 2}"], 16)

            for i in range(n_late):
                if i < 2:
                    sp.wait_ge(s["w_lo"], n_stage - 1 + i)
                else:
                    sp.wait_ge(s["late_lo"], i - 1)
                c = HE * E * P + i * LCH
                sp.dma_start(stage[i % 2][:].rearrange("p (k c) -> p k c", k=KD), dr["vw"][:, :, c:c + LCH]).then_inc(s[f"late_in{i % 2}"], 16)

            def step(b, last=False):
                if not last:
                    load_a(b + 1)
                sp.wait_ge(s["gT"], b + 1)
                sp.dma_start(dr["gscr"][:, bass.ds(b * S, S)], gT[:]).then_inc(s["gT_out"], 16)
                if not last:
                    load_v(b + 1)
                sp.wait_ge(s["cs"], 2 * b + 2)
                sp.dma_start(dr["cscr"][:, :, bass.ds(b * S, S)], cs[:]).then_inc(s["c_out"], 16)

            step(0)
            with sp.Fori(1, B - 1) as b:
                step(b)
            step(B - 1, last=True)
            sp.wait_ge(s["gT_out"], 16 * B)
            sp.wait_ge(s["c_out"], 16 * B)

        @block.gpsimd
        def _(pool):
            g = nc.gpsimd
            for e in range(E):
                m = g.memset(rank[:, :, e], float(E - e))
            m.then_inc(s["rank"], 1)
            pool.wait_ge(s["sel_hi"], 1)
            g.tensor_tensor(sel_lo[:], sel_in[:], sel_hi[:].bitcast(F32), ALU.subtract).then_inc(s["sel_lo"], 1)

            for i in range(n_late):
                c = slice(i * LCH, i * LCH + LCH)
                st = stage[i % 2][:].rearrange("p (k c) -> p k c", k=KD)
                pool.wait_ge(s[f"late_in{i % 2}"], 16 * (i // 2) + 16)
                g.tensor_copy(late[0][:, :, c], st).then_inc(s["late_hi"], 1)
                pool.wait_ge(s["late_hi"], i + 1)
                g.tensor_tensor(late[1][:, :, c], st, late[0][:, :, c].bitcast(F32), ALU.subtract).then_inc(s["late_lo"], 1)

            def normalise(b):
                pool.wait_ge(s["rden"], b + 1)
                if not is_first(b):
                    pool.wait_ge(s["attTp"], 2 * (b - 1) + 2)
                g.tensor_tensor(att[:], pe_[:], spread(rden[:], 2, S), ALU.mult).then_inc(s["att"], 1)

            normalise(0)
            with pool.Fori(1, B) as b:
                normalise(b)

        @block.scalar
        def _(act):
            a = nc.scalar
            act.wait_ge(s["sel_in"], 32)
            a.copy(sel_hi[:], sel_in[:]).then_inc(s["sel_hi"], 1)
            for i in range(n_stage):
                act.wait_ge(s[f"stage_in{i % 2}"], 16 * (i // 2) + 16)
                a.copy(qk_hi[:, i % KD, (i // KD) * H * P:(i // KD + 1) * H * P], stage[i % 2][:]).then_inc(s["w_hi"], 1)

            def pre(b):
                act.wait_ge(s["lgp"], b + 1)
                if not is_first(b):
                    act.wait_ge(s["gate"], 2 * (b - 1) + 2)
                a.copy(lg[:], PS[0:S, 4, 0:G * E].rearrange("p (g e) -> p g e", g=G)).then_inc(s["lg"], 1)
                a.activation(ex[:], PS[0:S, 4, 0:G * E].rearrange("p (g e) -> p g e", g=G), ACT.Exp, scale=-1.0).then_inc(s["ex"], 1)
                for i in range(4):
                    act.wait_ge(s["qkp"], 4 * b + i + 1)
                    a.copy(qk[:, 4 * i:4 * i + 4], PS[:, 5 - i % 2, 0:4 * S].rearrange("p (m s) -> p m s", m=4)).then_inc(s["qk"], 1)
                if not is_first(b):
                    act.wait_ge(s["att"], b)
                for h in range(H):
                    if h % 4 == 0:
                        act.wait_ge(s["nms"], 2 * b + h // 4 + 1)
                    a.activation(pe_[:, h], PS[0:S, 5 - h // 4, (h % 4) * S:(h % 4 + 1) * S], ACT.Exp, bias=nms[:, h:h + 1],
                                 scale=scale, accum_out=den[:, h:h + 1]).then_inc(s["exp"], 1)

            def step(b, last=False):
                for n, u in enumerate(halves0):
                    h, _ = units[u]
                    act.wait_ge(s["vp"], NU * b + u + 1)
                    if n == 0:
                        act.wait_ge(s["gate"], 2 * b + 2)
                        if not is_first(b):
                            act.wait_ge(s["cxp"], 2 * (b - 1) + 2)
                    a.activation(vacc[:, h], PS[0:S, u % 4, 0:P], ACT.Copy, scale=gate[0][:, h, 0:1]).then_inc(s["v0"], 1)
                    if n == 1:
                        act.wait_ge(s["gTp"], b + 1)
                        if not is_first(b):
                            act.wait_ge(s["gT_out"], 16 * (b - 1) + 16)
                        a.copy(gT[:], PS[:, 4, 0:S]).then_inc(s["gT"], 1)
                        for i in range(2):
                            act.wait_ge(s["attTp"], 2 * b + i + 1)
                            a.copy(attT[:, 4 * i:4 * i + 4], PS[0:S, 6 + i, 0:4 * S].rearrange("p (m s) -> p m s", m=4)).then_inc(s["attT"], 1)
                if not last:
                    pre(b + 1)
                for i in range(2):
                    act.wait_ge(s["cxp"], 2 * b + i + 1)
                    if i == 0 and not is_first(b):
                        act.wait_ge(s["c_out"], 16 * (b - 1) + 16)
                    a.copy(cs[:, 4 * i:4 * i + 4], PS[:, 6 + i, 0:4 * S].rearrange("p (m s) -> p m s", m=4)).then_inc(s["cs"], 1)

            pre(0)
            step(0)
            with act.Fori(1, B - 1) as b:
                step(b)
            step(B - 1, last=True)

        @block.vector
        def _(dve):
            v = nc.vector
            for i in range(n_stage):
                c = slice((i // KD) * H * P, (i // KD + 1) * H * P)
                dve.wait_ge(s["w_hi"], i + 1)
                v.tensor_tensor(qk_lo[:, i % KD, c], stage[i % 2][:], qk_hi[:, i % KD, c].bitcast(F32), ALU.subtract).then_inc(s["w_lo"], 1)
            dve.wait_ge(s["rank"], 1)
            dve.wait_ge(s["route_in"], 16)
            NG = 17

            def gates(b):
                count = [0]

                def then(ins):
                    count[0] += 1
                    ins.then_inc(s["gs"], 1)
                    dve.wait_ge(s["gs"], NG * b + count[0])

                dve.wait_ge(s["ex"], b + 1)
                if not is_first(b):
                    dve.wait_ge(s["g_lo"], b)
                v.tensor_scalar(pr[:], ex[:], 1.0, None, ALU.add)
                then(v.tensor_reduce(gm[:, 0], lg[:], AX.X, ALU.max))
                then(v.tensor_tensor(ea[:], lg[:], spread(gm[:, 0], 2, E), ALU.is_equal))
                then(v.reciprocal(pr[:], pr[:]))
                then(v.tensor_tensor(eb[:], ea[:], rank[:], ALU.mult))
                then(v.tensor_reduce(gm[:, 1], eb[:], AX.X, ALU.max))
                then(v.tensor_tensor(oh1[:], eb[:], spread(gm[:, 1], 2, E), ALU.is_equal))
                then(v.scalar_tensor_tensor(out=l2[:], in0=oh1[:], scalar=-BIG, in1=lg[:], op0=ALU.mult, op1=ALU.add))
                then(v.tensor_reduce(gm[:, 2], l2[:], AX.X, ALU.max))
                then(v.tensor_tensor(ea[:], l2[:], spread(gm[:, 2], 2, E), ALU.is_equal))
                then(v.tensor_tensor(eb[:], ea[:], rank[:], ALU.mult))
                then(v.tensor_reduce(gm[:, 3], eb[:], AX.X, ALU.max))
                then(v.tensor_tensor(oh2[:], eb[:], spread(gm[:, 3], 2, E), ALU.is_equal))
                then(v.tensor_tensor(ea[:], oh1[:], oh2[:], ALU.add))
                then(v.tensor_tensor(eb[:], ea[:], pr[:], ALU.mult))
                then(v.tensor_reduce(gr[:, 0], eb[:], AX.X, ALU.add))
                then(v.tensor_scalar(gr[:, 1], gr[:, 0], 1e-9, None, ALU.max))
                then(v.reciprocal(gr[:, 2], gr[:, 1]))
                for i in range(2):
                    v.scalar_tensor_tensor(out=gate[i][:], in0=eb[:, H * i:H * i + H], scalar=route[0:S, :],
                                           in1=spread(gr[:, 2, H * i:H * i + H], 2, E), op0=ALU.mult,
                                           op1=ALU.mult).then_inc(s["gate"], 1)
                dve.wait_ge(s["gate"], 2 * b + 2)
                if not is_first(b):
                    dve.wait_ge(s["gTp"], b)
                v.tensor_copy(gsp[:, :, 0], gate[1][:]).then_inc(s["g_hi"], 1)
                dve.wait_ge(s["g_hi"], b + 1)
                v.tensor_tensor(gsp[:, :, 1], gate[1][:], gsp[:, :, 0].bitcast(F32), ALU.subtract).then_inc(s["g_lo"], 1)

            def maxima(b):
                for i in range(2):
                    dve.wait_ge(s["scp"], 2 * b + i + 1)
                    v.tensor_reduce(nm[:, 4 * i:4 * i + 4], PS[0:S, 5 - i, 0:4 * S].rearrange("p (m s) -> p m s", m=4),
                                    AX.X, ALU.max, negate=True).then_inc(s["nm"], 1)
                    dve.wait_ge(s["nm"], 2 * b + i + 1)
                    v.tensor_scalar(nms[:, 4 * i:4 * i + 4], nm[:, 4 * i:4 * i + 4], scale, None, ALU.mult).then_inc(s["nms"], 1)

            def step(b, last=False):
                dve.wait_ge(s["exp"], H * b + H)
                v.reciprocal(rden[:], den[:]).then_inc(s["rden"], 1)
                PER = E * H - H
                for hp in range(H // 2):
                    for half in range(2):
                        for k in range(4):
                            if half == 0 and k == 0:
                                continue
                            for j in range(2):
                                u = 4 * hp + 2 * half + j
                                h = 2 * hp + j
                                e = 4 * half + k
                                i = 14 * hp + 2 * (e - 1) + j
                                if e == 1:
                                    dve.wait_ge(s["v0"], H * b + h + 1)
                                else:
                                    dve.wait_ge(s["acc"], PER * b + i - 1)
                                if k == 0:
                                    dve.wait_ge(s["vp"], NU * b + u + 1)
                                ins = v.scalar_tensor_tensor(out=vacc[:, h], in0=PS[0:S, u % 4, k * P:(k + 1) * P],
                                                             scalar=gate[0][:, h, e:e + 1], in1=vacc[:, h],
                                                             op0=ALU.mult, op1=ALU.add)
                                ins.then_inc(s["acc"], 1)
                if not last:
                    gates(b + 1)
                    maxima(b + 1)

            gates(0)
            maxima(0)
            step(0)
            with dve.Fori(1, B - 1) as b:
                step(b)
            step(B - 1, last=True)

        @block.tensor
        def _(pe):
            mm = nc.tensor.matmul
            PER = E * H - H

            def pre(b):
                if is_first(b):
                    pe.wait_ge(s["sel_lo"], 1)
                pe.wait_ge(s["x2a_in"], 16 * b + 16)
                if not is_first(b):
                    pe.wait_ge(s["gT"], b)
                xh, xl = x2a[:, 0], x2a[:, 1]
                n = 0
                for k in range(KD):
                    for l, r in ((xl, sel_hi), (xh, sel_lo), (xh, sel_hi)):
                        m = mm(PS[0:S, 4, 0:G * E], l[:, k], r[:, k], start=(n == 0), stop=(n == 5))
                        n += 1
                m.then_inc(s["lgp"], 1)
                if is_first(b):
                    pe.wait_ge(s["w_lo"], n_stage)
                for i in range(4):
                    bank = 5 - i % 2
                    if i == 0 and not is_first(b):
                        pe.wait_ge(s["exp"], H * (b - 1) + H)
                    if i == 1:
                        pe.wait_ge(s["ex"], b + 1)
                    if i >= 2:
                        pe.wait_ge(s["qk"], 4 * b + i - 1)
                    for j in range(4):
                        c = slice((4 * i + j) * P, (4 * i + j + 1) * P)
                        n = 0
                        for k in range(KD):
                            for l, r in ((qk_lo, xh), (qk_hi, xl), (qk_hi, xh)):
                                m = mm(PS[:, bank, j * S:(j + 1) * S], l[:, k, c], r[:, k], start=(n == 0), stop=(n == 5))
                                n += 1
                    m.then_inc(s["qkp"], 1)
                for i in range(2):
                    pe.wait_ge(s["qk"], 4 * b + 3 + i)
                    if i == 0:
                        pe.wait_ge(s["qk"], 4 * b + 4)
                    for j in range(4):
                        h = 4 * i + j
                        m = mm(PS[0:S, 5 - i, j * S:(j + 1) * S], qk[:, h], qk[:, H + h], start=True, stop=True)
                    m.then_inc(s["scp"], 1)

            def step(b, last=False):
                pe.wait_ge(s["x2v_in"], 16 * b + 16)
                for u, (h, half) in enumerate(units):
                    hp, j = h // 2, h % 2
                    if u >= 4 or not is_first(b):
                        w = u - 4 if u >= 4 else u - 4 + NU
                        ph, phalf = units[w]
                        place = 14 * (ph // 2) + 2 * (4 * phalf + 2) + ph % 2 + 1
                        pe.wait_ge(s["acc"], PER * b + place if u >= 4 else PER * (b - 1) + place)
                    if h >= HE and is_first(b):
                        pe.wait_ge(s["late_lo"], n_late)
                    n = 0
                    for k in range(KD):
                        for l, r in ((1, 0), (0, 1), (0, 0)):
                            m = mm(PS[0:S, u % 4], x2v[:, l, k], expert_columns(r, k, h, half * 512), start=(n == 0), stop=(n == 5))
                            n += 1
                    m.then_inc(s["vp"], 1)
                    if u == 3:
                        pe.wait_ge(s["g_lo"], b + 1)
                        pe.wait_ge(s["exp"], H * b + H)
                        nc.tensor.transpose(PS[:, 4, 0:S], gsp[:].rearrange("p h a e -> p (h a e)").bitcast(F32), ident[0:S, 0:S]).then_inc(s["gTp"], 1)
                        pe.wait_ge(s["att"], b + 1)
                        for i in range(2):
                            if i == 0 and not is_first(b):
                                pe.wait_ge(s["cs"], 2 * (b - 1) + 2)
                            for jj in range(4):
                                m = nc.tensor.transpose(PS[0:S, 6 + i, jj * S:(jj + 1) * S], att[:, 4 * i + jj], ident[0:S, 0:S])
                            m.then_inc(s["attTp"], 1)
                if not last:
                    pre(b + 1)
                pe.wait_ge(s["attT"], 2 * b + 2)
                pe.wait_ge(s["acc"], PER * b + PER)
                for i in range(2):
                    for jj in range(4):
                        h = 4 * i + jj
                        m = mm(PS[:, 6 + i, jj * S:(jj + 1) * S], vacc[:, h], attT[:, h], start=True, stop=True)
                    m.then_inc(s["cxp"], 1)

            pre(0)
            step(0)
            with pe.Fori(1, B - 1) as b:
                step(b)
            step(B - 1, last=True)


def output_block(nc, t, dr):
    with ExitStack() as ctx:
        def sb(name, shape, dt=F32):
            return ctx.enter_context(nc.sbuf_tensor("c_" + name, shape, dt))

        TT = TOK // 128
        EP = E // 2
        UPC = H * EP
        ow = sb("ow", [P, H * E, 2, D], F32R)
        stage = [sb(f"stage{i}", [P, E, D]) for i in range(2)]
        pick = sb("pick", [2 * E, E, 128], F32R)
        pickf = stage[0][0:2 * E, 0:E // 2].rearrange("p a d -> p (a d)").rearrange("p (e m) -> p e m", e=E)
        gs = [sb(f"gs{i}", [2 * E, H, TOK], F32R) for i in range(2)]
        cx = [sb(f"cx{i}", [P, H, TOK]) for i in range(2)]
        xr = [sb(f"xr{i}", [128, TT, D]) for i in range(2)]
        wh = [sb(f"wh{i}", [P, 2, TOK], F32R) for i in range(EP)]
        wl = [sb(f"wl{i}", [P, 2, TOK], F32R) for i in range(EP)]
        y = sb("y", [128, TT, D])
        PS = ctx.enter_context(nc.psum_tensor("ps3", [128, 8, 512], F32))
        s = {n: ctx.enter_context(nc.semaphore("c_" + n)) for n in (
            "pick0", "pickf", "pick", "stage_in0", "stage_in1", "o_hi", "o_lo", "in0", "in1", "g", "w", "w_hi", "w_lo", "used", "y1", "y", "out")}
        w = [PS[:, q].rearrange("p (e t) -> p e t", e=2) for q in range(EP)]
        block = ctx.enter_context(nc.Block())

        def chunks(eng, f):
            f(0, 0, 0)
            with eng.Fori(0, (NT - 1) // 2) as i:
                f(2 * i + 1, 1, i)
                f(2 * i + 2, 0, i + 1)

        def heads(eng, f):
            f(0)
            with eng.Fori(1, H - 1) as h:
                f(h)
            f(H - 1)

        @block.sync
        def _(sp):
            def load(c, slot):
                if not isinstance(c, int) or c > 1:
                    sp.wait_ge(s["y"], TT * (c - 2) + TT)
                sp.dma_start(gs[slot][:].bitcast(F32), dr["gscr"][:, bass.ds(c * TOK, TOK)].rearrange("(h a) t -> a h t", h=H)).then_inc(s[f"in{slot}"], 16)
                sp.dma_start(cx[slot][:], dr["cscr"][:, :, bass.ds(c * TOK, TOK)]).then_inc(s[f"in{slot}"], 16)
                sp.dma_start(xr[slot][:], dr["x1scr"].rearrange("b s d -> (b s) d")[bass.ds(c * TOK, TOK)].rearrange("(a p) d -> p a d", p=128)).then_inc(s[f"in{slot}"], 16)

            def store(c):
                sp.wait_ge(s["y"], TT * c + TT)
                sp.dma_start(dr["out"].rearrange("b s d -> (b s) d")[bass.ds(c * TOK, TOK)].rearrange("(a p) d -> p a d", p=128), y[:]).then_inc(s["out"], 16)

            load(0, 0)
            sp.wait_ge(s["pick"], 1)
            for h in range(H):
                if h >= 2:
                    sp.wait_ge(s["o_lo"], h - 1)
                sp.dma_start(stage[h % 2][:], dr["ow"][:, E * h:E * h + E]).then_inc(s[f"stage_in{h % 2}"], 16)
            load(1, 1)
            store(0)
            with sp.Fori(0, (NT - 1) // 2 - 1) as i:
                load(2 * i + 2, 0)
                store(2 * i + 1)
                load(2 * i + 3, 1)
                store(2 * i + 2)
            load(NT - 1, 0)
            store(NT - 2)
            store(NT - 1)
            sp.wait_ge(s["out"], 16 * NT)

        @block.gpsimd
        def _(pool):
            g = nc.gpsimd
            g.memset(pickf, 0.0).then_inc(s["pick0"], 1)
            pool.wait_ge(s["pick0"], 1)
            for r in range(2):
                g.affine_select(out=pickf, in_=pickf, compare_op=ALU.not_equal, fill=1.0, base=-E * r,
                                pattern=[[-1, E], [0, 128]], channel_multiplier=1).then_inc(s["pickf"], 1)
                pool.wait_ge(s["pickf"], r + 1)
            g.tensor_copy(pick[:], pickf).then_inc(s["pick"], 1)
            for h in range(H):
                pool.wait_ge(s["o_hi"], h + 1)
                g.tensor_tensor(ow[:, E * h:E * h + E, 1], stage[h % 2][:], ow[:, E * h:E * h + E, 0].bitcast(F32),
                                ALU.subtract).then_inc(s["o_lo"], 1)

        @block.scalar
        def _(act):
            a = nc.scalar

            def o_high(h):
                act.wait_ge(s[f"stage_in{h % 2}"], 16 * (h // 2) + 16)
                a.copy(ow[:, E * h:E * h + E, 0], stage[h % 2][:]).then_inc(s["o_hi"], 1)

            def head(c, h):
                for q in range(EP):
                    n = UPC * c + EP * h + q
                    act.wait_ge(s["w"], n + 1)
                    if not (isinstance(n, int) and n < EP):
                        act.wait_ge(s["used"], UPC * c + EP * h + q - (EP - 1) if isinstance(n, int) else n - (EP - 1))
                    a.copy(wh[q][:], w[q]).then_inc(s["w_hi"], 1)

            o_high(0)
            for h in range(H):
                if h + 1 < H:
                    o_high(h + 1)
                head(0, h)
            with act.Fori(1, NT) as c:
                head(c, 0)
                with act.Fori(1, H) as h:
                    head(c, h)

        @block.vector
        def _(dve):
            v = nc.vector

            def low(n, q):
                dve.wait_ge(s["w_hi"], n + 1)
                v.tensor_tensor(wl[q][:], w[q], wh[q][:].bitcast(F32), ALU.subtract).then_inc(s["w_lo"], 1)

            def head(c, slot, h):
                for q in range(EP):
                    n = UPC * c + EP * h + q
                    dve.wait_ge(s["g"], n + 1)
                    v.tensor_tensor(w[q], spread(cx[slot][:, h], 1, 2), w[q], ALU.mult).then_inc(s["w"], 1)
                    if q:
                        low(n - 1, q - 1)
                low(UPC * c + EP * h + EP - 1, EP - 1)

            def chunk(c, slot, turn):
                dve.wait_ge(s[f"in{slot}"], 48 * turn + 48)
                heads(dve, lambda h: head(c, slot, h))
                dve.wait_ge(s["used"], UPC * c + UPC)
                if not is_first(c):
                    dve.wait_ge(s["out"], 16 * (c - 1) + 16)
                for i in range(TT):
                    v.tensor_tensor(xr[slot][:, i], PS[:, 4 + i, D:2 * D], xr[slot][:, i], ALU.add).then_inc(s["y1"], 1)
                for i in range(TT):
                    dve.wait_ge(s["y1"], TT * c + i + 1)
                    v.tensor_tensor(y[:, i], PS[:, 4 + i, 0:D], xr[slot][:, i], ALU.add).then_inc(s["y"], 1)

            chunks(dve, chunk)

        @block.tensor
        def _(pe):
            mm = nc.tensor.matmul

            def spread_gates(c, slot, h, q):
                for e in range(2):
                    m = mm(PS[:, q, e * TOK:(e + 1) * TOK], pick[:, 2 * q + e, :], gs[slot][:, h], start=True, stop=True)
                m.then_inc(s["g"], 1)

            def experts(c, h, q, first):
                if is_first(c) and q == 0:
                    pe.wait_ge(s["o_lo"], h + 1)
                pe.wait_ge(s["w_lo"], UPC * c + EP * h + q + 1)
                if first and not is_first(c):
                    pe.wait_ge(s["y"], TT * (c - 1) + TT)
                for e in range(2):
                    he = h * E + 2 * q + e
                    for i in range(TT):
                        r = slice(128 * i, 128 * i + 128)
                        mm(PS[:, 4 + i], wh[q][:, e, r], ow[:, he], start=(first and e == 0), stop=False, skip_group_check=True)
                        m = mm(PS[:, 4 + i, 0:D], wl[q][:, e, r], ow[:, he, 0], start=False,
                               stop=False, skip_group_check=True)
                m.then_inc(s["used"], 1)

            def chunk(c, slot, turn):
                pe.wait_ge(s[f"in{slot}"], 48 * turn + 48)
                for q in range(EP):
                    spread_gates(c, slot, 0, q)

                def head(h):
                    for q in range(EP):
                        experts(c, h, q, first=isinstance(h, int) and h == 0 and q == 0)
                        if not (isinstance(h, int) and h == H - 1):
                            spread_gates(c, slot, h + 1, q)
                heads(pe, head)

            pe.wait_ge(s["pick"], 1)
            chunks(pe, chunk)


def weights(w):
    return w.T.reshape(KD, 128, -1).transpose(1, 0, 2)


def laid_out(i):
    xc, ff = "L0_xcond_", "L0_ffn_"
    paired = np.arange(D).reshape(2, HALF, DK).transpose(1, 0, 2).reshape(-1)

    def pad(a):
        return np.pad(a, [(0, 0)] * (a.ndim - 1) + [(0, SKP - SK)])

    return {
        "x": i["x"],
        "ctxT": pad(i["ctx_1024"].transpose(0, 2, 1).reshape(B, KD, 128, SK).transpose(0, 2, 1, 3)),
        "tau": i["condB_tau"], "delta": pad(i["fside_BxS2_0"]),
        "wq": weights(i[xc + "Wq"]).reshape(128, -1), "wk": weights(i[xc + "Wk"]).reshape(128, -1),
        "wv": weights(i[xc + "Wv"][paired]).reshape(128, -1), "wo": weights(i[xc + "Wo"][:, paired]).reshape(128, -1),
        "bq": i[xc + "bq"].reshape(KD, 128).T, "bk": i[xc + "bk"].reshape(KD, 128).T,
        "bv": i[xc + "bv"][paired], "bo": i[xc + "bo"],
        "vw": i[ff + "v_w"].reshape(H, E, KD, 128, P).transpose(3, 2, 0, 1, 4).reshape(128, KD, H * E * P),
        "qkw": np.concatenate([weights(i[ff + "q_w"]), weights(i[ff + "k_w"])], axis=2),
        "sel_v": weights(i[ff + "sel_v_w"]), "sel_o": weights(i[ff + "sel_o_w"]),
        "route": i[ff + "route_scale"],
        "ow": i[ff + "o_w"].transpose(1, 0, 2),
    }


def build(nc, dr):
    with ExitStack() as ctx:
        t = {"ident": ctx.enter_context(nc.sbuf_tensor("ident", [128, 128], F32))}
        ident_done = ctx.enter_context(nc.semaphore("ident_done"))
        with nc.Block() as block:
            @block.gpsimd
            def _(pool):
                nc.gpsimd.memset(t["ident"][:], 0.0).then_inc(ident_done, 1)
                pool.wait_ge(ident_done, 1)
                nc.gpsimd.affine_select(out=t["ident"][:], in_=t["ident"][:], compare_op=ALU.not_equal, fill=1.0, base=0,
                                        pattern=[[-1, 128]], channel_multiplier=1).then_inc(ident_done, 1)
                pool.wait_ge(ident_done, 2)
        with ExitStack() as both:
            for n in ("v_hi", "v_lo"):
                t[n] = both.enter_context(nc.sbuf_tensor(n, [128, KD, HE * E * P], F32R))
            cross_block(nc, t, dr)
            attend_block(nc, t, dr)
        output_block(nc, t, dr)


def kernel(**inputs):
    import numpy as np
    import concourse.bacc as bacc
    from concourse.bass_utils import run_bass_kernel_spmd as run

    nc = bacc.Bacc("TRN2", target_bir_lowering=False, num_devices=1)
    arrays, dr = {}, {}
    for name, a in laid_out({k: np.asarray(v) for k, v in inputs.items()}).items():
        arrays["in_" + name] = np.ascontiguousarray(a)
        dr[name] = nc.dram_tensor("in_" + name, a.shape, F32, kind="ExternalInput").ap()
    for name, shape in (("kscr", [2, 128, KD, SKP]), ("qscr", [2, 128, KD, S]), ("dscr", [4, B, SKP]), ("x1scr", [B, S, D]),
                        ("x2scr", [B, 128, 2, KD, S]), ("gscr", [128, B * S]), ("cscr", [P, H, B * S])):
        dr[name] = nc.dram_tensor(name, shape, F32, kind="Internal").ap()
    dr["out"] = nc.dram_tensor("out", [B, S, D], F32, kind="ExternalOutput").ap()
    build(nc, dr)
    return run(nc, [arrays], core_ids=[0]).results[0]["out"]
```

```python
from contextlib import ExitStack

import numpy as np

import concourse.bass as bass
from concourse import mybir

F32 = mybir.dt.float32
F32R = mybir.dt.float32r
ALU = mybir.AluOpType
ACT = mybir.ActivationFunctionType
AX = mybir.AxisListType

B, S, D = 16, 112, 256
SK, KC = 375, 125
NC = SK // KC
SKP = SK + SK % 2
XH, DK = 16, 16
H, E, P = 8, 8, 128
KD = D // 128
HALF = XH // 2
QUAD = HALF // 2
HE = H - 3
VCH = HE * E * P // B
DV = 32
UN = 4 * NC
RING = 4
LEAD = RING - 1
Q_AT = 2
V_AT = (4, 5, 9)
K_AT = (3, 5, 6, 7)
EPS = 1e-5
N_QKW = 2 * KD
NS = 3
TOK = 256
NT = B * S // TOK
BIG = 1e30

ROW_D = 3 * DK
ROW_M = ROW_D + 2
ROWS_S = ROW_M


def spread(ap, axis, n):
    ap = ap.unsqueeze(axis)
    shape = list(ap.shape)
    shape[axis] = n
    return ap.broadcast_to(shape)


def is_first(b):
    return isinstance(b, int) and b == 0


def passing(nc, *specs):
    with ExitStack() as held:
        return [held.enter_context(nc.sbuf_tensor(name, shape, dt)) for name, shape, dt in specs]


def qk_piece(t, dr, i):
    k, c = i % KD, (i // KD) * H * P
    return t["qk_full"][:, k, c:c + H * P], dr["qkw"][:, k, c:c + H * P]


def load_chunk(sp, dr, c, gs, cx, xr, arrived):
    tokens = bass.ds(c * TOK, TOK)
    sp.dma_start(gs[:].bitcast(F32), dr["gscr"][:, tokens].rearrange("(h a) t -> a h t", h=H)).then_inc(arrived, 16)
    sp.dma_start(cx[:], dr["cscr"][:, :, tokens]).then_inc(arrived, 16)
    sp.dma_start(xr[:], dr["x1scr"].rearrange("b s d -> (b s) d")[tokens].rearrange("(a p) d -> p a d", p=128)).then_inc(arrived, 16)


def arriving(nc, ctx, name, shape):
    with nc.sbuf_tensor(name + "_full", shape, F32) as full:
        pass
    return ctx.enter_context(nc.sbuf_tensor(name, shape, F32R)), full


def cross_block(nc, t, dr):
    with ExitStack() as ctx:
        def sb(name, shape, dt=F32):
            return ctx.enter_context(nc.sbuf_tensor("a_" + name, shape, dt))

        names = ("wk", "wq", "wv", "wo")
        w_hi = {n: sb(n + "_hi", [128, KD, D], F32R) for n in names}
        w_lo, w_full = {}, {}
        for n in names:
            w_lo[n], w_full[n] = arriving(nc, ctx, "a_" + n + "_lo", [128, KD, D])
        bq = sb("bq", [128, KD]); bk = sb("bk", [128, KD])
        bv = sb("bv", [128, D]); bo = sb("bo", [128, D])
        tau4 = sb("tau4", [128, B])
        tick = sb("tick", [128, 1])
        pool_tick = sb("pool_tick", [128, 1])
        half_pow = sb("half_pow", [128, 1])
        cst = sb("cst", [128, KD, SKP])
        ch = sb("ch", [128, KD, SKP], F32R); cl = sb("cl", [128, KD, SKP], F32R)
        xin = sb("xin", [S, D]); xb = sb("xb", [S, D])
        xq = sb("xq", [128, D]); xn = xq[0:S, :]
        stat = sb("stat", [S, 6]); mv = sb("mv", [S, 2]); ve = sb("ve", [S, 1]); rstd = sb("rstd", [S, 1])
        stat2 = sb("stat2", [S, 6]); mv2 = sb("mv2", [S, 2]); ve2 = sb("ve2", [S, 1]); rstd2 = sb("rstd2", [S, 1])
        xth = sb("xth", [128, KD, S], F32R); xtl = sb("xtl", [128, KD, S], F32R)
        ah, al = xth, xtl
        qf = xq[:, 0:KD * S].rearrange("p (k s) -> p k s", k=KD)
        qh = sb("qh", [128, KD, S], F32R); ql = sb("ql", [128, KD, S], F32R)
        kh = sb("kh", [128, KD, SKP], F32R); kl = sb("kl", [128, KD, SKP], F32R)
        kst = [t["kst0"], sb("kst1", [128, HALF, SKP], F32R)]
        qst = [t["qst0"], sb("qst1", [128, HALF, 2 * S], F32R)]
        vxh = t["vxh"]; vxl = sb("vxl", [KC, NC, XH, DV], F32R)
        vf = t["vf"]
        nm = sb("nm", [S, 2, 2, QUAD])
        mh = [sb(f"mh{n}", [HALF, S], F32R) for n in range(2)]
        ml = [sb(f"ml{n}", [HALF, S], F32R) for n in range(2)]
        ph = [sb(f"ph{i}", [KC, 4 * S], F32R) for i in range(RING)]
        pl = [sb(f"pl{i}", [KC, 4 * S], F32R) for i in range(RING)]
        pf = [sb(f"pf{i}", [KC, 4 * S]) for i in range(RING // 2)]
        d_in, d_q, d_hi, d_lo = pf[0][0:B, 0:SKP], pf[1][0:B, 0:SKP], kh[0:B, 0], kl[0:B, 0]
        od = [sb(f"od{i}", [128, S]) for i in range(2)]
        rs = sb("rs", [S, XH]); af = sb("af", [S, D])
        x1 = sb("x1", [S, D]); x2 = af
        x2s = t["x2s"]
        PS = ctx.enter_context(nc.psum_tensor("ps1", [128, 8, 512], F32))
        bank7 = PS[:, 7, 0:KD * S].rearrange("p (k s) -> p k s", k=KD)

        s = {n: ctx.enter_context(nc.semaphore("a_" + n)) for n in (
            "wk_in", "wq_in", "wv_in", "wo_in", "small_in", "w_hi", "w_lo", "d_q", "d_hi", "d_lo", "d_out", "zeros0", "zeros1", "ones", "tau", "pow_c",
            "vst_in", "v_hi", "v_lo",
            "ctx_in", "x_in", "xb_in", "c_hi", "c_lo", "st", "mv", "ve", "rstd", "xn", "xb", "xT", "xt_hi", "xt_lo",
            "kp", "k_hi", "k_lo", "qp", "qf", "q_hi", "q_lo", "k_out0", "k_out1", "q_out", "kst_in", "qst_in",
            "vp", "vf", "vx_hi", "vx_lo", "sc", "mx", "mT", "m_hi", "m_lo", "m_in0", "m_in1", "st_sc", "p", "p_hi", "p_lo", "pv", "od", "oT", "rs", "af",
            "aT", "a_hi", "a_lo", "op", "x1", "x1_out", "st2", "mv2", "ve2", "rstd2", "x2", "x2T", "x2_hi", "x2_lo", "x2_out")}
        block = ctx.enter_context(nc.Block())
        kscr, qscr, dscr = dr["kscr"], dr["qscr"], dr["dscr"]
        ident = t["ident"]

        def flat(w):
            return w[:].rearrange("p k d -> p (k d)")

        def own_queries(g4, j):
            r = slice(DV * j, DV * j + DV)
            return od[g4 % 2][r], PS[r, 5 + g4 % 2, S * j:S * j + S]

        def more(b, n):
            return not isinstance(b, int) or b + n < B

        def run(eng, step):
            step(0, 0)
            step(1, 1)
            with eng.Fori(1, B // 2 - 1) as i:
                step(2 * i, 0)
                step(2 * i + 1, 1)
            step(B - 2, 0)
            step(B - 1, 1)

        @block.sync
        def _(sp):
            def load_ctx(b):
                if not is_first(b):
                    sp.wait_ge(s["c_lo"], b)
                sp.dma_start(cst[:], dr["ctxT"][b]).then_inc(s["ctx_in"], 16)

            def load_x(b):
                if not is_first(b):
                    sp.wait_ge(s["xn"], b)
                sp.dma_start(xin[:], dr["x"][b]).then_inc(s["x_in"], 16)

            def load_residual(b):
                if not is_first(b):
                    sp.wait_ge(s["x1"], b)
                sp.dma_start(xb[:], dr["x"][b]).then_inc(s["xb_in"], 16)

            load_ctx(0)
            sp.dma_start(flat(w_full["wk"]), dr["wk"]).then_inc(s["wk_in"], 16)
            load_x(0)
            for o, a in ((d_in, dr["delta"]), (bq[:], dr["bq"]), (bk[:], dr["bk"]), (bv[:], spread(dr["bv"], 0, 128)),
                         (bo[:], spread(dr["bo"], 0, 128)), (tau4[:], spread(dr["tau"], 0, 128))):
                sp.dma_start(o, a).then_inc(s["small_in"], 16)
            for n in names[1:]:
                sp.dma_start(flat(w_full[n]), dr[n]).then_inc(s[n + "_in"], 16)
            load_residual(0)
            sp.wait_ge(s["d_hi"], 1)
            sp.wait_ge(s["d_lo"], 1)
            sp.dma_start(dscr[0], d_hi.bitcast(F32)).then_inc(s["d_out"], 16)
            sp.dma_start(dscr[1], d_lo.bitcast(F32)).then_inc(s["d_out"], 16)
            sp.wait_ge(s["pow_c"], 3)
            for j in (2, 3):
                sp.dma_start(dscr[j], vxh[0:B].rearrange("p c h d -> p (c h d)")[:, 0:SKP].bitcast(F32)).then_inc(s["d_out"], 16)

            def k_bounce(b, m, before=None):
                sp.wait_ge(s["k_lo"], 2 * b + m + 1)
                if not is_first(b):
                    sp.wait_ge(s["kst_in"], 128 * before + 128)
                for part, k in enumerate((kh, kl)):
                    sp.dma_start(kscr[part, :, m], k[:, m].bitcast(F32)).then_inc(s[f"k_out{m}"], 16)

            def q_bounce(b, before=None):
                if not is_first(b):
                    sp.wait_ge(s["qst_in"], 96 * before + 96)
                sp.wait_ge(s["q_hi"], b + 1)
                sp.wait_ge(s["q_lo"], b + 1)
                sp.dma_start(qscr[0], qh[:].bitcast(F32)).then_inc(s["q_out"], 16)
                sp.dma_start(qscr[1], ql[:].bitcast(F32)).then_inc(s["q_out"], 16)

            def stack_k(b, slot):
                for half in range(2):
                    sp.wait_ge(s[f"k_out{half}"], 32 * b + 32)
                    for j, part in enumerate((0, 1, 0)):
                        r = 64 * half + DK * j
                        src = kscr[part, :, half].rearrange("(i r) k -> r i k", r=DK)
                        sp.dma_start(kst[slot][r:r + DK].bitcast(F32), src).then_inc(s["kst_in"], 16)
                    r = 64 * half + ROW_D
                    sp.dma_start(kst[slot][r:r + 4].bitcast(F32), spread(dscr[:, b, :], 1, HALF)).then_inc(s["kst_in"], 16)

            def stack_q(b, slot):
                sp.wait_ge(s["q_out"], 32 * b + 32)
                for half in range(2):
                    for j, part in enumerate((0, 0, 1)):
                        r = 64 * half + DK * j
                        src = qscr[part, :, half].rearrange("(i r) k -> r i k", r=DK)
                        sp.dma_start(qst[slot][r:r + DK, :, S * half:S * half + S].bitcast(F32), src).then_inc(s["qst_in"], 16)

            def maxima(b, n, slot):
                sp.wait_ge(s["m_hi"], 2 * b + n + 1)
                sp.wait_ge(s["m_lo"], 2 * b + n + 1)
                for half in range(2):
                    for j, m in enumerate((mh, ml)):
                        r = 64 * half + ROW_M + j
                        sp.dma_start(qst[slot][r:r + 1, QUAD * n:QUAD * n + QUAD, S * half:S * half + S].bitcast(F32),
                                     m[n][QUAD * half:QUAD * half + QUAD, :].bitcast(F32)).then_inc(s[f"m_in{n}"], 16)

            def store_x2(b):
                sp.wait_ge(s["x2_hi"], b + 1)
                sp.wait_ge(s["x2_lo"], b + 1)
                sp.dma_start(dr["x2scr"][b], x2s[:].bitcast(F32)).then_inc(s["x2_out"], 16)

            def finish(b):
                sp.wait_ge(s["x1"], b + 1)
                sp.dma_start(dr["x1scr"][b], x1[:]).then_inc(s["x1_out"], 16)

            def step(b, slot):
                if more(b, 2):
                    load_x(b + 2)
                    load_ctx(b + 2)
                if not is_first(b):
                    sp.wait_ge(s["v_lo"], b)
                sp.dma_start(t["v_full"][:, :, bass.ds(b * VCH, VCH)],
                             dr["vw"][:, :, bass.ds(b * VCH, VCH)]).then_inc(s["vst_in"], 16)
                if not is_first(b):
                    finish(b - 1)
                    load_residual(b)
                maxima(b, 0, slot)
                if more(b, 1):
                    k_bounce(b + 1, 0, b)
                maxima(b, 1, slot)
                if more(b, 1):
                    k_bounce(b + 1, 1, b)
                if isinstance(b, int) and b == B - 1:
                    sp.wait_ge(s["st_sc"], UN * b)
                    for i in range(N_QKW):
                        sp.dma_start(*qk_piece(t, dr, i)).then_inc(t["qkw_in"][i], 16)
                if is_first(b):
                    sp.wait_ge(s["ones"], 4)
                if more(b, 1):
                    q_bounce(b + 1, b)
                    stack_k(b + 1, 1 - slot)
                    stack_q(b + 1, 1 - slot)
                if not is_first(b):
                    store_x2(b - 1)

            load_x(1)
            k_bounce(0, 0)
            k_bounce(0, 1)
            q_bounce(0)
            sp.wait_ge(s["ones"], 2)
            sp.wait_ge(s["d_out"], 64)
            stack_k(0, 0)
            stack_q(0, 0)
            load_ctx(1)
            run(sp, step)
            finish(B - 1)
            store_x2(B - 1)
            sp.wait_ge(s["x1_out"], 16 * B)
            sp.wait_ge(s["x2_out"], 16 * B)

        @block.gpsimd
        def _(pool):
            g = nc.gpsimd
            g.memset(half_pow[:], -0.5).then_inc(s["pow_c"], 1)
            g.memset(vxh[:].bitcast(F32), 1.0).then_inc(s["pow_c"], 1)
            g.memset(vxl[:].bitcast(F32), 0.0).then_inc(s["pow_c"], 1)

            def fixed_rows(i):
                pool.wait_ge(s["rstd"], i + 1)
                pool.wait_ge(s[f"zeros{i}"], 2)
                for half in range(2):
                    g.memset(qst[i][64 * half + 32:64 * half + 64, :, S * half:S * half + S].bitcast(F32), 1.0).then_inc(s["ones"], 1)
                    pool.wait_ge(s["ones"], 2 * i + half + 1)

            pool.wait_ge(s["pow_c"], 3)

            def c_low(b):
                pool.wait_ge(s["c_hi"], b + 1)
                g.tensor_tensor(cl[:], cst[:], ch[:].bitcast(F32), ALU.subtract).then_inc(s["c_lo"], 1)

            def inverse_root(b):
                pool.wait_ge(s["ve"], b + 1)
                g.tensor_tensor(rstd[:], ve[:], half_pow[0:S, :], ALU.pow).then_inc(s["rstd"], 1)

            def q_low(b):
                pool.wait_ge(s["q_hi"], b + 1)
                g.tensor_tensor(ql[:], qf, qh[:].bitcast(F32), ALU.subtract).then_inc(s["q_lo"], 1)

            def residual(b):
                pool.wait_ge(s["xb_in"], 16 * b + 16)
                if is_first(b):
                    pool.wait_ge(s["small_in"], 96)
                g.tensor_tensor(xb[:], xb[:], bo[0:S, :], ALU.add).then_inc(s["xb"], 1)

            def values_low(b):
                pool.wait_ge(s["vx_hi"], b + 1)
                g.tensor_tensor(vxl[:, :, :, 0:DK], vf[:], vxh[:, :, :, 0:DK].bitcast(F32), ALU.subtract).then_inc(s["vx_lo"], 1)

            def v_split(b):
                pool.wait_ge(s["vst_in"], 16 * b + 16)
                hi = t["v_hi"][:, :, bass.ds(b * VCH, VCH)]
                lo = t["v_lo"][:, :, bass.ds(b * VCH, VCH)]
                full = t["v_full"][:, :, bass.ds(b * VCH, VCH)]
                g.tensor_copy(hi, full).then_inc(s["v_hi"], 1)
                pool.wait_ge(s["v_hi"], b + 1)
                g.tensor_tensor(pool_tick[:], half_pow[:], half_pow[:], ALU.add)
                g.tensor_tensor(lo, full, hi.bitcast(F32), ALU.subtract).then_inc(s["v_lo"], 1)

            def finish(b):
                pool.wait_ge(s["ve2"], b + 1)
                g.tensor_tensor(rstd2[:], ve2[:], half_pow[0:S, :], ALU.pow).then_inc(s["rstd2"], 1)

            def step(b, slot):
                values_low(b)
                if not is_first(b):
                    finish(b - 1)
                v_split(b)
                if more(b, 1):
                    q_low(b + 1)
                if not is_first(b):
                    residual(b)
                if more(b, 2):
                    inverse_root(b + 2)
                    c_low(b + 2)

            c_low(0)
            inverse_root(0)
            fixed_rows(0)
            residual(0)
            q_low(0)
            inverse_root(1)
            g.memset(kst[1][:].bitcast(F32), 0.0).then_inc(s["zeros1"], 1)
            g.memset(qst[1][:].bitcast(F32), 0.0).then_inc(s["zeros1"], 1)
            fixed_rows(1)
            c_low(1)
            run(pool, step)
            finish(B - 1)

        @block.scalar
        def _(act):
            a = nc.scalar

            def c_high(b):
                act.wait_ge(s["ctx_in"], 16 * b + 16)
                if not is_first(b):
                    act.wait_ge(s["vp"], 2 * b)
                a.copy(ch[:], cst[:]).then_inc(s["c_hi"], 1)

            def x_high(b):
                act.wait_ge(s["xT"], b + 1)
                a.copy(xth[:], bank7).then_inc(s["xt_hi"], 1)

            def k_high(b, m):
                if not is_first(b):
                    act.wait_ge(s[f"k_out{m}"], 32 * b)
                act.wait_ge(s["kp"], KD * b + m + 1)
                a.activation(kh[:, m], PS[:, 4 + m, 0:SKP], ACT.Identity, bias=bk[:, m:m + 1]).then_inc(s["k_hi"], 1)

            def q_high(b):
                act.wait_ge(s["qf"], 2 * b + 2)
                if not is_first(b):
                    act.wait_ge(s["q_out"], 32 * b)
                a.copy(qh[:], qf).then_inc(s["q_hi"], 1)

            def values_high(b):
                act.wait_ge(s["vf"], 2 * b + 2)
                if not is_first(b):
                    act.wait_ge(s["pv"], UN * b)
                a.copy(vxh[:, :, :, 0:DK], vf[:]).then_inc(s["vx_hi"], 1)

            def x2_high(b):
                act.wait_ge(s["x2T"], b + 1)
                if not is_first(b):
                    act.wait_ge(s["x2_out"], 16 * b)
                a.copy(x2s[:, 0], bank7).then_inc(s["x2_hi"], 1)

            def max_high(b, n):
                act.wait_ge(s["mT"], 2 * b + n + 1)
                if not is_first(b):
                    act.wait_ge(s[f"m_in{n}"], 64 * b)
                a.copy(mh[n][:], PS[0:HALF, 6, 128 * n:128 * n + S]).then_inc(s["m_hi"], 1)

            def diagonal_last(b):
                act.wait_ge(s["pv"], UN * b + UN)
                act.wait_ge(s["oT"], 4 * b + 2)
                for j in range(4):
                    o, i = own_queries(3, j)
                    m = a.copy(o, i)
                m.then_inc(s["od"], 1)

            def attention_high(b):
                act.wait_ge(s["aT"], b + 1)
                a.copy(ah[:], bank7).then_inc(s["a_hi"], 1)

            def step(b, slot):
                if not is_first(b):
                    diagonal_last(b - 1)
                values_high(b)
                if not is_first(b):
                    attention_high(b - 1)
                max_high(b, 0)
                if more(b, 1):
                    x_high(b + 1)
                if more(b, 1):
                    k_high(b + 1, 0)
                if not is_first(b):
                    x2_high(b - 1)
                max_high(b, 1)
                if more(b, 1):
                    k_high(b + 1, 1)
                for u in range(UN):
                    act.wait_ge(s["st_sc"], UN * b + u + 1)
                    if u >= 2 or not is_first(b):
                        act.wait_ge(s["p_lo"], UN * b + u - 1)
                    a.activation(pf[u % 2][:], PS[0:KC, u % RING, 0:4 * S], ACT.Exp).then_inc(s["p"], 1)
                    if u >= RING or not is_first(b):
                        act.wait_ge(s["pv"], UN * b + u - RING + 1)
                    a.activation(ph[u % RING][:], PS[0:KC, u % RING, 0:4 * S], ACT.Exp).then_inc(s["p_hi"], 1)
                    if u == 1 and more(b, 1):
                        q_high(b + 1)
                if more(b, 2):
                    c_high(b + 2)

            c_high(0)
            act.wait_ge(s["d_q"], 1)
            a.copy(d_hi, d_q).then_inc(s["d_hi"], 1)
            for i, n in enumerate(names):
                act.wait_ge(s[n + "_in"], 16)
                a.copy(flat(w_hi[n]), flat(w_full[n])).then_inc(s["w_hi"], 1)
            x_high(0)
            act.wait_ge(s["d_out"], 64)
            k_high(0, 0)
            k_high(0, 1)
            q_high(0)
            c_high(1)
            run(act, step)
            diagonal_last(B - 1)
            attention_high(B - 1)
            x2_high(B - 1)

        @block.vector
        def _(dve):
            v = nc.vector

            def stats(b):
                dve.wait_ge(s["x_in"], 16 * b + 16)
                v.bn_stats(stat[:], xin[:]).then_inc(s["st"], 1)
                dve.wait_ge(s["st"], b + 1)
                v.memset(tick[:], 0.0)
                v.bn_aggr(mv[:], stat[:]).then_inc(s["mv"], 1)
                dve.wait_ge(s["mv"], b + 1)
                v.tensor_scalar(ve[:], mv[:, 1:2], EPS, None, ALU.add).then_inc(s["ve"], 1)

            def norm(b):
                dve.wait_ge(s["rstd"], b + 1)
                if not is_first(b):
                    dve.wait_ge(s["q_lo"], b)
                v.tensor_scalar(xn, xin[:], mv[:, 0:1], rstd[:], ALU.subtract, ALU.mult).then_inc(s["xn"], 1)

            def x_low(b):
                dve.wait_ge(s["xt_hi"], b + 1)
                v.tensor_tensor(xtl[:], bank7, xth[:].bitcast(F32), ALU.subtract).then_inc(s["xt_lo"], 1)

            def k_low(b, m):
                dve.wait_ge(s["k_hi"], KD * b + m + 1)
                v.scalar_tensor_tensor(out=kl[:, m], in0=PS[:, 4 + m, 0:SKP], scalar=bk[:, m:m + 1],
                                       in1=kh[:, m].bitcast(F32), op0=ALU.add, op1=ALU.subtract).then_inc(s["k_lo"], 1)

            def max_low(b, n):
                dve.wait_ge(s["m_hi"], 2 * b + n + 1)
                if not is_first(b):
                    dve.wait_ge(s[f"m_in{n}"], 64 * b)
                v.tensor_tensor(ml[n][:], PS[0:HALF, 6, 128 * n:128 * n + S], mh[n][:].bitcast(F32), ALU.subtract).then_inc(s["m_lo"], 1)

            def q_scaled(b):
                dve.wait_ge(s["qp"], b + 1)
                for m in range(KD):
                    v.tensor_scalar(qf[:, m], PS[:, 7, m * S:(m + 1) * S], bq[:, m:m + 1], tau4[:, bass.ds(b, 1)],
                                    ALU.add, ALU.mult).then_inc(s["qf"], 1)

            def values(b, c):
                dve.wait_ge(s["vp"], 2 * b + c + 1)
                k = 2 - c
                if c == 0 and not is_first(b):
                    dve.wait_ge(s["vx_lo"], b)
                v.tensor_tensor(vf[:, 2 * c:2 * c + k],
                                PS[0:KC, 7, 0:k * D].rearrange("p (c h d) -> p c h d", c=k, h=XH),
                                spread(bv[0:KC, :].rearrange("p (h d) -> p h d", h=XH), 1, k), ALU.add).then_inc(s["vf"], 1)

            def diagonal(b, g4):
                dve.wait_ge(s["pv"], UN * b + NC * (g4 + 1))
                if g4 >= 2 or not is_first(b):
                    dve.wait_ge(s["oT"], 4 * b + g4 - 1)
                for j in range(4):
                    o, i = own_queries(g4, j)
                    m = v.tensor_copy(o, i)
                m.then_inc(s["od"], 1)

            def x2_norm(b):
                dve.wait_ge(s["rstd2"], b + 1)
                v.tensor_scalar(x2[:], x1[:], mv2[:, 0:1], rstd2[:], ALU.subtract, ALU.mult).then_inc(s["x2"], 1)

            def x2_low(b):
                dve.wait_ge(s["x2_hi"], b + 1)
                v.tensor_tensor(x2s[:, 1], bank7, x2s[:, 0].bitcast(F32), ALU.subtract).then_inc(s["x2_lo"], 1)

            def attended(b):
                dve.wait_ge(s["oT"], 4 * b + 4)
                o = PS[0:S, 4].rearrange("p (h d) -> p h d", h=XH)
                v.reciprocal(rs[:], o[:, :, DK]).then_inc(s["rs"], 1)
                dve.wait_ge(s["rs"], b + 1)
                v.tensor_tensor(af[:].rearrange("p (h d) -> p h d", h=XH), o[:, :, 0:DK],
                                spread(rs[:], 2, DK), ALU.mult).then_inc(s["af"], 1)

            def attention_low(b):
                dve.wait_ge(s["a_hi"], b + 1)
                v.tensor_tensor(al[:], bank7, ah[:].bitcast(F32), ALU.subtract).then_inc(s["a_lo"], 1)

            def residual_sum(b):
                dve.wait_ge(s["op"], b + 1)
                dve.wait_ge(s["xb"], b + 1)
                if not is_first(b):
                    dve.wait_ge(s["x1_out"], 16 * b)
                v.tensor_tensor(x1[:], PS[0:S, 7, 0:D], xb[:], ALU.add).then_inc(s["x1"], 1)
                dve.wait_ge(s["x1"], b + 1)
                v.bn_stats(stat2[:], x1[:]).then_inc(s["st2"], 1)
                dve.wait_ge(s["st2"], b + 1)
                v.memset(tick[:], 0.0)
                v.bn_aggr(mv2[:], stat2[:]).then_inc(s["mv2"], 1)
                dve.wait_ge(s["mv2"], b + 1)
                v.tensor_scalar(ve2[:], mv2[:, 1:2], EPS, None, ALU.add).then_inc(s["ve2"], 1)

            def step(b, slot):
                late = not is_first(b)
                for g in range(8):
                    dve.wait_ge(s["sc"], 8 * b + g + 1)
                    if g == 0 and late:
                        dve.wait_ge(s["mT"], 2 * b)
                    bank = 2 * (g % 2)
                    v.tensor_reduce(nm[:, g // QUAD, :, g % QUAD], PS[0:S, bank:bank + 2, 0:SK], AX.X, ALU.max,
                                    negate=True).then_inc(s["mx"], 1)
                    if g == 1 and late:
                        attended(b - 1)
                    if g == 2 and late:
                        attention_low(b - 1)
                    if g == 4 and late:
                        residual_sum(b - 1)
                    if g == 5:
                        max_low(b, 0)
                        if more(b, 1):
                            x_low(b + 1)
                    if g == 6 and late:
                        x2_norm(b - 1)
                    if g == 7 and late:
                        x2_low(b - 1)
                    if g == 6 and more(b, 1):
                        k_low(b + 1, 0)
                max_low(b, 1)
                if more(b, 1):
                    k_low(b + 1, 1)
                for u in range(UN):
                    dve.wait_ge(s["p_hi"], UN * b + u + 1)
                    v.tensor_tensor(pl[u % RING][:], pf[u % 2][:], ph[u % RING][:].bitcast(F32),
                                    ALU.subtract).then_inc(s["p_lo"], 1)
                    if u == 0 and more(b, 1):
                        q_scaled(b + 1)
                    if u == 2 and more(b, 2):
                        stats(b + 2)
                    if u % NC == 1 and u > NC:
                        diagonal(b, u // NC - 1)
                    if u == 5 and more(b, 1):
                        values(b + 1, 0)
                    if u == 9 and more(b, 1):
                        values(b + 1, 1)
                if more(b, 2):
                    norm(b + 2)

            v.memset(kst[0][:].bitcast(F32), 0.0).then_inc(s["zeros0"], 1)
            v.memset(qst[0][:].bitcast(F32), 0.0).then_inc(s["zeros0"], 1)
            dve.wait_ge(s["small_in"], 96)
            v.tensor_scalar(d_q, d_in, 0.25, None, ALU.mult).then_inc(s["d_q"], 1)
            v.tensor_scalar(tau4[:], tau4[:], 0.25, None, ALU.mult).then_inc(s["tau"], 1)
            dve.wait_ge(s["d_hi"], 1)
            v.tensor_tensor(d_lo, d_q, d_hi.bitcast(F32), ALU.subtract).then_inc(s["d_lo"], 1)
            stats(0)
            for i, n in enumerate(names):
                dve.wait_ge(s["w_hi"], i + 1)
                v.tensor_tensor(flat(w_lo[n]), flat(w_full[n]), flat(w_hi[n]).bitcast(F32), ALU.subtract).then_inc(s["w_lo"], 1)
            dve.wait_ge(s["tau"], 1)
            norm(0)
            x_low(0)
            dve.wait_ge(s["d_out"], 64)
            k_low(0, 0)
            k_low(0, 1)
            q_scaled(0)
            stats(1)
            values(0, 0)
            values(0, 1)
            norm(1)
            run(dve, step)
            attended(B - 1)
            attention_low(B - 1)
            residual_sum(B - 1)
            x2_norm(B - 1)
            x2_low(B - 1)

        @block.tensor
        def _(pe):
            mm = nc.tensor.matmul

            def products(out, pairs, first=True, last=True):
                n, total = 0, 3 * len(pairs)
                for lh, ll, rh, rl in pairs:
                    for l, r in ((ll, rh), (lh, rl), (lh, rh)):
                        m = mm(out, l, r, start=(first and n == 0), stop=(last and n == total - 1))
                        n += 1
                return m

            def transposed(src):
                for k in range(KD):
                    m = nc.tensor.transpose(PS[:, 7, k * S:(k + 1) * S], src[:, 128 * k:128 * k + 128], ident[0:S, 0:S])
                return m

            def x_transpose(b):
                pe.wait_ge(s["xn"], b + 1)
                if not isinstance(b, int) or b > 1:
                    pe.wait_ge(s["x1"], b - 1)
                transposed(xn).then_inc(s["xT"], 1)

            def k_part(b, m, k):
                if m == 0 and k == 0:
                    if is_first(b):
                        pe.wait_ge(s["w_lo"], 1)
                    pe.wait_ge(s["c_lo"], b + 1)
                c = slice(128 * m, 128 * m + 128)
                x = products(PS[:, 4 + m, 0:SKP], [(w_hi["wk"][:, k, c], w_lo["wk"][:, k, c], ch[:, k], cl[:, k])],
                             first=(k == 0), last=(k == KD - 1))
                if k == KD - 1:
                    x.then_inc(s["kp"], 1)

            def q_project(b):
                if is_first(b):
                    pe.wait_ge(s["w_lo"], 2)
                pe.wait_ge(s["xt_lo"], b + 1)
                for m in range(KD):
                    c = slice(128 * m, 128 * m + 128)
                    x = products(PS[:, 7, m * S:(m + 1) * S],
                                 [(w_hi["wq"][:, k, c], w_lo["wq"][:, k, c], xth[:, k], xtl[:, k]) for k in range(KD)])
                x.then_inc(s["qp"], 1)

            def v_project(b, c):
                if is_first(b) and c == 0:
                    pe.wait_ge(s["w_lo"], len(names))
                if c == 0:
                    pe.wait_ge(s["qf"], 2 * b + 2)
                if c == 2:
                    pe.wait_ge(s["vf"], 2 * b + 1)
                r = slice(KC * c, KC * c + KC)
                x = products(PS[0:KC, 7, D * (c % 2):D * (c % 2) + D],
                             [(ch[:, k, r], cl[:, k, r], w_hi["wv"][:, k], w_lo["wv"][:, k]) for k in range(KD)])
                if c:
                    x.then_inc(s["vp"], 1)

            def max_transpose(b, n):
                if n:
                    pe.wait_ge(s["m_lo"], 2 * b + n)
                nc.tensor.transpose(PS[0:HALF, 6, 128 * n:128 * n + S], nm[:, n].rearrange("p a i -> p (a i)"), ident[0:S, 0:S]).then_inc(s["mT"], 1)

            def attended(b, g4):
                pe.wait_ge(s["od"], 4 * b + g4 + 1)
                nc.tensor.transpose(PS[0:S, 4, 128 * g4:128 * g4 + 128], od[g4 % 2][:], ident[:]).then_inc(s["oT"], 1)

            def x2_transpose(b):
                pe.wait_ge(s["x2"], b + 1)
                if more(b, 2):
                    pe.wait_ge(s["xt_lo"], b + 3)
                transposed(x2).then_inc(s["x2T"], 1)

            def x2_transpose(b):
                pe.wait_ge(s["x2"], b + 1)
                if more(b, 2):
                    pe.wait_ge(s["xt_lo"], b + 3)
                transposed(x2).then_inc(s["x2T"], 1)

            def attention_transpose(b):
                pe.wait_ge(s["af"], b + 1)
                if more(b, 1):
                    pe.wait_ge(s["vf"], 2 * b + 4)
                transposed(af).then_inc(s["aT"], 1)

            def output_project(b):
                pe.wait_ge(s["a_lo"], b + 1)
                products(PS[0:S, 7, 0:D], [(ah[:, k], al[:, k], w_hi["wo"][:, k], w_lo["wo"][:, k])
                                           for k in range(KD)]).then_inc(s["op"], 1)

            def step(b, slot):
                ks, qs = kst[slot], qst[slot]
                pe.wait_ge(s["kst_in"], 128 * b + 128)
                pe.wait_ge(s["qst_in"], 96 * b + 96)
                if not is_first(b):
                    pe.wait_ge(s["p_hi"], UN * b)
                for g in range(8):
                    if g >= 2:
                        pe.wait_ge(s["mx"], 8 * b + g - 1)
                    if g == 5:
                        max_transpose(b, 0)
                    for half in range(2):
                        r = slice(64 * half, 64 * half + ROWS_S)
                        m = mm(PS[0:S, 2 * (g % 2) + half, 0:SKP], qs[r, g, S * half:S * half + S], ks[r, g],
                               start=True, stop=True)
                    m.then_inc(s["sc"], 1)
                    late = not is_first(b)
                    if g == 1 and late:
                        attended(b - 1, 3)
                    if g == 2 and late:
                        attention_transpose(b - 1)
                    if g == 4 and late:
                        output_project(b - 1)
                    if g == 5 and more(b, 1):
                        x_transpose(b + 1)
                    if g in K_AT and more(b, 1):
                        part = K_AT.index(g)
                        k_part(b + 1, part // KD, part % KD)
                if not is_first(b):
                    x2_transpose(b - 1)
                pe.wait_ge(s["mx"], 8 * b + 8)
                max_transpose(b, 1)
                for u in range(UN + LEAD):
                    if u < UN:
                        if u >= RING:
                            pe.wait_ge(s["p_hi"], UN * b + u - RING + 1)
                        g4, c = u // NC, u % NC
                        if u % (UN // 2) == 0:
                            pe.wait_ge(s[f"m_in{u // (UN // 2)}"], 64 * b + 64)
                        for j in range(2):
                            i = 2 * g4 + j
                            m = mm(PS[0:KC, u % RING, j * 2 * S:(j + 1) * 2 * S],
                                   ks[:, i, KC * c:KC * c + KC], qs[:, i], start=True, stop=True)
                        m.then_inc(s["st_sc"], 1)
                    if u == Q_AT and more(b, 1):
                        if not is_first(b):
                            pe.wait_ge(s["x2_lo"], b)
                        q_project(b + 1)
                    if u in V_AT and more(b, 1):
                        v_project(b + 1, V_AT.index(u))
                    if u >= LEAD:
                        w = u - LEAD
                        g4, c = w // NC, w % NC
                        if w == 0:
                            pe.wait_ge(s["vx_lo"], b + 1)
                            if more(b, 1):
                                pe.wait_ge(s["k_lo"], 2 * b + 4)
                        pe.wait_ge(s["p_lo"], UN * b + w + 1)
                        val = [x[:, c].rearrange("p h d -> p (h d)")[:, 4 * DV * g4:4 * DV * g4 + 4 * DV] for x in (vxh, vxl)]
                        products(PS[:, 5 + g4 % 2, 0:4 * S], [(val[0], val[1], ph[w % RING][:], pl[w % RING][:])],
                                 first=(c == 0), last=(c == NC - 1)).then_inc(s["pv"], 1)
                        if c == 1 and g4:
                            attended(b, g4 - 1)
            x_transpose(0)
            for m in range(KD):
                for k in range(KD):
                    k_part(0, m, k)
            q_project(0)
            for c in range(NC):
                v_project(0, c)
            run(pe, step)
            attended(B - 1, 3)
            attention_transpose(B - 1)
            output_project(B - 1)
            x2_transpose(B - 1)


def attend_block(nc, t, dr):
    with ExitStack() as ctx:
        def sb(name, shape, dt=F32):
            return ctx.enter_context(nc.sbuf_tensor("b_" + name, shape, dt))

        G = 2 * H
        scale = float(P) ** -0.5
        qk_lo, qk_full = t["qk_lo"], t["qk_full"]
        qk_hi = sb("qk_hi", [128, KD, 2 * H * P], F32R)
        sel_hi = sb("sel_hi", [128, KD, G * E], F32R)
        sel_lo, sel_full = arriving(nc, ctx, "b_sel_lo", [128, KD, G * E])
        route = sb("route", [128, 1])
        pickf = sb("pickf", [2 * E, E])
        rank = sb("rank", [S, E])
        x2a = sb("x2a", [128, 2, KD, 2, S], F32R)
        x2v = sb("x2v", [128, 2, KD, S], F32R)
        G2 = 2 * G
        lg = sb("lg", [S, G2, E]); ex = sb("ex", [S, G2, E]); l2 = sb("l2", [S, G2, E])
        ea = sb("ea", [S, G2, E]); eb = sb("eb", [S, G2, E]); oh1 = sb("oh1", [S, G2, E]); oh2 = sb("oh2", [S, G2, E])
        gm = sb("gm", [S, 4, G2]); gr = sb("gr", [S, 3, G2])
        gate = sb("gate", [S, G2, E])
        gate_o = gate[:].rearrange("p (j i h) e -> p j i h e", j=2, i=2)[:, :, 1]
        gsp = sb("gsp", [S, 2, H, 2, E], F32R)
        gT = sb("gT", [128, S])
        qk = t["qk"]
        nm = sb("nm", [S, H]); nms = sb("nms", [S, H]); den = sb("den", [S, H]); rden = sb("rden", [S, H])
        att = sb("att", [S, H, S]); attT = sb("attT", [S, H, S])
        vacc = sb("vacc", [S, H, P])
        cs = sb("cs", [P, H, S])
        PS = ctx.enter_context(nc.psum_tensor("ps2", [128, 8, 512], F32))
        s = {n: ctx.enter_context(nc.semaphore("b_" + n)) for n in (
            "late_in0", "late_in1", "late_in2", "late_hi0", "late_hi1", "late_hi2", "late_lo", "sel_in", "route_in", "w_hi", "w_lo", "sel_hi", "sel_lo", "rank", "pick",
            "x2a_in", "x2v_in", "lgp", "lg", "ex", "gs", "gate", "g_hi", "g_lo", "gTp", "gT", "gT_out",
            "qkp", "qk", "scp", "nm", "nms", "exp", "rden", "att", "attTp", "attT",
            "vp", "v0", "acc", "cxp", "cs", "c_out")}
        block = ctx.enter_context(nc.Block())
        ident = t["ident"]
        late_hi = sb("late_hi", [128, KD, (H - HE) * E * P], F32R)
        late_lo, late_full = arriving(nc, ctx, "b_late_lo", [128, KD, (H - HE) * E * P])
        n_late = H - HE

        def expert_columns(part, k, h, c):
            if h >= HE:
                return (late_lo if part else late_hi)[:, k, (h - HE) * E * P + c:(h - HE) * E * P + c + 512]
            return t["v_lo" if part else "v_hi"][:, k, h * E * P + c:h * E * P + c + 512]

        NQ = H

        def run(eng, step):
            step(0, 0, False)
            step(1, 0, True)
            with eng.Fori(1, B // 2 - 1) as i:
                step(2 * i, i, False)
                step(2 * i + 1, i, True)
            step(B - 2, B // 2 - 1, False)
            step(B - 1, B // 2 - 1, True, last=True)

        units = [(2 * hp + j, half) for hp in range(H // 2) for half in range(2) for j in range(2)]
        NU = len(units)
        halves0 = [u for u, (_, half) in enumerate(units) if half == 0]

        @block.sync
        def _(sp):
            sp.dma_start(sel_full[:, :, 0:G * E // 2], dr["sel_v"]).then_inc(s["sel_in"], 16)
            sp.dma_start(sel_full[:, :, G * E // 2:], dr["sel_o"]).then_inc(s["sel_in"], 16)

            def load_a(pair):
                if not is_first(pair):
                    sp.wait_ge(s["qkp"], NQ * pair)
                for j in range(2):
                    sp.dma_start(x2a[:, :, :, j].bitcast(F32), dr["x2scr"][2 * pair + j]).then_inc(s["x2a_in"], 16)

            def load_v(b):
                if not is_first(b):
                    sp.wait_ge(s["vp"], NU * (b - 1) + NU)
                sp.dma_start(x2v[:].bitcast(F32), dr["x2scr"][b]).then_inc(s["x2v_in"], 16)

            load_a(0)
            sp.dma_start(route[:], spread(dr["route"], 0, 128)).then_inc(s["route_in"], 16)
            load_v(0)
            for i in range(n_late):
                c = (HE + i) * E * P
                sp.dma_start(late_full[:, :, E * P * i:E * P * i + E * P], dr["vw"][:, :, c:c + E * P]).then_inc(s[f"late_in{i}"], 16)

            def step(b, pair, odd, last=False):
                if odd and not last:
                    load_a(pair + 1)
                if last:
                    sp.wait_ge(s["scp"], 2 * B)
                    sp.dma_start(t["stage0"][:], dr["ow"][:, 0:E]).then_inc(t["o_in"][0], 16)
                    sp.wait_ge(s["gT_out"], 16 * (b - 1))
                    sp.wait_ge(s["c_out"], 32 * (b - 1))
                    load_chunk(sp, dr, 0, t["gs0"], t["cx0"], t["xr"][0], t["in0"])
                sp.wait_ge(s["gT"], b + 1)
                sp.dma_start(dr["gscr"][:, bass.ds(b * S, S)], gT[:]).then_inc(s["gT_out"], 16)
                if not last:
                    load_v(b + 1)
                for i in range(2):
                    sp.wait_ge(s["cs"], 2 * b + i + 1)
                    sp.dma_start(dr["cscr"][:, 4 * i:4 * i + 4, bass.ds(b * S, S)], cs[:, 4 * i:4 * i + 4]).then_inc(s["c_out"], 16)

            run(sp, step)
            sp.wait_ge(s["gT_out"], 16 * B)
            sp.wait_ge(s["c_out"], 32 * B)

        @block.gpsimd
        def _(pool):
            g = nc.gpsimd
            for e in range(E):
                m = g.memset(rank[:, e:e + 1], float(E - e))
            m.then_inc(s["rank"], 1)
            pool.wait_ge(s["rank"], 1)
            g.memset(pickf[:], 0.0).then_inc(s["pick"], 1)
            pool.wait_ge(s["pick"], 1)
            for r in range(2):
                g.affine_select(out=pickf[:], in_=pickf[:], compare_op=ALU.not_equal, fill=1.0, base=-E * r,
                                pattern=[[-1, E]], channel_multiplier=1).then_inc(s["pick"], 1)
                pool.wait_ge(s["pick"], r + 2)
            g.tensor_copy(t["pick"][:], pickf[:]).then_inc(s["pick"], 1)
            pool.wait_ge(s["pick"], 4)
            pool.wait_ge(s["sel_hi"], 1)
            g.tensor_tensor(sel_lo[:], sel_full[:], sel_hi[:].bitcast(F32), ALU.subtract).then_inc(s["sel_lo"], 1)

            def late_low(i):
                c = slice(i * E * P, i * E * P + E * P)
                pool.wait_ge(s[f"late_hi{i}"], 1)
                g.tensor_tensor(late_lo[:, :, c], late_full[:, :, c], late_hi[:, :, c].bitcast(F32), ALU.subtract).then_inc(s["late_lo"], 1)

            def normalise(b):
                pool.wait_ge(s["rden"], b + 1)
                g.tensor_tensor(att[:], att[:], spread(rden[:], 2, S), ALU.mult).then_inc(s["att"], 1)

            late_low(0)
            late_low(1)
            normalise(0)
            late_low(2)
            with pool.Fori(1, B) as b:
                normalise(b)

        @block.scalar
        def _(act):
            a = nc.scalar

            def qk_high(i):
                k, c = i % KD, slice((i // KD) * H * P, (i // KD + 1) * H * P)
                act.wait_ge(t["qkw_in"][i], 16)
                a.copy(qk_hi[:, k, c], qk_full[:, k, c]).then_inc(s["w_hi"], 1)

            qk_high(0)
            qk_high(1)
            act.wait_ge(s["sel_in"], 32)
            a.copy(sel_hi[:], sel_full[:]).then_inc(s["sel_hi"], 1)
            for i in range(2, N_QKW):
                qk_high(i)

            def pre(b, pair, odd):
                if not odd:
                    act.wait_ge(s["lgp"], pair + 1)
                    if not is_first(b):
                        act.wait_ge(s["gate"], pair)
                    logits = PS[0:S, 4, 0:G2 * E].rearrange("p (g e) -> p g e", g=G2)
                    a.copy(lg[:], logits).then_inc(s["lg"], 1)
                    a.activation(ex[:], logits, ACT.Exp, scale=-1.0).then_inc(s["ex"], 1)
                for i in range(0 if odd else NQ):
                    act.wait_ge(s["qkp"], NQ * pair + i + 1)
                    a.copy(qk[:, 2 * i:2 * i + 2], PS[:, 5 - i % 2, 0:4 * S].rearrange("p (m j s) -> p m j s", m=2, j=2)).then_inc(s["qk"], 1)
                    if is_first(b) and i == 0:
                        act.wait_ge(s["late_in0"], 16)
                        a.copy(late_hi[:, :, 0:E * P], late_full[:, :, 0:E * P]).then_inc(s["late_hi0"], 1)
                if not is_first(b):
                    act.wait_ge(s["attTp"], 2 * b)
                for h in range(H):
                    if h % 4 == 0:
                        act.wait_ge(s["nms"], 2 * b + h // 4 + 1)
                    a.activation(att[:, h], PS[0:S, 5 - h // 4, (h % 4) * S:(h % 4 + 1) * S], ACT.Exp, bias=nms[:, h:h + 1],
                                 scale=scale, accum_out=den[:, h:h + 1]).then_inc(s["exp"], 1)

            def step(b, pair, odd, last=False):
                for n, u in enumerate(halves0):
                    h, _ = units[u]
                    act.wait_ge(s["vp"], NU * b + u + 1)
                    if n == 0:
                        act.wait_ge(s["gate"], pair + 1)
                        if not is_first(b):
                            act.wait_ge(s["cxp"], 2 * (b - 1) + 2)
                    a.activation(vacc[:, h], PS[0:S, u % 4, 0:P], ACT.Copy, scale=gate[:, G * odd + h, 0:1]).then_inc(s["v0"], 1)
                    if n == 1:
                        act.wait_ge(s["gTp"], b + 1)
                        if not is_first(b):
                            act.wait_ge(s["gT_out"], 16 * (b - 1) + 16)
                        a.copy(gT[:], PS[:, 4, 0:S]).then_inc(s["gT"], 1)
                        for i in range(2):
                            act.wait_ge(s["attTp"], 2 * b + i + 1)
                            a.copy(attT[:, 4 * i:4 * i + 4], PS[0:S, 6 + i, 0:4 * S].rearrange("p (m s) -> p m s", m=4)).then_inc(s["attT"], 1)
                if not last:
                    pre(b + 1, pair + 1 if odd else pair, not odd)
                for i in range(2):
                    act.wait_ge(s["cxp"], 2 * b + i + 1)
                    if i == 0 and not is_first(b):
                        act.wait_ge(s["c_out"], 32 * (b - 1) + 32)
                    a.copy(cs[:, 4 * i:4 * i + 4], PS[:, 6 + i, 0:4 * S].rearrange("p (m s) -> p m s", m=4)).then_inc(s["cs"], 1)

            pre(0, 0, False)
            run(act, step)

        @block.vector
        def _(dve):
            v = nc.vector
            for i in range(N_QKW):
                c = slice((i // KD) * H * P, (i // KD + 1) * H * P)
                dve.wait_ge(s["w_hi"], i + 1)
                v.tensor_tensor(qk_lo[:, i % KD, c], qk_full[:, i % KD, c], qk_hi[:, i % KD, c].bitcast(F32), ALU.subtract).then_inc(s["w_lo"], 1)
            dve.wait_ge(s["rank"], 1)
            dve.wait_ge(s["route_in"], 16)
            NG = 17

            def gates(pair):
                count = [0]
                ranks = spread(rank[:], 1, G2)

                def then(ins):
                    count[0] += 1
                    ins.then_inc(s["gs"], 1)
                    dve.wait_ge(s["gs"], NG * pair + count[0])

                dve.wait_ge(s["ex"], pair + 1)
                if not is_first(pair):
                    dve.wait_ge(s["g_lo"], pair)
                v.tensor_scalar(ex[:], ex[:], 1.0, None, ALU.add)
                then(v.tensor_reduce(gm[:, 0], lg[:], AX.X, ALU.max))
                then(v.tensor_tensor(ea[:], lg[:], spread(gm[:, 0], 2, E), ALU.is_equal))
                then(v.reciprocal(ex[:], ex[:]))
                then(v.tensor_tensor(eb[:], ea[:], ranks, ALU.mult))
                then(v.tensor_reduce(gm[:, 1], eb[:], AX.X, ALU.max))
                then(v.tensor_tensor(oh1[:], eb[:], spread(gm[:, 1], 2, E), ALU.is_equal))
                then(v.scalar_tensor_tensor(out=l2[:], in0=oh1[:], scalar=-BIG, in1=lg[:], op0=ALU.mult, op1=ALU.add))
                then(v.tensor_reduce(gm[:, 2], l2[:], AX.X, ALU.max))
                then(v.tensor_tensor(ea[:], l2[:], spread(gm[:, 2], 2, E), ALU.is_equal))
                then(v.tensor_tensor(eb[:], ea[:], ranks, ALU.mult))
                then(v.tensor_reduce(gm[:, 3], eb[:], AX.X, ALU.max))
                then(v.tensor_tensor(oh2[:], eb[:], spread(gm[:, 3], 2, E), ALU.is_equal))
                then(v.tensor_tensor(ea[:], oh1[:], oh2[:], ALU.add))
                then(v.tensor_tensor(eb[:], ea[:], ex[:], ALU.mult))
                then(v.tensor_reduce(gr[:, 0], eb[:], AX.X, ALU.add))
                then(v.tensor_scalar(gr[:, 1], gr[:, 0], 1e-9, None, ALU.max))
                then(v.reciprocal(gr[:, 2], gr[:, 1]))
                v.scalar_tensor_tensor(out=gate[:], in0=eb[:], scalar=route[0:S, :], in1=spread(gr[:, 2], 2, E),
                                       op0=ALU.mult, op1=ALU.mult).then_inc(s["gate"], 1)
                dve.wait_ge(s["gate"], pair + 1)
                if not is_first(pair):
                    dve.wait_ge(s["gTp"], 2 * pair)
                v.tensor_copy(gsp[:, :, :, 0], gate_o).then_inc(s["g_hi"], 1)
                dve.wait_ge(s["g_hi"], pair + 1)
                v.tensor_tensor(gsp[:, :, :, 1], gate_o, gsp[:, :, :, 0].bitcast(F32), ALU.subtract).then_inc(s["g_lo"], 1)

            def maxima(b):
                for i in range(2):
                    dve.wait_ge(s["scp"], 2 * b + i + 1)
                    v.tensor_reduce(nm[:, 4 * i:4 * i + 4], PS[0:S, 5 - i, 0:4 * S].rearrange("p (m s) -> p m s", m=4),
                                    AX.X, ALU.max, negate=True).then_inc(s["nm"], 1)
                    dve.wait_ge(s["nm"], 2 * b + i + 1)
                    v.tensor_scalar(nms[:, 4 * i:4 * i + 4], nm[:, 4 * i:4 * i + 4], scale, None, ALU.mult).then_inc(s["nms"], 1)

            def step(b, pair, odd, last=False):
                dve.wait_ge(s["exp"], H * b + H)
                v.reciprocal(rden[:], den[:]).then_inc(s["rden"], 1)
                PER = E * H - H
                for hp in range(H // 2):
                    for half in range(2):
                        for k in range(4):
                            if half == 0 and k == 0:
                                continue
                            for j in range(2):
                                u = 4 * hp + 2 * half + j
                                h = 2 * hp + j
                                e = 4 * half + k
                                i = 14 * hp + 2 * (e - 1) + j
                                if e == 1:
                                    dve.wait_ge(s["v0"], H * b + h + 1)
                                else:
                                    dve.wait_ge(s["acc"], PER * b + i - 1)
                                if k == 0:
                                    dve.wait_ge(s["vp"], NU * b + u + 1)
                                ins = v.scalar_tensor_tensor(out=vacc[:, h], in0=PS[0:S, u % 4, k * P:(k + 1) * P],
                                                             scalar=gate[:, G * odd + h, e:e + 1], in1=vacc[:, h],
                                                             op0=ALU.mult, op1=ALU.add)
                                ins.then_inc(s["acc"], 1)
                if odd and not last:
                    gates(pair + 1)
                if not last:
                    maxima(b + 1)

            gates(0)
            for i in range(1, n_late):
                c = slice(i * E * P, i * E * P + E * P)
                dve.wait_ge(s[f"late_in{i}"], 16)
                v.tensor_copy(late_hi[:, :, c], late_full[:, :, c]).then_inc(s[f"late_hi{i}"], 1)
            maxima(0)
            run(dve, step)

        @block.tensor
        def _(pe):
            mm = nc.tensor.matmul
            PER = E * H - H

            def pre(b, pair, odd):
                if is_first(b):
                    pe.wait_ge(s["sel_lo"], 1)
                if not is_first(b):
                    pe.wait_ge(s["gT"], b)
                if not odd:
                    pe.wait_ge(s["x2a_in"], 32 * pair + 32)
                    for j in range(2):
                        n = 0
                        for k in range(KD):
                            for l, r in ((1, sel_hi), (0, sel_lo), (0, sel_hi)):
                                m = mm(PS[0:S, 4, G * E * j:G * E * (j + 1)], x2a[:, l, k, j], r[:, k], start=(n == 0), stop=(n == 5))
                                n += 1
                    m.then_inc(s["lgp"], 1)
                    project(b, pair)
                for i in range(2):
                    if not odd:
                        pe.wait_ge(s["qk"], NQ * pair + NQ)
                    for j in range(4):
                        h = 4 * i + j
                        m = mm(PS[0:S, 5 - i, j * S:(j + 1) * S], qk[:, h, int(odd)], qk[:, H + h, int(odd)], start=True, stop=True)
                    m.then_inc(s["scp"], 1)

            def project(b, pair):
                if is_first(b):
                    pe.wait_ge(s["w_lo"], N_QKW)
                for i in range(NQ):
                    if i == 0 and not is_first(b):
                        pe.wait_ge(s["exp"], H * (b - 1) + H)
                    if i == 1:
                        pe.wait_ge(s["ex"], pair + 1)
                    if i >= 2:
                        pe.wait_ge(s["qk"], NQ * pair + i - 1)
                    for j in range(2):
                        c = slice((2 * i + j) * P, (2 * i + j + 1) * P)
                        n = 0
                        for k in range(KD):
                            for l, r in ((qk_lo, 0), (qk_hi, 1), (qk_hi, 0)):
                                m = mm(PS[:, 5 - i % 2, 2 * j * S:2 * (j + 1) * S], l[:, k, c], x2a[:, r, k],
                                       start=(n == 0), stop=(n == 5))
                                n += 1
                    m.then_inc(s["qkp"], 1)

            def step(b, pair, odd, last=False):
                pe.wait_ge(s["x2v_in"], 16 * b + 16)
                for u, (h, half) in enumerate(units):
                    hp, j = h // 2, h % 2
                    if u >= 4 or not is_first(b):
                        w = u - 4 if u >= 4 else u - 4 + NU
                        ph, phalf = units[w]
                        place = 14 * (ph // 2) + 2 * (4 * phalf + 2) + ph % 2 + 1
                        pe.wait_ge(s["acc"], PER * b + place if u >= 4 else PER * (b - 1) + place)
                    if h >= HE and is_first(b):
                        pe.wait_ge(s["late_lo"], h - HE + 1)
                    n = 0
                    for k in range(KD):
                        for l, r in ((1, 0), (0, 1), (0, 0)):
                            m = mm(PS[0:S, u % 4], x2v[:, l, k], expert_columns(r, k, h, half * 512), start=(n == 0), stop=(n == 5))
                            n += 1
                    m.then_inc(s["vp"], 1)
                    if u == 3:
                        pe.wait_ge(s["g_lo"], pair + 1)
                        pe.wait_ge(s["exp"], H * b + H)
                        nc.tensor.transpose(PS[:, 4, 0:S], gsp[:, int(odd)].rearrange("p h a e -> p (h a e)").bitcast(F32), ident[0:S, 0:S]).then_inc(s["gTp"], 1)
                        pe.wait_ge(s["att"], b + 1)
                        for i in range(2):
                            if i == 0 and not is_first(b):
                                pe.wait_ge(s["cs"], 2 * (b - 1) + 2)
                            for jj in range(4):
                                m = nc.tensor.transpose(PS[0:S, 6 + i, jj * S:(jj + 1) * S], att[:, 4 * i + jj], ident[0:S, 0:S])
                            m.then_inc(s["attTp"], 1)
                if not last:
                    pre(b + 1, pair + 1 if odd else pair, not odd)
                pe.wait_ge(s["attT"], 2 * b + 2)
                pe.wait_ge(s["acc"], PER * b + PER)
                for i in range(2):
                    for jj in range(4):
                        h = 4 * i + jj
                        m = mm(PS[:, 6 + i, jj * S:(jj + 1) * S], vacc[:, h], attT[:, h], start=True, stop=True)
                    m.then_inc(s["cxp"], 1)

            pre(0, 0, False)
            run(pe, step)


def output_block(nc, t, dr):
    with ExitStack() as ctx:
        def sb(name, shape, dt=F32):
            return ctx.enter_context(nc.sbuf_tensor("c_" + name, shape, dt))

        TT = TOK // 128
        EP = E // 2
        UPC = H * EP
        ow = sb("ow", [P, H * E, 2, D], F32R)
        pick = t["pick"]
        gs = [t["gs0"], sb("gs1", [2 * E, H, TOK], F32R)]
        cx = [t["cx0"], sb("cx1", [P, H, TOK])]
        buffers = [t["stage0"][:], *(sb(f"stage{i}", [P, E, D])[:] for i in range(1, NS)), cx[1][:].rearrange("p h t -> p (h t)").rearrange("p (e d) -> p e d", e=E)]
        place = [0, 1, 2, 3, 0, 1, 2, 0]
        stage = [buffers[i] for i in place]
        xr = t["xr"]
        wh = [t["wh0"]] + [sb(f"wh{i}", [P, 2, TOK], F32R) for i in range(1, EP)]
        wl = [sb(f"wl{i}", [P, 2, TOK], F32R) for i in range(EP)]
        PS = ctx.enter_context(nc.psum_tensor("ps3", [128, 8, 512], F32))
        s = {n: ctx.enter_context(nc.semaphore("c_" + n)) for n in (
            "first_hi", "first_lo", "o_hi", "o_lo", "in1", "g", "w", "w_hi", "w_lo", "used", "y1", "y", "out")}
        s["in0"] = t["in0"]
        w = [PS[:, q].rearrange("p (e t) -> p e t", e=2) for q in range(EP)]
        block = ctx.enter_context(nc.Block())

        def chunks(eng, f):
            f(0, 0, 0)
            with eng.Fori(0, (NT - 1) // 2 - 1) as i:
                f(2 * i + 1, 1, i)
                f(2 * i + 2, 0, i + 1)
            f(NT - 2, 1, (NT - 2) // 2)
            f(NT - 1, 0, (NT - 1) // 2)

        def heads(eng, f):
            f(0)
            with eng.Fori(1, H - 1) as h:
                f(h)
            f(H - 1)

        @block.sync
        def _(sp):
            def load(c, slot):
                if not isinstance(c, int) or c > 1:
                    sp.wait_ge(s["out"], 16 * (c - 2) + 16)
                load_chunk(sp, dr, c, gs[slot], cx[slot], xr[slot], s[f"in{slot}"])

            def store(c, slot):
                sp.wait_ge(s["y"], TT * c + TT)
                sp.dma_start(dr["out"].rearrange("b s d -> (b s) d")[bass.ds(c * TOK, TOK)].rearrange("(a p) d -> p a d", p=128), xr[slot][:]).then_inc(s["out"], 16)

            for h in range(1, H):
                if h == place.index(0, 1):
                    sp.wait_ge(s["first_lo"], 1)
                if place[h] in place[0:h]:
                    sp.wait_ge(s["o_lo"], max(i for i in range(h) if place[i] == place[h]) + 1)
                sp.dma_start(stage[h], dr["ow"][:, E * h:E * h + E]).then_inc(t["o_in"][h], 16)
            load(1, 1)
            with sp.Fori(0, (NT - 1) // 2 - 1) as i:
                store(2 * i, 0)
                load(2 * i + 2, 0)
                store(2 * i + 1, 1)
                load(2 * i + 3, 1)
            store(NT - 3, 0)
            load(NT - 1, 0)
            store(NT - 2, 1)
            store(NT - 1, 0)
            sp.wait_ge(s["out"], 16 * NT)

        @block.gpsimd
        def _(pool):
            g = nc.gpsimd
            for h in range(H):
                n = 2 if h == 0 else 0
                pool.wait_ge(s["o_hi"], h + 1)
                g.tensor_tensor(ow[:, E * h + n:E * h + E, 1], stage[h][:, n:E], ow[:, E * h + n:E * h + E, 0].bitcast(F32),
                                ALU.subtract).then_inc(s["o_lo"], 1)

        @block.scalar
        def _(act):
            a = nc.scalar

            def o_high(h):
                act.wait_ge(t["o_in"][h], 16)
                n = 2 if h == 0 else 0
                if n:
                    a.copy(ow[:, 0:n, 0], stage[0][:, 0:n]).then_inc(s["first_hi"], 1)
                a.copy(ow[:, E * h + n:E * h + E, 0], stage[h][:, n:E]).then_inc(s["o_hi"], 1)

            def head(c, h):
                for q in range(EP):
                    if is_first(c) and q == EP // 2 and h + 1 < H:
                        o_high(h + 1)
                    n = UPC * c + EP * h + q
                    act.wait_ge(s["w"], n + 1)
                    if not (isinstance(n, int) and n < EP):
                        act.wait_ge(s["used"], UPC * c + EP * h + q - (EP - 1) if isinstance(n, int) else n - (EP - 1))
                    a.copy(wh[q][:], w[q]).then_inc(s["w_hi"], 1)

            o_high(0)
            for h in range(H):
                head(0, h)
            with act.Fori(1, NT) as c:
                head(c, 0)
                with act.Fori(1, H) as h:
                    head(c, h)

        @block.vector
        def _(dve):
            v = nc.vector

            def low(n, q):
                dve.wait_ge(s["w_hi"], n + 1)
                v.tensor_tensor(wl[q][:], w[q], wh[q][:].bitcast(F32), ALU.subtract).then_inc(s["w_lo"], 1)

            def head(c, slot, h):
                for q in range(EP):
                    n = UPC * c + EP * h + q
                    dve.wait_ge(s["g"], n + 1)
                    v.tensor_tensor(w[q], spread(cx[slot][:, h], 1, 2), w[q], ALU.mult).then_inc(s["w"], 1)
                    if q:
                        low(n - 1, q - 1)
                low(UPC * c + EP * h + EP - 1, EP - 1)

            def finish(c, slot):
                dve.wait_ge(s["used"], UPC * c + UPC)
                for i in range(TT):
                    v.tensor_tensor(xr[slot][:, i], PS[:, 4 + 2 * slot + i, D:2 * D], xr[slot][:, i], ALU.add).then_inc(s["y1"], 1)
                for i in range(TT):
                    dve.wait_ge(s["y1"], TT * c + i + 1)
                    v.tensor_tensor(xr[slot][:, i], PS[:, 4 + 2 * slot + i, 0:D], xr[slot][:, i], ALU.add).then_inc(s["y"], 1)

            def chunk(c, slot, turn):
                dve.wait_ge(s[f"in{slot}"], 48 * turn + 48)
                head(c, slot, 0)
                if not is_first(c):
                    finish(c - 1, 1 - slot)
                with dve.Fori(1, H) as h:
                    head(c, slot, h)

            dve.wait_ge(s["first_hi"], 1)
            v.tensor_tensor(ow[:, 0:2, 1], stage[0][:, 0:2], ow[:, 0:2, 0].bitcast(F32), ALU.subtract).then_inc(s["first_lo"], 1)
            chunks(dve, chunk)
            finish(NT - 1, 0)

        @block.tensor
        def _(pe):
            mm = nc.tensor.matmul

            def spread_gates(c, slot, h, q):
                for e in range(2):
                    m = mm(PS[:, q, e * TOK:(e + 1) * TOK], spread(pick[:, 2 * q + e], 1, 128), gs[slot][:, h], start=True, stop=True)
                m.then_inc(s["g"], 1)

            def experts(c, slot, h, q, first):
                if is_first(c) and q < 2:
                    if is_first(h) and q == 0:
                        pe.wait_ge(s["first_lo"], 1)
                    elif q == 0 or is_first(h):
                        pe.wait_ge(s["o_lo"], h + 1)
                pe.wait_ge(s["w_lo"], UPC * c + EP * h + q + 1)
                for e in range(2):
                    he = h * E + 2 * q + e
                    for i in range(TT):
                        r = slice(128 * i, 128 * i + 128)
                        mm(PS[:, 4 + 2 * slot + i], wh[q][:, e, r], ow[:, he], start=(first and e == 0), stop=False, skip_group_check=True)
                        m = mm(PS[:, 4 + 2 * slot + i, 0:D], wl[q][:, e, r], ow[:, he, 0], start=False,
                               stop=False, skip_group_check=True)
                m.then_inc(s["used"], 1)

            def chunk(c, slot, turn):
                if is_first(c):
                    pe.wait_ge(s["in0"], 48)
                    for q in range(EP):
                        spread_gates(0, 0, 0, q)

                def head(h):
                    end = isinstance(h, int) and h == H - 1
                    for q in range(EP):
                        experts(c, slot, h, q, first=isinstance(h, int) and h == 0 and q == 0)
                        if not end:
                            spread_gates(c, slot, h + 1, q)
                        elif not (isinstance(c, int) and c == NT - 1):
                            if q == 0:
                                pe.wait_ge(s[f"in{1 - slot}"], 48 * (turn + slot) + 48)
                            spread_gates(c + 1, 1 - slot, 0, q)
                heads(pe, head)

            chunks(pe, chunk)


def weights(w):
    return w.T.reshape(KD, 128, -1).transpose(1, 0, 2)


def laid_out(i):
    xc, ff = "L0_xcond_", "L0_ffn_"
    paired = np.arange(D).reshape(2, HALF, DK).transpose(1, 0, 2).reshape(-1)

    def pad(a):
        return np.pad(a, [(0, 0)] * (a.ndim - 1) + [(0, SKP - SK)])

    return {
        "x": i["x"],
        "ctxT": pad(i["ctx_1024"].transpose(0, 2, 1).reshape(B, KD, 128, SK).transpose(0, 2, 1, 3)),
        "tau": i["condB_tau"], "delta": pad(i["fside_BxS2_0"]),
        "wq": weights(i[xc + "Wq"]).reshape(128, -1), "wk": weights(i[xc + "Wk"]).reshape(128, -1),
        "wv": weights(i[xc + "Wv"][paired]).reshape(128, -1), "wo": weights(i[xc + "Wo"][:, paired]).reshape(128, -1),
        "bq": i[xc + "bq"].reshape(KD, 128).T, "bk": i[xc + "bk"].reshape(KD, 128).T,
        "bv": i[xc + "bv"][paired], "bo": i[xc + "bo"],
        "vw": i[ff + "v_w"].reshape(H, E, KD, 128, P).transpose(3, 2, 0, 1, 4).reshape(128, KD, H * E * P),
        "qkw": np.concatenate([weights(i[ff + "q_w"]), weights(i[ff + "k_w"])], axis=2),
        "sel_v": weights(i[ff + "sel_v_w"]), "sel_o": weights(i[ff + "sel_o_w"]),
        "route": i[ff + "route_scale"],
        "ow": i[ff + "o_w"].transpose(1, 0, 2),
    }


def build(nc, dr):
    with ExitStack() as ctx:
        t = {"ident": ctx.enter_context(nc.sbuf_tensor("ident", [128, 128], F32))}
        t["pick"] = ctx.enter_context(nc.sbuf_tensor("pick", [2 * E, E], F32R))
        ident_done = ctx.enter_context(nc.semaphore("ident_done"))
        with nc.Block() as block:
            @block.gpsimd
            def _(pool):
                nc.gpsimd.memset(t["ident"][:], 0.0).then_inc(ident_done, 1)
                pool.wait_ge(ident_done, 1)
                nc.gpsimd.affine_select(out=t["ident"][:], in_=t["ident"][:], compare_op=ALU.not_equal, fill=1.0, base=0,
                                        pattern=[[-1, 128]], channel_multiplier=1).then_inc(ident_done, 1)
                pool.wait_ge(ident_done, 2)
        t["in0"] = ctx.enter_context(nc.semaphore("c_in0"))
        t["qkw_in"] = [ctx.enter_context(nc.semaphore(f"qkw_in{i}")) for i in range(N_QKW)]
        t["o_in"] = [ctx.enter_context(nc.semaphore(f"o_in{h}")) for h in range(H)]
        t["kst0"], t["qst0"], t["vxh"], t["vf"], t["x2s"] = passing(
            nc, ("a_kst0", [128, HALF, SKP], F32R), ("a_qst0", [128, HALF, 2 * S], F32R), ("a_vxh", [KC, NC, XH, DV], F32R),
            ("a_vf", [KC, NC, XH, DK], F32), ("a_x2s", [128, 2, KD, S], F32R))
        wide = [128, KD, 2 * H * P]
        t["qk_lo"], t["qk"] = passing(nc, ("b_qk_lo", wide, F32R), ("b_qk", [128, 2 * H, 2, S], F32))
        t["qk_full"], = passing(nc, ("b_qk_full", wide, F32))

        def kept(name, shape, dt=F32):
            return ctx.enter_context(nc.sbuf_tensor("c_" + name, shape, dt))

        t["stage0"] = kept("stage0", [P, E, D])
        t["gs0"] = kept("gs0", [2 * E, H, TOK], F32R)
        t["cx0"] = kept("cx0", [P, H, TOK])
        t["xr"] = [kept(f"xr{i}", [128, TOK // 128, D]) for i in range(2)]
        t["wh0"] = kept("wh0", [P, 2, TOK], F32R)
        with ExitStack() as both:
            t["v_hi"] = both.enter_context(nc.sbuf_tensor("v_hi", [128, KD, HE * E * P], F32R))
            t["v_lo"], t["v_full"] = arriving(nc, both, "v_lo", [128, KD, HE * E * P])
            cross_block(nc, t, dr)
            attend_block(nc, t, dr)
        output_block(nc, t, dr)


def kernel(**inputs):
    import numpy as np
    import concourse.bacc as bacc
    from concourse.bass_utils import run_bass_kernel_spmd as run

    nc = bacc.Bacc("TRN2", target_bir_lowering=False, num_devices=1)
    arrays, dr = {}, {}
    for name, a in laid_out({k: np.asarray(v) for k, v in inputs.items()}).items():
        arrays["in_" + name] = np.ascontiguousarray(a)
        dr[name] = nc.dram_tensor("in_" + name, a.shape, F32, kind="ExternalInput").ap()
    for name, shape in (("kscr", [2, 128, KD, SKP]), ("qscr", [2, 128, KD, S]), ("dscr", [4, B, SKP]), ("x1scr", [B, S, D]),
                        ("x2scr", [B, 128, 2, KD, S]), ("gscr", [128, B * S]), ("cscr", [P, H, B * S])):
        dr[name] = nc.dram_tensor(name, shape, F32, kind="Internal").ap()
    dr["out"] = nc.dram_tensor("out", [B, S, D], F32, kind="ExternalOutput").ap()
    build(nc, dr)
    return run(nc, [arrays], core_ids=[0]).results[0]["out"]
```
